# Optimizing a Trainium2 kernel written in Bass

```python
import numpy as np
import jax
import jax.numpy as jnp

def _softmax(x, axis=-1):
    return jax.nn.softmax(x, axis=axis)

def _gelu(x):
    return jax.nn.gelu(x, approximate=True)

def _silu(x):
    return jax.nn.silu(x)

def _sigmoid(x):
    return jax.nn.sigmoid(x)

def _layernorm(x, axis=-1, eps=1e-05):
    m = jnp.mean(x, axis=axis, keepdims=True)
    v = jnp.var(x, axis=axis, keepdims=True)
    return (x - m) / jnp.sqrt(v + eps)

def _scatter_add(tgt, idx, src, axis=0):
    return tgt.at[idx].add(src)

def _segment_sum(src, seg, n):
    return jax.ops.segment_sum(src, seg, n)
kernel_name = 'mk_prb_d1_jaxref_r4_b98e42'

def setup_inputs(seed: int=0):
    np.random.seed(seed)
    _w = jnp.asarray

    def _L0_attn_setup():
        import jax, jax.numpy as jnp
        import numpy as np
        D_MODEL = 256
        D_STATE = 16
        D_CONV = 4
        EXPAND = 2
        D_INNER = EXPAND * D_MODEL
        DT_RANK = (D_MODEL + 15) // 16
        B, L = (1, 512)

        def _silu(v):
            return v * jax.nn.sigmoid(v)

        def _mamba_fwd(x, in_proj_w, conv_w, conv_b, x_proj_w, dt_proj_w, dt_proj_b, A_log, D_param, out_proj_w):
            b, l, _ = x.shape
            d_state = A_log.shape[1]
            dt_rank = dt_proj_w.shape[1]
            xz = x @ in_proj_w.T
            x_inner, z = jnp.split(xz, 2, axis=-1)
            x_c = jax.lax.conv_general_dilated(x_inner.transpose(0, 2, 1), conv_w, window_strides=(1,), padding=[(conv_w.shape[-1] - 1, 0)], feature_group_count=x_inner.shape[-1], dimension_numbers=('NCH', 'OIH', 'NCH'))
            x_conv = _silu((x_c + conv_b[None, :, None]).transpose(0, 2, 1))
            x_dbl = x_conv @ x_proj_w.T
            dt_lr = x_dbl[..., :dt_rank]
            B_ssm = x_dbl[..., dt_rank:dt_rank + d_state]
            C_ssm = x_dbl[..., dt_rank + d_state:]
            dt = jax.nn.softplus(dt_lr @ dt_proj_w.T + dt_proj_b)
            A = -jnp.exp(A_log)
            dA = jnp.exp(jnp.einsum('bld,dn->bldn', dt, A))
            dBx = jnp.einsum('bld,bln->bldn', dt * x_conv, B_ssm)

            def step(h, inp):
                a_t, bx_t, c_t = inp
                h = a_t * h + bx_t
                y_t = jnp.einsum('bdn,bn->bd', h, c_t)
                return (h, y_t)
            h0 = jnp.zeros((b, x_conv.shape[-1], d_state), dtype=x.dtype)
            _, ys = jax.lax.scan(step, h0, (dA.transpose(1, 0, 2, 3), dBx.transpose(1, 0, 2, 3), C_ssm.transpose(1, 0, 2)))
            y = ys.transpose(1, 0, 2) + x_conv * D_param
            return y * _silu(z) @ out_proj_w.T
        key = jax.random.key(seed)
        ks = jax.random.split(key, 8)
        s = lambda fan_in: 1.0 / np.sqrt(fan_in)
        x = jax.random.normal(ks[0], (B, L, D_MODEL), dtype=jnp.float32)
        in_proj_w = jax.random.normal(ks[1], (2 * D_INNER, D_MODEL), dtype=jnp.float32) * s(D_MODEL)
        conv_w = jax.random.normal(ks[2], (D_INNER, 1, D_CONV), dtype=jnp.float32) * s(D_CONV)
        conv_b = jax.random.normal(ks[3], (D_INNER,), dtype=jnp.float32) * s(D_CONV)
        x_proj_w = jax.random.normal(ks[4], (DT_RANK + 2 * D_STATE, D_INNER), dtype=jnp.float32) * s(D_INNER)
        dt_proj_w = jax.random.normal(ks[5], (D_INNER, DT_RANK), dtype=jnp.float32) * s(DT_RANK)
        dt_proj_b = jax.random.normal(ks[6], (D_INNER,), dtype=jnp.float32) * s(DT_RANK)
        A_log = jnp.log(jnp.arange(1, D_STATE + 1, dtype=jnp.float32))[None, :] * jnp.ones((D_INNER, 1), jnp.float32)
        D_param = jnp.ones((D_INNER,), dtype=jnp.float32)
        out_proj_w = jax.random.normal(ks[7], (D_MODEL, D_INNER), dtype=jnp.float32) * s(D_INNER)
        return {'x': x, 'in_proj_w': in_proj_w, 'conv_w': conv_w, 'conv_b': conv_b, 'x_proj_w': x_proj_w, 'dt_proj_w': dt_proj_w, 'dt_proj_b': dt_proj_b, 'A_log': A_log, 'D_param': D_param, 'out_proj_w': out_proj_w}
    _L0_attn_in = _L0_attn_setup()

    def _L0_ffn_setup():
        import jax, jax.numpy as jnp
        import numpy as np
        DIM = 256
        DEPTH = 2
        HEADS = 8
        DIM_HEAD = 64
        WINDOW = 128
        INNER = HEADS * DIM_HEAD
        HID = int(DIM * 4 * 2 / 3)
        B, N = (2, 2048)
        QK_SCALE = 8.0

        def shift_token(t):
            t1, t2 = jnp.split(t, 2, axis=-1)
            t2 = jnp.pad(t2, ((0, 0), (1, 0), (0, 0)))[:, :-1]
            return jnp.concatenate([t1, t2], axis=-1)

        def l2norm(t):
            return t / jnp.clip(jnp.linalg.norm(t, axis=-1, keepdims=True), 1e-12)

        def rotate_half(x):
            x1, x2 = jnp.split(x, 2, axis=-1)
            return jnp.concatenate([-x2, x1], axis=-1)

        def rotary_xpos(q, k):
            n = q.shape[-2]
            half_idx = jnp.arange(0, DIM_HEAD, 2, dtype=jnp.float32)
            inv_freq = 1.0 / 10000.0 ** (half_idx / DIM_HEAD)
            t = jnp.arange(n, dtype=jnp.float32)
            freqs = t[:, None] * inv_freq[None, :]
            freqs = jnp.concatenate([freqs, freqs], axis=-1)
            base = (half_idx + 0.4 * DIM_HEAD) / (1.4 * DIM_HEAD)
            power = (t - n // 2) / float(WINDOW // 2)
            scale = base[None, :] ** power[:, None]
            scale = jnp.concatenate([scale, scale], axis=-1)
            cos, sin = (jnp.cos(freqs), jnp.sin(freqs))
            q = q * cos * scale + rotate_half(q) * sin * scale
            k = k * cos / scale + rotate_half(k) * sin / scale
            return (q, k)

        def local_attention(q, k, v):
            b, h, n, d = q.shape
            w = n // WINDOW
            bq = q.reshape(b, h, w, WINDOW, d) * QK_SCALE
            bk = k.reshape(b, h, w, WINDOW, d)
            bv = v.reshape(b, h, w, WINDOW, d)

            def look_around(t):
                p = jnp.pad(t, ((0, 0), (0, 0), (1, 0), (0, 0), (0, 0)))
                return jnp.concatenate([p[:, :, :w], p[:, :, 1:]], axis=3)
            bk, bv = (look_around(bk), look_around(bv))
            bt = jnp.arange(n).reshape(w, WINDOW)
            btp = jnp.pad(bt, ((1, 0), (0, 0)), constant_values=-1)
            btk = jnp.concatenate([btp[:w], btp[1:]], axis=1)
            sim = jnp.einsum('bhwid,bhwjd->bhwij', bq, bk)
            i = bt[:, :, None]
            j = btk[:, None, :]
            mask = (i < j) | (i > j + WINDOW) | (j == -1)
            sim = jnp.where(mask, -jnp.finfo(sim.dtype).max, sim)
            attn = jax.nn.softmax(sim, axis=-1)
            out = jnp.einsum('bhwij,bhwjd->bhwid', attn, bv)
            return out.reshape(b, h, n, d)

        def _layer(x, wqkv, qs, ksc, wo, lg, lb, w1, b1, w2, b2):
            b, n, _ = x.shape
            h = shift_token(x)
            qkv = h @ wqkv
            q, k, v = jnp.split(qkv, 3, axis=-1)
            to_heads = lambda t: t.reshape(b, n, HEADS, DIM_HEAD).transpose(0, 2, 1, 3)
            q, k, v = (to_heads(q), to_heads(k), to_heads(v))
            q = l2norm(q) * qs
            k = l2norm(k) * ksc
            q, k = rotary_xpos(q, k)
            o = local_attention(q, k, v)
            o = o.transpose(0, 2, 1, 3).reshape(b, n, INNER)
            x = x + o @ wo
            h = shift_token(x)
            mu = h.mean(-1, keepdims=True)
            var = h.var(-1, keepdims=True)
            h = (h - mu) / jnp.sqrt(var + 1e-05) * lg + lb
            h = h @ w1 + b1
            a, g = jnp.split(h, 2, axis=-1)
            h = a * jax.nn.gelu(g, approximate=False)
            x = x + h @ w2 + b2
            return x
        key = jax.random.key(seed)
        ks = jax.random.split(key, 6)
        return {'x': jax.random.normal(ks[0], (B, N, DIM), jnp.float32), 'wqkv': jax.random.normal(ks[1], (DEPTH, DIM, 3 * INNER), jnp.float32) * 0.02, 'q_scale': jnp.ones((DEPTH, DIM_HEAD), jnp.float32), 'k_scale': jnp.ones((DEPTH, DIM_HEAD), jnp.float32), 'wo': jax.random.normal(ks[2], (DEPTH, INNER, DIM), jnp.float32) * 0.02, 'ln_g': jnp.ones((DEPTH, DIM), jnp.float32), 'ln_b': jnp.zeros((DEPTH, DIM), jnp.float32), 'w1': jax.random.normal(ks[3], (DEPTH, DIM, 2 * HID), jnp.float32) * 0.02, 'b1': jnp.zeros((DEPTH, 2 * HID), jnp.float32), 'w2': jax.random.normal(ks[4], (DEPTH, HID, DIM), jnp.float32) * 0.02, 'b2': jnp.zeros((DEPTH, DIM), jnp.float32)}
    _L0_ffn_in = _L0_ffn_setup()
    _d = {'L0_attn_x': _L0_attn_in['x'], 'L0_attn_in_proj_w': _L0_attn_in['in_proj_w'], 'L0_attn_conv_w': _L0_attn_in['conv_w'], 'L0_attn_conv_b': _L0_attn_in['conv_b'], 'L0_attn_x_proj_w': _L0_attn_in['x_proj_w'], 'L0_attn_dt_proj_w': _L0_attn_in['dt_proj_w'], 'L0_attn_dt_proj_b': _L0_attn_in['dt_proj_b'], 'L0_attn_A_log': _L0_attn_in['A_log'], 'L0_attn_D_param': _L0_attn_in['D_param'], 'L0_attn_out_proj_w': _L0_attn_in['out_proj_w'], 'L0_ffn_wqkv': _L0_ffn_in['wqkv'], 'L0_ffn_q_scale': _L0_ffn_in['q_scale'], 'L0_ffn_k_scale': _L0_ffn_in['k_scale'], 'L0_ffn_wo': _L0_ffn_in['wo'], 'L0_ffn_ln_g': _L0_ffn_in['ln_g'], 'L0_ffn_ln_b': _L0_ffn_in['ln_b'], 'L0_ffn_w1': _L0_ffn_in['w1'], 'L0_ffn_b1': _L0_ffn_in['b1'], 'L0_ffn_w2': _L0_ffn_in['w2'], 'L0_ffn_b2': _L0_ffn_in['b2']}
    _x0 = _d['L0_attn_x']
    _d['L0_attn_x'] = jax.random.normal(jax.random.fold_in(jax.random.key(seed), 1), (1, 4096, 256), dtype=_x0.dtype)
    del _x0
    return _d

def reference(L0_attn_x, L0_attn_in_proj_w, L0_attn_conv_w, L0_attn_conv_b, L0_attn_x_proj_w, L0_attn_dt_proj_w, L0_attn_dt_proj_b, L0_attn_A_log, L0_attn_D_param, L0_attn_out_proj_w, L0_ffn_wqkv, L0_ffn_q_scale, L0_ffn_k_scale, L0_ffn_wo, L0_ffn_ln_g, L0_ffn_ln_b, L0_ffn_w1, L0_ffn_b1, L0_ffn_w2, L0_ffn_b2):

    def _L0_attn_ref(x, in_proj_w, conv_w, conv_b, x_proj_w, dt_proj_w, dt_proj_b, A_log, D_param, out_proj_w):
        import jax, jax.numpy as jnp
        import numpy as np
        D_MODEL = 256
        D_STATE = 16
        D_CONV = 4
        EXPAND = 2
        D_INNER = EXPAND * D_MODEL
        DT_RANK = (D_MODEL + 15) // 16
        B, L = (1, 512)

        def _silu(v):
            return v * jax.nn.sigmoid(v)

        def _mamba_fwd(x, in_proj_w, conv_w, conv_b, x_proj_w, dt_proj_w, dt_proj_b, A_log, D_param, out_proj_w):
            b, l, _ = x.shape
            d_state = A_log.shape[1]
            dt_rank = dt_proj_w.shape[1]
            xz = x @ in_proj_w.T
            x_inner, z = jnp.split(xz, 2, axis=-1)
            x_c = jax.lax.conv_general_dilated(x_inner.transpose(0, 2, 1), conv_w, window_strides=(1,), padding=[(conv_w.shape[-1] - 1, 0)], feature_group_count=x_inner.shape[-1], dimension_numbers=('NCH', 'OIH', 'NCH'))
            x_conv = _silu((x_c + conv_b[None, :, None]).transpose(0, 2, 1))
            x_dbl = x_conv @ x_proj_w.T
            dt_lr = x_dbl[..., :dt_rank]
            B_ssm = x_dbl[..., dt_rank:dt_rank + d_state]
            C_ssm = x_dbl[..., dt_rank + d_state:]
            dt = jax.nn.softplus(dt_lr @ dt_proj_w.T + dt_proj_b)
            A = -jnp.exp(A_log)
            dA = jnp.exp(jnp.einsum('bld,dn->bldn', dt, A))
            dBx = jnp.einsum('bld,bln->bldn', dt * x_conv, B_ssm)

            def step(h, inp):
                a_t, bx_t, c_t = inp
                h = a_t * h + bx_t
                y_t = jnp.einsum('bdn,bn->bd', h, c_t)
                return (h, y_t)
            h0 = jnp.zeros((b, x_conv.shape[-1], d_state), dtype=x.dtype)
            _, ys = jax.lax.scan(step, h0, (dA.transpose(1, 0, 2, 3), dBx.transpose(1, 0, 2, 3), C_ssm.transpose(1, 0, 2)))
            y = ys.transpose(1, 0, 2) + x_conv * D_param
            return y * _silu(z) @ out_proj_w.T
        return _mamba_fwd(x, in_proj_w, conv_w, conv_b, x_proj_w, dt_proj_w, dt_proj_b, A_log, D_param, out_proj_w)

    def _L0_ffn_ref(x, wqkv, q_scale, k_scale, wo, ln_g, ln_b, w1, b1, w2, b2):
        import jax, jax.numpy as jnp
        import numpy as np
        DIM = 256
        DEPTH = 2
        HEADS = 8
        DIM_HEAD = 64
        WINDOW = 128
        INNER = HEADS * DIM_HEAD
        HID = int(DIM * 4 * 2 / 3)
        B, N = (2, 2048)
        QK_SCALE = 8.0

        def shift_token(t):
            t1, t2 = jnp.split(t, 2, axis=-1)
            t2 = jnp.pad(t2, ((0, 0), (1, 0), (0, 0)))[:, :-1]
            return jnp.concatenate([t1, t2], axis=-1)

        def l2norm(t):
            return t / jnp.clip(jnp.linalg.norm(t, axis=-1, keepdims=True), 1e-12)

        def rotate_half(x):
            x1, x2 = jnp.split(x, 2, axis=-1)
            return jnp.concatenate([-x2, x1], axis=-1)

        def rotary_xpos(q, k):
            n = q.shape[-2]
            half_idx = jnp.arange(0, DIM_HEAD, 2, dtype=jnp.float32)
            inv_freq = 1.0 / 10000.0 ** (half_idx / DIM_HEAD)
            t = jnp.arange(n, dtype=jnp.float32)
            freqs = t[:, None] * inv_freq[None, :]
            freqs = jnp.concatenate([freqs, freqs], axis=-1)
            base = (half_idx + 0.4 * DIM_HEAD) / (1.4 * DIM_HEAD)
            power = (t - n // 2) / float(WINDOW // 2)
            scale = base[None, :] ** power[:, None]
            scale = jnp.concatenate([scale, scale], axis=-1)
            cos, sin = (jnp.cos(freqs), jnp.sin(freqs))
            q = q * cos * scale + rotate_half(q) * sin * scale
            k = k * cos / scale + rotate_half(k) * sin / scale
            return (q, k)

        def local_attention(q, k, v):
            b, h, n, d = q.shape
            w = n // WINDOW
            bq = q.reshape(b, h, w, WINDOW, d) * QK_SCALE
            bk = k.reshape(b, h, w, WINDOW, d)
            bv = v.reshape(b, h, w, WINDOW, d)

            def look_around(t):
                p = jnp.pad(t, ((0, 0), (0, 0), (1, 0), (0, 0), (0, 0)))
                return jnp.concatenate([p[:, :, :w], p[:, :, 1:]], axis=3)
            bk, bv = (look_around(bk), look_around(bv))
            bt = jnp.arange(n).reshape(w, WINDOW)
            btp = jnp.pad(bt, ((1, 0), (0, 0)), constant_values=-1)
            btk = jnp.concatenate([btp[:w], btp[1:]], axis=1)
            sim = jnp.einsum('bhwid,bhwjd->bhwij', bq, bk)
            i = bt[:, :, None]
            j = btk[:, None, :]
            mask = (i < j) | (i > j + WINDOW) | (j == -1)
            sim = jnp.where(mask, -jnp.finfo(sim.dtype).max, sim)
            attn = jax.nn.softmax(sim, axis=-1)
            out = jnp.einsum('bhwij,bhwjd->bhwid', attn, bv)
            return out.reshape(b, h, n, d)

        def _layer(x, wqkv, qs, ksc, wo, lg, lb, w1, b1, w2, b2):
            b, n, _ = x.shape
            h = shift_token(x)
            qkv = h @ wqkv
            q, k, v = jnp.split(qkv, 3, axis=-1)
            to_heads = lambda t: t.reshape(b, n, HEADS, DIM_HEAD).transpose(0, 2, 1, 3)
            q, k, v = (to_heads(q), to_heads(k), to_heads(v))
            q = l2norm(q) * qs
            k = l2norm(k) * ksc
            q, k = rotary_xpos(q, k)
            o = local_attention(q, k, v)
            o = o.transpose(0, 2, 1, 3).reshape(b, n, INNER)
            x = x + o @ wo
            h = shift_token(x)
            mu = h.mean(-1, keepdims=True)
            var = h.var(-1, keepdims=True)
            h = (h - mu) / jnp.sqrt(var + 1e-05) * lg + lb
            h = h @ w1 + b1
            a, g = jnp.split(h, 2, axis=-1)
            h = a * jax.nn.gelu(g, approximate=False)
            x = x + h @ w2 + b2
            return x
        for l in range(DEPTH):
            x = _layer(x, wqkv[l], q_scale[l], k_scale[l], wo[l], ln_g[l], ln_b[l], w1[l], b1[l], w2[l], b2[l])
        return x
    x = L0_attn_x
    xn = _layernorm(x, axis=-1)
    x = x + _L0_attn_ref(xn, L0_attn_in_proj_w, L0_attn_conv_w, L0_attn_conv_b, L0_attn_x_proj_w, L0_attn_dt_proj_w, L0_attn_dt_proj_b, L0_attn_A_log, L0_attn_D_param, L0_attn_out_proj_w) + _L0_ffn_ref(xn, L0_ffn_wqkv, L0_ffn_q_scale, L0_ffn_k_scale, L0_ffn_wo, L0_ffn_ln_g, L0_ffn_ln_b, L0_ffn_w1, L0_ffn_b1, L0_ffn_w2, L0_ffn_b2)
    return x

_drawn_inputs = setup_inputs


def setup_inputs(seed=0):
    import zlib

    import numpy as np

    out = dict(_drawn_inputs(seed))
    spreads = {'L0_attn_D_param': (1.0, 0.2),
     'L0_ffn_q_scale': (1.0, 0.6),
     'L0_ffn_k_scale': (1.0, 0.6),
     'L0_ffn_ln_g': (1.0, 0.6),
     'L0_ffn_ln_b': (0.0, 0.8),
     'L0_ffn_b1': (0.0, 0.8),
     'L0_ffn_b2': (0.0, 0.1)}
    factors = {'L0_ffn_wqkv': 4.197, 'L0_ffn_wo': 4.106}
    for name, (base, spread) in spreads.items():
        noise = np.random.default_rng([zlib.crc32(name.encode()), seed]).standard_normal(out[name].shape)
        drawn = base * np.exp(spread * noise) if base else spread * noise
        out[name] = jnp.asarray(drawn.astype(out[name].dtype))
    for name, factor in factors.items():
        out[name] = (out[name] * factor).astype(out[name].dtype)
    return out
```

```python
import numpy as np
import concourse.bass as bass
from concourse import mybir
from contextlib import ExitStack

P = 128
TOKENS, D = 4096, 256
T = 512
CHUNKS = TOKENS // T
WIN = 128
NW = T // WIN
FT = D // P
INNER = 512
NJ = INNER // P
STATES = 16
TAPS = 4
RANK = 16
XROWS = 2 * STATES + RANK
HEADS, DH = 8, 64
PAIRS = HEADS // 2
QKV = 3 * HEADS * DH
HID = 682
NH = -(-HID // P)
LAST = HID - (NH - 1) * P
LAYERS = 2
EPS = 1e-5
UNITS = STATES * NJ
GROUP = 2
NGROUPS = STATES // GROUP
DA_RING, H_RING = 3, 4
BANKS = 4
NEG = -1e30
C_ALOG = 0
C_CW = C_ALOG + NJ * STATES
C_CB = C_CW + NJ * TAPS
C_DTB = C_CB + NJ
C_DP = C_DTB + NJ
C_LG = C_DP + NJ
C_LB = C_LG + LAYERS * FT
C_B1A = C_LB + LAYERS * FT
C_B1G = C_B1A + LAYERS * NH
NPAR = C_B1G + LAYERS * NH


def build(nc, io):
    f32, bf16 = mybir.dt.float32, mybir.dt.bfloat16
    ALU, ACT = mybir.AluOpType, mybir.ActivationFunctionType
    AX = mybir.AxisListType
    ctx = ExitStack()

    def sb(name, shape, dt=f32):
        return ctx.enter_context(nc.sbuf_tensor(name, shape, dt))

    inw = sb("inw", [P, FT, 2 * INNER])
    xpw = sb("xpw", [P, NJ, XROWS])
    dtw = sb("dtw", [XROWS, INNER])
    outw = sb("outw", [P, NJ, D])
    wo = sb("wo", [P, LAYERS, NJ, D])
    w1 = sb("w1", [P, LAYERS, FT, 2 * HID])
    w2 = sb("w2", [P, LAYERS, NH, D])
    par = sb("par", [P, NPAR])
    qks = sb("qks", [P, LAYERS, 4, DH])
    ident = sb("ident", [P, P])
    identb = sb("identb", [P, P], bf16)
    mask = sb("mask", [P, 2, 2 * WIN], bf16)
    mask0 = sb("mask0", [P, 2 * WIN], bf16)
    amat = sb("amat", [P, NJ * STATES])
    powers = sb("powers", [P, HEADS * 2])
    wqkv = sb("wqkv", [P, FT, QKV])
    xtok = sb("xtok", [P, NW, D])
    tab = sb("tab", [P, 2, 4, DH])
    bc = sb("bc", [P, 2, GROUP, 2, T])
    xnT = sb("xnT", [P, FT, 1 + T])
    xin = sb("xin", [P, NJ, TAPS - 1 + T])
    halo = sb("halo", [P, NJ, TAPS - 1])
    xconv = sb("xconv", [P, NJ, T])
    dt_sb = sb("dt_sb", [P, NJ, T])
    xdbl = sb("xdbl", [XROWS, T])
    dA = sb("dA", [P, DA_RING, T])
    hb = sb("hb", [P, H_RING, T])
    state = sb("state", [P, UNITS])
    X = sb("X", [P, NW, D])
    stats = sb("stats", [P, NW, 2, 6])
    mv = sb("mv", [P, NW, 2])
    rstd = sb("rstd", [P, NW])
    x2T = sb("x2T", [P, FT, 1 + T])
    sq = sb("sq", [P, 2, HEADS * DH])
    rot = sb("rot", [P, 2, HEADS * DH])
    ssum = sb("ssum", [P, 2 * HEADS])
    rnorm = sb("rnorm", [P, 2 * HEADS])
    tabs = sb("tabs", [P, 4, DH])
    qT = sb("qT", [P, PAIRS, WIN])
    kT = sb("kT", [P, LAYERS, PAIRS, 2, WIN])
    V = sb("V", [P, LAYERS, 2, HEADS * DH])
    nmax = sb("nmax", [P, HEADS])
    rowsum = sb("rowsum", [P, HEADS])
    rinv = sb("rinv", [P, HEADS])
    probs = sb("probs", [P, 2, 2, 2 * WIN])
    pT = sb("pT", [P, 2, 4, WIN])
    o_sb = sb("o_sb", [P, HEADS * DH])
    oT = sb("oT", [P, NJ, WIN])
    sh = sb("sh", [P, LAYERS, NW, P])
    stats2 = sb("stats2", [P, 2, 2, 6])
    mv2 = sb("mv2", [P, 2, 2])
    rstd2 = sb("rstd2", [P, 2])
    hn = sb("hn", [P, 2, D])
    hT = sb("hT", [P, FT, 2 * WIN])
    gel = sb("gel", [P, 2, 2 * WIN])
    hid = sb("hid", [P, NH, 2 * WIN])
    scratch = nc.dram_tensor("bc_rows", [2 * STATES, T], f32, kind="Internal").ap()

    ybank = [ctx.enter_context(nc.psum_tensor(f"ysum{j}", [P, T], f32)) for j in range(NJ)]
    ring = [ctx.enter_context(nc.psum_tensor(f"ring{b}", [P, T], f32)) for b in range(BANKS)]

    class Signal:
        def __init__(self, name, per_chunk):
            self.sem = ctx.enter_context(nc.semaphore(name))
            self.per_chunk = per_chunk

        def at(self, it, count):
            assert -self.per_chunk < count <= self.per_chunk, (self.sem, count)
            return self.sem, it * self.per_chunk + (self.per_chunk + count)

    passed = ctx.enter_context(nc.semaphore("passed"))
    D16 = 16
    x_loaded = Signal("x_loaded", D16)
    mask0_ready = Signal("mask0_ready", 1)
    tab_loaded = [Signal(f"tab_loaded{s}", D16 * LAYERS * NW // 2) for s in range(2)]
    wqkv_loaded = Signal("wqkv_loaded", D16 * LAYERS)
    bc_stored = Signal("bc_stored", D16)
    bc_loaded = [Signal(f"bc_loaded{s}", D16 * NGROUPS // 2) for s in range(2)]
    shifted = [Signal(f"shifted{w}", D16 * LAYERS) for w in range(NW)]
    carried = [Signal(f"carried{w}", D16 * LAYERS) for w in range(NW)]
    out_stored = Signal("out_stored", D16)
    stats_ready = Signal("stats_ready", NW)
    mv_ready = Signal("mv_ready", NW)
    eps_added = Signal("eps_added", 1)
    rstd_ready = Signal("rstd_ready", 1)
    xn_ready = Signal("xn_ready", NW)
    full = [Signal(f"bank_full{b}", 0) for b in range(BANKS)]
    xnT_ready = Signal("xnT_ready", 2)
    halo_ready = Signal("halo_ready", 1)
    halo_saved = Signal("halo_saved", 1)
    xin_ready = Signal("xin_ready", NJ)
    tap0_ready = Signal("tap0_ready", NJ)
    conv_step = Signal("conv_step", NJ * (TAPS - 1))
    xconv_ready = Signal("xconv_ready", NJ)
    xdbl_ready = Signal("xdbl_ready", 1)
    dtv_ready = Signal("dtv_ready", NJ)
    dtmin_ready = Signal("dtmin_ready", NJ)
    dtexp_ready = Signal("dtexp_ready", NJ)
    dtlog_ready = Signal("dtlog_ready", NJ)
    dt_ready = Signal("dt_ready", NJ)
    u_ready = Signal("u_ready", NJ)
    dA_ready = Signal("dA_ready", UNITS)
    dBx_ready = Signal("dBx_ready", UNITS)
    h_ready = Signal("h_ready", UNITS)
    state_saved = Signal("state_saved", UNITS)
    hC_ready = Signal("hC_ready", UNITS)
    summed = Signal("summed", UNITS)
    silu_ready = Signal("silu_ready", NJ)
    skip_added = Signal("skip_added", NJ)
    gated = Signal("gated", NJ)
    branch_added = Signal("branch_added", 2)
    out_ready = Signal("out_ready", 1)
    xnT_carried = Signal("xnT_carried", 1)
    x2T_carried = Signal("x2T_carried", 1)
    NA = LAYERS * NW
    sq_ready = Signal("sq_ready", 2 * NA)
    ssum_ready = Signal("ssum_ready", NA)
    ssum_clipped = Signal("ssum_clipped", NA)
    rnorm_ready = Signal("rnorm_ready", NA)
    tabs_ready = Signal("tabs_ready", NA)
    cos_ready = Signal("cos_ready", 2 * NA)
    sin_ready = Signal("sin_ready", 2 * NA)
    rot_ready = Signal("rot_ready", 2 * NA)
    normed = Signal("normed", 2 * NA)
    v_ready = Signal("v_ready", NA)
    qT_ready = Signal("qT_ready", NA)
    kT_ready = Signal("kT_ready", NA)
    nmax_ready = Signal("nmax_ready", PAIRS * NA)
    probs_ready = Signal("probs_ready", HEADS * NA)
    pT_ready = Signal("pT_ready", PAIRS * NA)
    rinv_ready = Signal("rinv_ready", PAIRS * NA)
    o_ready = Signal("o_ready", PAIRS * NA)
    oT_ready = Signal("oT_ready", NA)
    x1_ready = Signal("x1_ready", NA)
    NF = LAYERS * 2
    stats2_ready = Signal("stats2_ready", 4 * NF)
    mv2_ready = Signal("mv2_ready", 2 * NF)
    eps2_added = Signal("eps2_added", NF)
    rstd2_ready = Signal("rstd2_ready", NF)
    hn_ready = Signal("hn_ready", 4 * NF)
    hT_ready = Signal("hT_ready", FT * NF)
    gelu_ready = Signal("gelu_ready", NH * NF)
    hid_ready = Signal("hid_ready", NH * NF)
    x2_ready = Signal("x2_ready", NF)
    x2T_ready = Signal("x2T_ready", 2)
    consts_loaded = ctx.enter_context(nc.semaphore("consts_loaded"))
    memory_set = ctx.enter_context(nc.semaphore("memory_set"))
    casts_done = ctx.enter_context(nc.semaphore("casts_done"))
    a_exp = ctx.enter_context(nc.semaphore("a_exp"))
    a_ready = ctx.enter_context(nc.semaphore("a_ready"))

    ITEMS = [("W", 0, 0), ("W", 0, 1), ("F", 0, 0), ("W", 0, 2), ("W", 0, 3), ("F", 0, 1),
             ("W", 1, 0), ("W", 1, 1), ("F", 1, 0), ("W", 1, 2), ("W", 1, 3), ("F", 1, 1)]
    order, emptied = [], {}

    def group(name, read):
        order.append(name)
        emptied[name] = read

    for h in range(2):
        group(("xnT", h), (xnT_ready, h + 1))
    for j in range(NJ):
        group(("xin", j), (xin_ready, j + 1))
    group(("xdbl",), (xdbl_ready, 1))
    for j in range(NJ):
        group(("dt", j), (dtv_ready, j + 1))
    for kind, l, w in ITEMS:
        if kind == "W":
            a = l * NW + w
            group(("q", a), (sin_ready, 2 * a + 1))
            group(("k", a), (sin_ready, 2 * a + 2))
            group(("v", a), (v_ready, a + 1))
            group(("qT", a), (qT_ready, a + 1))
            group(("kT", a), (kT_ready, a + 1))

            def scores(p):
                group(("s", a, p), (probs_ready, a * HEADS + 2 * p + 2))
            scores(0)
            scores(1)
            for p in range(PAIRS):
                group(("pT", a, p), (pT_ready, a * PAIRS + p + 1))
                group(("o", a, p), (o_ready, a * PAIRS + p + 1))
                if p + 2 < PAIRS:
                    scores(p + 2)
            group(("oT", a), (oT_ready, a + 1))
            group(("wo", a), (x1_ready, a + 1))
        else:
            f = l * 2 + w
            group(("hT", f), (hT_ready, FT * (f + 1)))
            for i in range(NH):
                group(("h", f, i), (hid_ready, f * NH + i + 1))
            group(("w2", f), (x2_ready, f + 1))
            if l == 0:
                group(("x2T", w), (x2T_ready, w + 1))
    for j in range(NJ):
        group(("z", j), (silu_ready, j + 1))
    for h in range(2):
        group(("out", h), (branch_added, h + 1))
    while len(order) % BANKS:
        order.append(None)
    at = {name: n for n, name in enumerate(order) if name}
    for s in full:
        s.per_chunk = len(order) // BANKS

    def bank(name):
        return ring[at[name] % BANKS]

    def freed(it, name):
        n = at[name] - BANKS
        while order[n] is None:
            n -= BANKS
        sig, count = emptied[order[n]]
        return sig.at(it, count if n >= 0 else count - sig.per_chunk)

    def done(name):
        n = at[name]
        spare = n + BANKS < len(order) and order[n + BANKS] is None
        return full[n % BANKS].sem, 2 if spare else 1

    def filled(it, name):
        n = at[name]
        return full[n % BANKS].at(it, n // BANKS + done(name)[1])

    def heads_of(p):
        first = 4 * (p // 2) + p % 2
        return first, first + 2

    block = ctx.enter_context(nc.Block())

    def prime(eng, signals):
        for s in signals:
            eng.sem_inc(s.sem, s.per_chunk)

    @block.sync
    def _(sp):
        prime(sp, [x_loaded, *tab_loaded, wqkv_loaded, bc_stored, *bc_loaded, *shifted,
                   *carried, out_stored])
        consts = [(inw, io["inw"]), (par, io["par"]), (ident, io["ident"]),
                  (xpw, io["xpw"]), (outw, io["outw"]), (wo, io["wo"]), (w1, io["w1"]), (w2, io["w2"]),
                  (qks, io["qks"])]
        for dst, src in consts:
            full_dst = dst[tuple(slice(None) for _ in dst.shape)]
            sp.dma_start(full_dst, src).then_inc(consts_loaded, D16)
        sp.dma_start(hb[:, 0, :], io["mask"]).then_inc(consts_loaded, D16)
        sp.dma_start(hb[:, 1, 0:2 * WIN], io["mask0"]).then_inc(consts_loaded, D16)
        sp.dma_start(dtw[2 * STATES:XROWS, :], io["dtw"]).then_inc(consts_loaded, D16)
        sp.wait_ge(memory_set, N_SET)

        with sp.Fori(0, CHUNKS) as it:
            sp.wait_ge(*out_ready.at(it, 0))
            sp.sem_inc(passed, 1)
            sp.dma_start(xtok[:, :, :], io["x"][bass.ds(it * T, T), :].rearrange("(w p) d -> p w d", p=P))\
              .then_inc(x_loaded.sem, D16)
            def load_wqkv(l):
                a_last = (l * NW - 1) % (LAYERS * NW)
                n = at[("v", a_last)]
                sp.wait_ge(*full[n % BANKS].at(it, n // BANKS + 1 - (full[n % BANKS].per_chunk if l == 0 else 0)))
                sp.sem_inc(passed, 1)
                sp.dma_start(wqkv[:, :, :], io["wqkv"][:, l, :, :]).then_inc(wqkv_loaded.sem, D16)

            def load_tab(a):
                sp.wait_ge(*tabs_ready.at(it, a - 1))
                sp.sem_inc(passed, 1)
                sp.dma_start(tab[:, a % 2, :, :],
                             io["tab"][bass.ds(it * T + (a % NW) * WIN, WIN), :, :]).then_inc(tab_loaded[a % 2].sem, D16)

            def load_bc(g):
                sp.wait_ge(*hC_ready.at(it, (g - 1) * GROUP * NJ))
                sp.sem_inc(passed, 1)
                rows = 2 * GROUP
                src = scratch[g * rows:(g + 1) * rows, :].rearrange("r t -> (r t)")
                sp.dma_start(bc[:, g % 2, :, :, :].rearrange("p n c t -> p (n c t)"), src.partition_broadcast(P)).then_inc(bc_loaded[g % 2].sem, D16)

            def shift(l, w):
                a = l * NW + w
                sp.wait_ge(*x1_ready.at(it, a + 1))
                sp.sem_inc(passed, 1)
                sp.wait_ge(*hn_ready.at(it, hn_reads(l, w)))
                sp.sem_inc(passed, 1)
                sp.dma_start(sh[1:P, l, w, :], X[0:P - 1, w, P:D]).then_inc(shifted[w].sem, D16)
                sp.wait_ge(*hn_ready.at(it, hn_carry(l, w)))
                sp.sem_inc(passed, 1)
                sp.dma_start(sh[0:1, l, (w + 1) % NW, :], X[P - 1:P, w, P:D]).then_inc(carried[w].sem, D16)

            def hn_reads(l, w):
                return 4 * (l * 2 + w // 2) + 4 - hn_ready.per_chunk

            def hn_carry(l, w):
                if w == NW - 1:
                    return 4 * (l * 2) + 4
                return hn_reads(l, w + 1)

            load_wqkv(0)
            load_tab(0)
            load_tab(1)
            sp.wait_ge(*xdbl_ready.at(it, 1))
            sp.sem_inc(passed, 1)
            sp.wait_ge(*bc_loaded[0].at(it, 0))
            sp.sem_inc(passed, 1)
            sp.wait_ge(*bc_loaded[1].at(it, 0))
            sp.sem_inc(passed, 1)
            sp.dma_start(scratch, xdbl[0:2 * STATES, :]).then_inc(bc_stored.sem, D16)
            sp.wait_ge(*bc_stored.at(it, D16))
            sp.sem_inc(passed, 1)
            load_bc(0)
            load_bc(1)
            unit, g_next = 0, 2
            for kind, l, w in ITEMS:
                if kind == "W":
                    a = l * NW + w
                    if a + 2 < NA:
                        load_tab(a + 2)
                    if a == NW - 1:
                        load_wqkv(1)
                    unit += W_FILLS
                    while g_next < NGROUPS and (g_next - 1) * GROUP * NJ <= unit - 3:
                        load_bc(g_next)
                        g_next += 1
                    shift(l, w)
                else:
                    unit += F_FILLS
            while g_next < NGROUPS:
                load_bc(g_next)
                g_next += 1
            sp.wait_ge(*out_ready.at(it, 1))
            sp.sem_inc(passed, 1)
            sp.dma_start(io["out"][bass.ds(it * T, T), :].rearrange("(w p) d -> p w d", p=P), X[:, :, :])\
              .then_inc(out_stored.sem, D16)
        sp.wait_ge(out_stored.sem, D16 * (CHUNKS + 1))
        sp.wait_ge(bc_stored.sem, D16 * (CHUNKS + 1))

    @block.vector
    def _(dve):
        prime(dve, [stats_ready, mv_ready, xn_ready, conv_step, dt_ready, u_ready, dBx_ready, h_ready,
                    hC_ready, skip_added, gated, branch_added, ssum_ready, cos_ready, sin_ready,
                    nmax_ready, rinv_ready, o_ready, x1_ready, stats2_ready, mv2_ready, hid_ready,
                    x2_ready])
        dve.wait_ge(consts_loaded, N_CONST * D16)
        dve.wait_ge(memory_set, N_SET)
        dve.tensor_copy(mask[:, :, :], hb[:, 0, :].rearrange("p (s k) -> p s k", s=2)).then_inc(casts_done, 1)
        dve.tensor_copy(mask0[:, :], hb[:, 1, 0:2 * WIN]).then_inc(casts_done, 1)
        dve.tensor_copy(identb[:, :], ident[:, :]).then_inc(casts_done, 1)
        dve.wait_ge(casts_done, 3)

        with dve.Fori(0, CHUNKS) as it:
            def u_of(j):
                return xin[:, j, TAPS - 1:]

            def dBx(k):
                n, j = divmod(k, NJ)
                g = n // GROUP
                if j == 0 and n % GROUP == 0:
                    dve.wait_ge(*bc_loaded[g % 2].at(it, D16 * (g // 2 + 1)))
                if n == 0:
                    dve.wait_ge(*u_ready.at(it, j + 1))
                dve.wait_ge(*summed.at(it, k + 1 - H_RING))
                dve.tensor_tensor(hb[:, k % H_RING, :], u_of(j), bc[:, g % 2, n % GROUP, 0, :], ALU.mult)\
                   .then_inc(dBx_ready.sem, 1)

            def scan(k):
                dve.wait_ge(*dA_ready.at(it, k + 1))
                dve.wait_ge(*dBx_ready.at(it, k + 1))
                dve.wait_ge(*state_saved.at(it, k + 1 - UNITS))
                dve.tensor_tensor_scan(hb[:, k % H_RING, :], dA[:, k % DA_RING, :], hb[:, k % H_RING, :],
                                       state[:, k:k + 1], ALU.mult, ALU.add).then_inc(h_ready.sem, 1)

            def hC(k):
                n, j = divmod(k, NJ)
                g = n // GROUP
                dve.wait_ge(*h_ready.at(it, k + 1))
                dve.wait_ge(*state_saved.at(it, k + 1))
                dve.tensor_tensor(hb[:, k % H_RING, :], hb[:, k % H_RING, :], bc[:, g % 2, n % GROUP, 1, :],
                                  ALU.mult).then_inc(hC_ready.sem, 1)

            at_unit = [0]

            def fill(count=1):
                for _ in range(count):
                    k = at_unit[0]
                    if k < UNITS:
                        dBx(k)
                    if 0 <= k - 1 < UNITS:
                        scan(k - 1)
                    if 0 <= k - 2 < UNITS:
                        hC(k - 2)
                    at_unit[0] += 1

            dve.wait_ge(*x_loaded.at(it, D16))
            for w in range(NW):
                dve.bn_stats(stats[:, w, 0, :], xtok[:, w, :]).then_inc(stats_ready.sem, 1)
            for w in range(NW):
                dve.wait_ge(*stats_ready.at(it, w + 1))
                dve.sem_inc(passed, 1)
                dve.bn_aggr(mv[:, w, :], stats[:, w, 0, :]).then_inc(mv_ready.sem, 1)
            dve.wait_ge(*rstd_ready.at(it, 1))
            dve.wait_ge(*out_stored.at(it, 0))
            for w in range(4):
                dve.tensor_scalar(X[:, w, :], xtok[:, w, :], mv[:, w, 0:1], rstd[:, w:w + 1],
                                  ALU.subtract, ALU.mult).then_inc(xn_ready.sem, 1)
            for j in range(NJ):
                dve.wait_ge(*tap0_ready.at(it, j + 1))
                for k in range(1, TAPS):
                    if k > 1:
                        dve.wait_ge(*conv_step.at(it, j * (TAPS - 1) + k - 1))
                    dve.scalar_tensor_tensor(xconv[:, j, :], xin[:, j, k:k + T],
                                             par[:, C_CW + j * TAPS + k:C_CW + j * TAPS + k + 1],
                                             xconv[:, j, :], ALU.mult, ALU.add).then_inc(conv_step.sem, 1)
            for j in range(NJ):
                dve.wait_ge(*dtlog_ready.at(it, j + 1))
                dve.tensor_tensor(dt_sb[:, j, :], dt_sb[:, j, :], dA[:, j % 3, :], ALU.max)\
                   .then_inc(dt_ready.sem, 1)
            dve.wait_ge(*halo_saved.at(it, 1))
            for j in range(NJ):
                dve.wait_ge(*dt_ready.at(it, j + 1))
                dve.wait_ge(*xconv_ready.at(it, j + 1))
                dve.tensor_tensor(u_of(j), dt_sb[:, j, :], xconv[:, j, :], ALU.mult).then_inc(u_ready.sem, 1)

            def attention(l, w):
                a = l * NW + w
                dve.wait_ge(*sq_ready.at(it, 2 * a + 2))
                dve.wait_ge(*rnorm_ready.at(it, a))
                dve.tensor_reduce(ssum[:, :], sq[:, :, :].rearrange("p a (h d) -> p (a h) d", d=DH),
                                  AX.X, ALU.add).then_inc(ssum_ready.sem, 1)
                dve.wait_ge(*tabs_ready.at(it, a + 1))
                for i, name in ((0, "q"), (1, "k")):
                    src = bank((name, a))[:, :].rearrange("p (h d) -> p h d", d=DH)
                    cos = tabs[:, 2 * i:2 * i + 1, :].to_broadcast([P, HEADS, DH])
                    if i == 0:
                        dve.wait_ge(*ssum_ready.at(it, a + 1))
                        dve.wait_ge(*normed.at(it, 2 * a))
                    dve.wait_ge(*filled(it, (name, a)))
                    dve.tensor_tensor(sq[:, i, :].rearrange("p (h d) -> p h d", d=DH), src, cos, ALU.mult)\
                       .then_inc(cos_ready.sem, 1)
                    out = rot[:, i, :].rearrange("p (h d) -> p h d", d=DH)
                    lo = tabs[:, 2 * i + 1:2 * i + 2, 0:DH // 2].to_broadcast([P, HEADS, DH // 2])
                    hi = tabs[:, 2 * i + 1:2 * i + 2, DH // 2:DH].to_broadcast([P, HEADS, DH // 2])
                    dve.tensor_tensor(out[:, :, 0:DH // 2], src[:, :, DH // 2:DH], lo, ALU.mult)
                    dve.tensor_tensor(out[:, :, DH // 2:DH], src[:, :, 0:DH // 2], hi, ALU.mult)\
                       .then_inc(sin_ready.sem, 1)
                fill()
                fill()

                def row_max(p):
                    dve.wait_ge(*filled(it, ("s", a, p)))
                    dve.wait_ge(*probs_ready.at(it, a * HEADS + 2 * p + 2 - HEADS))
                    dve.tensor_reduce(nmax[:, 2 * p:2 * p + 2],
                                      bank(("s", a, p))[:, :].rearrange("p (h k) -> p h k", h=2),
                                      AX.X, ALU.max, negate=True).then_inc(nmax_ready.sem, 1)
                row_max(0)
                row_max(1)
                for p in range(PAIRS):
                    n = a * PAIRS + p
                    fill()
                    dve.wait_ge(*probs_ready.at(it, 2 * n + 2))
                    dve.wait_ge(*o_ready.at(it, n + 1 - PAIRS))
                    dve.reciprocal(rinv[:, 2 * p:2 * p + 2], rowsum[:, 2 * p:2 * p + 2]).then_inc(rinv_ready.sem, 1)
                    if p + 2 < PAIRS:
                        row_max(p + 2)
                    dve.wait_ge(*filled(it, ("o", a, p)))
                    dve.wait_ge(*rinv_ready.at(it, n + 1))
                    if p == 0:
                        dve.wait_ge(*oT_ready.at(it, a))
                    o_view = o_sb[:, :].rearrange("p (c e a d) -> p c e a d", c=2, e=2, a=2)
                    dve.tensor_tensor(o_view[:, p // 2, :, p % 2, :],
                                      bank(("o", a, p))[:, 0:2 * DH].rearrange("p (h d) -> p h d", h=2),
                                      rinv[:, 2 * p:2 * p + 2].unsqueeze(2).to_broadcast([P, 2, DH]), ALU.mult)\
                       .then_inc(o_ready.sem, 1)
                fill()
                dve.wait_ge(*filled(it, ("wo", a)))
                if l:
                    dve.wait_ge(*x2_ready.at(it, w // 2 + 1))
                dve.tensor_tensor(X[:, w, :], bank(("wo", a))[:, 0:D], X[:, w, :], ALU.add)\
                   .then_inc(x1_ready.sem, 1)

            def feed_forward(l, half):
                f = l * 2 + half
                for v in range(2):
                    w = 2 * half + v
                    dve.wait_ge(*x1_ready.at(it, l * NW + w + 1))
                    dve.wait_ge(*mv2_ready.at(it, 2 * f + v - 1))
                    dve.bn_stats(stats2[:, v, 0, :], X[:, w, 0:P]).then_inc(stats2_ready.sem, 1)
                    dve.wait_ge(*shifted[w].at(it, D16 * (l + 1)))
                    dve.wait_ge(*carried[(w - 1) % NW].at(it, D16 * (l + 1) if w else D16 * (l + 1) - carried[0].per_chunk))
                    dve.bn_stats(stats2[:, v, 1, :], sh[:, l, w, :]).then_inc(stats2_ready.sem, 1)
                for v in range(2):
                    dve.wait_ge(*stats2_ready.at(it, 4 * f + 2 * v + 2))
                    dve.wait_ge(*hn_ready.at(it, 4 * f))
                    dve.sem_inc(passed, 1)
                    dve.bn_aggr(mv2[:, v, :], stats2[:, v, :, :].rearrange("p a b -> p (a b)"))\
                       .then_inc(mv2_ready.sem, 1)
                fill()
                for i in range(NH):
                    rows = P if i < NH - 1 else LAST
                    n = f * NH + i
                    dve.wait_ge(*filled(it, ("h", f, i)))
                    dve.wait_ge(*gelu_ready.at(it, n + 1))
                    b1a = C_B1A + l * NH + i
                    dve.scalar_tensor_tensor(hid[0:rows, i, :], bank(("h", f, i))[0:rows, 0:2 * WIN],
                                             par[0:rows, b1a:b1a + 1], gel[0:rows, i % 2, :], ALU.add, ALU.mult)\
                       .then_inc(hid_ready.sem, 1)
                fill()
                dve.wait_ge(*filled(it, ("w2", f)))
                for w in (2 * half, 2 * half + 1):
                    dve.wait_ge(*shifted[w].at(it, D16 * (l + 1)))
                    dve.wait_ge(*carried[w].at(it, D16 * (l + 1)))
                dve.wait_ge(*hn_ready.at(it, 4 * f + 4))
                dve.tensor_tensor(X[:, 2 * half:2 * half + 2, :],
                                  bank(("w2", f))[:, :].rearrange("p (w d) -> p w d", w=2),
                                  X[:, 2 * half:2 * half + 2, :], ALU.add).then_inc(x2_ready.sem, 1)

            for kind, l, w in ITEMS:
                (attention if kind == "W" else feed_forward)(l, w)
            fill(2)
            assert at_unit[0] == UNITS + 2
            for j in range(NJ):
                dve.wait_ge(*summed.at(it, UNITS - NJ + j + 1))
                dve.scalar_tensor_tensor(xconv[:, j, :], xconv[:, j, :], par[:, C_DP + j:C_DP + j + 1],
                                         ybank[j][:, :], ALU.mult, ALU.add).then_inc(skip_added.sem, 1)
            for j in range(NJ):
                dve.wait_ge(*skip_added.at(it, j + 1))
                dve.wait_ge(*silu_ready.at(it, j + 1))
                dve.tensor_tensor(xconv[:, j, :], xconv[:, j, :], dt_sb[:, j, :], ALU.mult).then_inc(gated.sem, 1)
            dve.wait_ge(*x2_ready.at(it, NF))
            for h in range(2):
                dve.wait_ge(*filled(it, ("out", h)))
                dve.tensor_tensor(X[:, 2 * h:2 * h + 2, :], bank(("out", h))[:, :].rearrange("p (w d) -> p w d", w=2),
                                  X[:, 2 * h:2 * h + 2, :], ALU.add).then_inc(branch_added.sem, 1)

    @block.scalar
    def _(act):
        prime(act, [xnT_ready, xin_ready, tap0_ready, xconv_ready, xdbl_ready, dtv_ready, dtexp_ready,
                    dtlog_ready, dA_ready, silu_ready, sq_ready, v_ready, qT_ready, kT_ready, probs_ready,
                    pT_ready, oT_ready, hT_ready, gelu_ready, x2T_ready])
        act.wait_ge(consts_loaded, N_CONST * D16)
        act.wait_ge(memory_set, N_SET)
        act.activation(amat[:, :], par[:, C_ALOG:C_ALOG + NJ * STATES], ACT.Exp).then_inc(a_exp, 1)
        act.wait_ge(a_exp, 1)
        act.mul(amat[:, :], amat[:, :], -1.0).then_inc(a_ready, 1)
        act.wait_ge(a_ready, 1)

        with act.Fori(0, CHUNKS) as it:
            at_unit = [0]

            def fill(count=1):
                for _ in range(count):
                    k = at_unit[0]
                    n, j = divmod(k, NJ)
                    if n == 0:
                        act.wait_ge(*dt_ready.at(it, j + 1))
                    if k < DA_RING:
                        act.wait_ge(*dt_ready.at(it, NJ))
                        act.wait_ge(*h_ready.at(it, 0))
                    else:
                        act.wait_ge(*h_ready.at(it, k + 1 - DA_RING))
                    act.activation(dA[:, k % DA_RING, :], dt_sb[:, j, :], ACT.Exp,
                                   scale=amat[:, j * STATES + n:j * STATES + n + 1]).then_inc(dA_ready.sem, 1)
                    at_unit[0] += 1

            act.wait_ge(*xnT_carried.at(it, 0))
            for h in range(2):
                act.wait_ge(*filled(it, ("xnT", h)))
                act.activation(xnT[:, :, 1 + h * 256:1 + (h + 1) * 256],
                               bank(("xnT", h))[:, :].rearrange("p (f t) -> p f t", f=FT), ACT.Copy)\
                   .then_inc(xnT_ready.sem, 1)
            act.wait_ge(*halo_ready.at(it, 1))
            act.wait_ge(*hC_ready.at(it, 0))
            act.wait_ge(*gated.at(it, 0))
            for j in range(NJ):
                act.wait_ge(*filled(it, ("xin", j)))
                act.activation(xin[:, j, TAPS - 1:], bank(("xin", j))[:, :], ACT.Copy).then_inc(xin_ready.sem, 1)
            for j in range(NJ):
                act.wait_ge(*xin_ready.at(it, j + 1))
                act.activation(xconv[:, j, :], xin[:, j, 0:T], ACT.Identity,
                               bias=par[:, C_CB + j:C_CB + j + 1],
                               scale=par[:, C_CW + j * TAPS:C_CW + j * TAPS + 1]).then_inc(tap0_ready.sem, 1)
            for j in range(NJ):
                act.wait_ge(*conv_step.at(it, (j + 1) * (TAPS - 1)))
                act.activation(xconv[:, j, :], xconv[:, j, :], ACT.Silu).then_inc(xconv_ready.sem, 1)
            act.wait_ge(*filled(it, ("xdbl",)))
            act.wait_ge(*bc_stored.at(it, 0))
            act.activation(xdbl[:, :], bank(("xdbl",))[0:XROWS, :], ACT.Copy).then_inc(xdbl_ready.sem, 1)
            for j in range(NJ):
                act.wait_ge(*filled(it, ("dt", j)))
                act.activation(dt_sb[:, j, :], bank(("dt", j))[:, :], ACT.Identity,
                               bias=par[:, C_DTB + j:C_DTB + j + 1]).then_inc(dtv_ready.sem, 1)
            for j in range(NJ):
                b = dA[:, j % 3, :]
                act.wait_ge(*dtmin_ready.at(it, j + 1))
                act.activation(b, b, ACT.Exp).then_inc(dtexp_ready.sem, 1)
                act.wait_ge(*dtexp_ready.at(it, j + 1))
                act.activation(b, b, ACT.Ln, bias=1.0).then_inc(dtlog_ready.sem, 1)

            def attention(l, w):
                a = l * NW + w
                act.wait_ge(*normed.at(it, 2 * a))
                act.wait_ge(*ssum_ready.at(it, a))
                for i, name in ((0, "q"), (1, "k")):
                    act.wait_ge(*filled(it, (name, a)))
                    act.activation(sq[:, i, :], bank((name, a))[:, :], ACT.Square).then_inc(sq_ready.sem, 1)
                act.wait_ge(*filled(it, ("v", a)))
                if a:
                    act.wait_ge(*o_ready.at(it, a * PAIRS))
                else:
                    act.wait_ge(*o_ready.at(it, 0))
                act.activation(V[:, l, w % 2, :], bank(("v", a))[:, :], ACT.Copy).then_inc(v_ready.sem, 1)
                fill()
                act.wait_ge(*filled(it, ("qT", a)))
                act.activation(qT[:, :, :], bank(("qT", a))[:, :].rearrange("p (a t) -> p a t", a=PAIRS), ACT.Copy)\
                   .then_inc(qT_ready.sem, 1)
                act.wait_ge(*filled(it, ("kT", a)))
                act.activation(kT[:, l, :, w % 2, :], bank(("kT", a))[:, :].rearrange("p (a t) -> p a t", a=PAIRS),
                               ACT.Copy).then_inc(kT_ready.sem, 1)
                fill()

                def exps(p):
                    n = a * PAIRS + p
                    act.wait_ge(*nmax_ready.at(it, n + 1))
                    act.wait_ge(*rinv_ready.at(it, n + 1 - PAIRS))
                    for hh in range(2):
                        h = 2 * p + hh
                        act.activation(probs[:, p % 2, hh, :], bank(("s", a, p))[:, hh * 256:(hh + 1) * 256], ACT.Exp,
                                       bias=nmax[:, h:h + 1], accum_out=rowsum[:, h:h + 1])\
                           .then_inc(probs_ready.sem, 1)

                exps(0)
                for p in range(PAIRS):
                    n = a * PAIRS + p
                    fill()
                    if p + 1 < PAIRS:
                        exps(p + 1)
                    act.wait_ge(*filled(it, ("pT", a, p)))
                    m = n - 2
                    act.wait_ge(*o_ready.at(it, m + 1))
                    act.activation(pT[:, p % 2, :, :], bank(("pT", a, p))[:, :].rearrange("p (a t) -> p a t", a=4),
                                   ACT.Copy).then_inc(pT_ready.sem, 1)
                fill()
                act.wait_ge(*filled(it, ("oT", a)))
                act.activation(oT[:, :, :], bank(("oT", a))[:, :].rearrange("p (a t) -> p a t", a=NJ), ACT.Copy)\
                   .then_inc(oT_ready.sem, 1)

            def feed_forward(l, half):
                f = l * 2 + half
                fill()
                act.wait_ge(*filled(it, ("hT", f)))
                for ft in range(FT):
                    act.activation(hT[:, ft, :], bank(("hT", f))[:, ft * 256:(ft + 1) * 256], ACT.Identity,
                                   bias=par[:, C_LB + l * FT + ft:C_LB + l * FT + ft + 1],
                                   scale=par[:, C_LG + l * FT + ft:C_LG + l * FT + ft + 1])\
                       .then_inc(hT_ready.sem, 1)
                for i in range(NH):
                    rows = P if i < NH - 1 else LAST
                    n = f * NH + i
                    act.wait_ge(*filled(it, ("h", f, i)))
                    act.wait_ge(*hid_ready.at(it, n - 1))
                    b1g = C_B1G + l * NH + i
                    act.activation(gel[0:rows, i % 2, :], bank(("h", f, i))[0:rows, 256:512], ACT.Gelu,
                                   bias=par[0:rows, b1g:b1g + 1]).then_inc(gelu_ready.sem, 1)
                fill()
                if l == 0:
                    act.wait_ge(*filled(it, ("x2T", half)))
                    act.wait_ge(*x2T_carried.at(it, 0))
                    act.activation(x2T[:, :, 1 + half * 256:1 + (half + 1) * 256],
                                   bank(("x2T", half))[:, :].rearrange("p (f t) -> p f t", f=FT), ACT.Copy)\
                       .then_inc(x2T_ready.sem, 1)

            for kind, l, w in ITEMS:
                (attention if kind == "W" else feed_forward)(l, w)
            assert at_unit[0] == UNITS
            act.wait_ge(*dA_ready.at(it, UNITS))
            for j in range(NJ):
                act.wait_ge(*filled(it, ("z", j)))
                act.activation(dt_sb[:, j, :], bank(("z", j))[:, :], ACT.Silu).then_inc(silu_ready.sem, 1)

    @block.gpsimd
    def _(pool):
        for t in (xnT, x2T, state, halo, V, kT, sh):
            pool.memset(t[tuple(slice(None) for _ in t.shape)], 0.0).then_inc(memory_set, 1)
        pool.memset(powers[:, :], -0.5).then_inc(memory_set, 1)
        pool.memset(hid[:, :, :], 1.0).then_inc(memory_set, 1)
        prime(pool, [eps_added, rstd_ready, halo_ready, halo_saved, dtmin_ready, state_saved, out_ready,
                     xnT_carried, x2T_carried, mask0_ready, ssum_clipped, rnorm_ready, tabs_ready, rot_ready, normed,
                     eps2_added, rstd2_ready, hn_ready])
        pool.wait_ge(consts_loaded, N_CONST * D16)
        pool.wait_ge(memory_set, N_SET)

        with pool.Fori(0, CHUNKS) as it:
            at_unit = [0]

            def fill(count=1):
                for _ in range(count):
                    k = at_unit[0] - 1
                    if k >= 0:
                        pool.wait_ge(*h_ready.at(it, k + 1))
                        pool.sem_inc(passed, 1)
                        pool.tensor_copy(state[:, k:k + 1], hb[:, k % H_RING, T - 1:T]).then_inc(state_saved.sem, 1)
                    at_unit[0] += 1

            pool.wait_ge(*halo_saved.at(it, 0))
            pool.wait_ge(*hC_ready.at(it, 0))
            pool.sem_inc(passed, 1)
            pool.tensor_copy(xin[:, :, 0:TAPS - 1], halo[:, :, :]).then_inc(halo_ready.sem, 1)
            pool.wait_ge(*mv_ready.at(it, NW))
            pool.wait_ge(*xn_ready.at(it, 0))
            pool.sem_inc(passed, 1)
            pool.tensor_scalar(rstd[:, :], mv[:, :, 1], EPS, None, ALU.add).then_inc(eps_added.sem, 1)
            pool.wait_ge(*eps_added.at(it, 1))
            pool.sem_inc(passed, 1)
            pool.tensor_tensor(rstd[:, :], rstd[:, :], powers[:, 0:NW], ALU.pow).then_inc(rstd_ready.sem, 1)
            pool.wait_ge(*xin_ready.at(it, NJ))
            pool.wait_ge(*halo_ready.at(it, 1))
            pool.sem_inc(passed, 1)
            pool.tensor_copy(halo[:, :, :], xin[:, :, T:T + TAPS - 1]).then_inc(halo_saved.sem, 1)
            for j in range(NJ):
                pool.wait_ge(*dtv_ready.at(it, j + 1))
                pool.sem_inc(passed, 1)
                if j >= 3:
                    pool.wait_ge(*dt_ready.at(it, j - 2))
                    pool.sem_inc(passed, 1)
                else:
                    pool.wait_ge(*h_ready.at(it, 0))
                    pool.sem_inc(passed, 1)
                pool.tensor_scalar(dA[:, j % 3, :], dt_sb[:, j, :], 40.0, None, ALU.min).then_inc(dtmin_ready.sem, 1)

            def attention(l, w):
                a = l * NW + w
                pool.wait_ge(*tab_loaded[a % 2].at(it, D16 * (a // 2 + 1)))
                pool.wait_ge(*sin_ready.at(it, 2 * a))
                pool.sem_inc(passed, 1)
                pool.tensor_tensor(tabs[:, :, :], tab[:, a % 2, :, :], qks[:, l, :, :], ALU.mult)\
                    .then_inc(tabs_ready.sem, 1)
                pool.wait_ge(*ssum_ready.at(it, a + 1))
                pool.wait_ge(*normed.at(it, 2 * a))
                pool.sem_inc(passed, 1)
                pool.tensor_scalar(rnorm[:, :], ssum[:, :], 1e-24, None, ALU.max).then_inc(ssum_clipped.sem, 1)
                pool.wait_ge(*ssum_clipped.at(it, a + 1))
                pool.sem_inc(passed, 1)
                pool.tensor_tensor(rnorm[:, :], rnorm[:, :], powers[:, :], ALU.pow).then_inc(rnorm_ready.sem, 1)
                for i in range(2):
                    n = 2 * a + i
                    pool.wait_ge(*cos_ready.at(it, n + 1))
                    pool.wait_ge(*sin_ready.at(it, n + 1))
                    pool.sem_inc(passed, 1)
                    pool.tensor_tensor(rot[:, i, :], rot[:, i, :], sq[:, i, :], ALU.add).then_inc(rot_ready.sem, 1)
                    pool.wait_ge(*rot_ready.at(it, n + 1))
                    pool.wait_ge(*rnorm_ready.at(it, a + 1))
                    pool.sem_inc(passed, 1)
                    r = rot[:, i, :].rearrange("p (h d) -> p h d", d=DH)
                    pool.tensor_tensor(r, r, rnorm[:, i * HEADS:(i + 1) * HEADS].unsqueeze(2)
                                       .to_broadcast([P, HEADS, DH]), ALU.mult).then_inc(normed.sem, 1)
                fill(7)

            def feed_forward(l, half):
                f = l * 2 + half
                pool.wait_ge(*mv2_ready.at(it, 2 * f + 2))
                pool.wait_ge(*hn_ready.at(it, 4 * f))
                pool.sem_inc(passed, 1)
                pool.tensor_scalar(rstd2[:, :], mv2[:, :, 1], EPS, None, ALU.add).then_inc(eps2_added.sem, 1)
                pool.wait_ge(*eps2_added.at(it, f + 1))
                pool.sem_inc(passed, 1)
                pool.tensor_tensor(rstd2[:, :], rstd2[:, :], powers[:, 0:2], ALU.pow).then_inc(rstd2_ready.sem, 1)
                pool.wait_ge(*rstd2_ready.at(it, f + 1))
                pool.sem_inc(passed, 1)
                for v in range(2):
                    w = 2 * half + v
                    for ft, src in ((0, X[:, w, 0:P]), (1, sh[:, l, w, :])):
                        pool.tensor_scalar(hn[:, v, ft * P:(ft + 1) * P], src, mv2[:, v, 0:1], rstd2[:, v:v + 1],
                                           ALU.subtract, ALU.mult).then_inc(hn_ready.sem, 1)
                fill(2)

            for kind, l, w in ITEMS:
                (attention if kind == "W" else feed_forward)(l, w)
            fill(1)
            n = at[("z", NJ - 1)]
            pool.wait_ge(*full[n % BANKS].at(it, n // BANKS + 1 + done(("z", NJ - 1))[1] - 1))
            pool.sem_inc(passed, 1)
            pool.tensor_copy(xnT[:, 1, 0:1], xnT[:, 1, T:T + 1]).then_inc(xnT_carried.sem, 1)
            n = at[("v", NA - 1)]
            pool.wait_ge(*full[n % BANKS].at(it, n // BANKS + 1))
            pool.sem_inc(passed, 1)
            pool.tensor_copy(x2T[:, 1, 0:1], x2T[:, 1, T:T + 1]).then_inc(x2T_carried.sem, 1)
            pool.wait_ge(*probs_ready.at(it, HEADS * (NW + 1)))
            pool.sem_inc(passed, 1)
            pool.tensor_copy(mask0[:, :], mask[:, 0, :]).then_inc(mask0_ready.sem, 1)
            pool.wait_ge(*branch_added.at(it, 2))
            pool.sem_inc(passed, 1)
            pool.tensor_tensor(X[:, :, :], X[:, :, :], xtok[:, :, :], ALU.add).then_inc(out_ready.sem, 1)

    @block.tensor
    def _(pe):
        prime(pe, [*full, summed])
        pe.wait_ge(consts_loaded, N_CONST * D16)
        pe.wait_ge(memory_set, N_SET)
        pe.wait_ge(casts_done, 3)

        with pe.Fori(0, CHUNKS) as it:
            at_unit = [0]

            def fill(count=1):
                for _ in range(count):
                    k = at_unit[0] - 2
                    if 0 <= k < UNITS:
                        n, j = divmod(k, NJ)
                        pe.wait_ge(*hC_ready.at(it, k + 1))
                        if n == 0:
                            pe.wait_ge(*skip_added.at(it, j + 1 - NJ))
                        pe.matmul(ybank[j][:, :], ident[:, :], hb[:, k % H_RING, :], start=(n == 0),
                                  stop=(n == STATES - 1)).then_inc(summed.sem, 1)
                    at_unit[0] += 1

            for h in range(2):
                pe.wait_ge(*xn_ready.at(it, 2 * h + 2))
                pe.wait_ge(*freed(it, ("xnT", h)))
                for ft in range(FT):
                    for v in range(2):
                        m = pe.transpose(bank(("xnT", h))[:, ft * 256 + v * P:ft * 256 + (v + 1) * P],
                                         X[:, 2 * h + v, ft * P:(ft + 1) * P], ident[:, :])
                m.then_inc(*done(("xnT", h)))

            def in_proj(name, j, col):
                pe.wait_ge(*freed(it, (name, j)))
                for ft in range(FT):
                    m = pe.matmul(bank((name, j))[:, :], inw[:, ft, col:col + P], xnT[:, ft, 1:1 + T],
                                  start=(ft == 0), stop=(ft == FT - 1))
                m.then_inc(*done((name, j)))

            pe.wait_ge(*xnT_ready.at(it, 2))
            for j in range(NJ):
                in_proj("xin", j, j * P)
            pe.wait_ge(*freed(it, ("xdbl",)))
            for j in range(NJ):
                pe.wait_ge(*xconv_ready.at(it, j + 1))
                m = pe.matmul(bank(("xdbl",))[0:XROWS, :], xpw[:, j, :], xconv[:, j, :],
                              start=(j == 0), stop=(j == NJ - 1))
            m.then_inc(*done(("xdbl",)))
            pe.wait_ge(*xdbl_ready.at(it, 1))
            for j in range(NJ):
                pe.wait_ge(*freed(it, ("dt", j)))
                pe.matmul(bank(("dt", j))[:, :], dtw[2 * STATES:XROWS, j * P:(j + 1) * P],
                          xdbl[2 * STATES:XROWS, :], start=True, stop=True).then_inc(*done(("dt", j)))

            def attention(l, w):
                a = l * NW + w
                src = x2T if l else xnT
                if w == 0:
                    pe.wait_ge(*wqkv_loaded.at(it, D16 * (l + 1)))
                if l:
                    pe.wait_ge(*x2T_ready.at(it, w // 2 + 1))
                for i, name in enumerate(("q", "k", "v")):
                    pe.wait_ge(*freed(it, (name, a)))
                    for ft in range(FT):
                        off = w * WIN + (1 - ft)
                        m = pe.matmul(bank((name, a))[:, :], src[:, ft, off:off + WIN],
                                      wqkv[:, ft, i * 512:(i + 1) * 512], start=(ft == 0), stop=(ft == FT - 1))
                    m.then_inc(*done((name, a)))
                fill()
                for i, name in enumerate(("qT", "kT")):
                    pe.wait_ge(*normed.at(it, 2 * a + i + 1))
                    pe.wait_ge(*freed(it, (name, a)))
                    for p in range(PAIRS):
                        m = pe.transpose(bank((name, a))[:, p * P:(p + 1) * P], rot[:, i, p * P:(p + 1) * P], ident[:, :])
                    m.then_inc(*done((name, a)))
                fill()
                pe.wait_ge(*qT_ready.at(it, a + 1))
                pe.wait_ge(*kT_ready.at(it, a + 1))
                if a == 0:
                    pe.wait_ge(*mask0_ready.at(it, 0))

                def scores(p):
                    pe.wait_ge(*freed(it, ("s", a, p)))
                    s = bank(("s", a, p))
                    msk = mask0[:, :] if w == 0 else mask[:, w % 2, :]
                    for hh in range(2):
                        pe.matmul(s[:, hh * 256:(hh + 1) * 256], identb[:, :], msk, start=(hh == 0), stop=False,
                                  skip_group_check=True)
                    for hh, h in enumerate(heads_of(p)):
                        rows = slice((h % 2) * DH, (h % 2 + 1) * DH)
                        m = pe.matmul(s[:, hh * 256:(hh + 1) * 256], qT[rows, h // 2, :],
                                      kT[rows, l, h // 2, :, :].rearrange("p a b -> p (a b)"),
                                      start=False, stop=True, skip_group_check=True)
                    m.then_inc(*done(("s", a, p)))

                scores(0)
                scores(1)
                pe.wait_ge(*v_ready.at(it, a + 1))
                for p in range(PAIRS):
                    n = a * PAIRS + p
                    fill()
                    pe.wait_ge(*probs_ready.at(it, 2 * n + 2))
                    pe.wait_ge(*freed(it, ("pT", a, p)))
                    for hh in range(2):
                        for s in range(2):
                            q = 2 * hh + s
                            m = pe.transpose(bank(("pT", a, p))[:, q * P:(q + 1) * P],
                                             probs[:, p % 2, hh, s * WIN:(s + 1) * WIN], ident[:, :])
                    m.then_inc(*done(("pT", a, p)))
                    pe.wait_ge(*pT_ready.at(it, n + 1))
                    pe.wait_ge(*freed(it, ("o", a, p)))
                    for hh, h in enumerate(heads_of(p)):
                        for s in range(2):
                            m = pe.matmul(bank(("o", a, p))[:, hh * DH:(hh + 1) * DH], pT[:, p % 2, 2 * hh + s, :],
                                          V[:, l, s, h * DH:(h + 1) * DH], start=(s == 0), stop=(s == 1))
                    m.then_inc(*done(("o", a, p)))
                    if p + 2 < PAIRS:
                        scores(p + 2)
                pe.wait_ge(*o_ready.at(it, (a + 1) * PAIRS))
                pe.wait_ge(*freed(it, ("oT", a)))
                for k in range(NJ):
                    m = pe.transpose(bank(("oT", a))[:, k * P:(k + 1) * P], o_sb[:, k * P:(k + 1) * P], ident[:, :])
                m.then_inc(*done(("oT", a)))
                fill()
                pe.wait_ge(*oT_ready.at(it, a + 1))
                pe.wait_ge(*freed(it, ("wo", a)))
                for k in range(NJ):
                    m = pe.matmul(bank(("wo", a))[:, 0:D], oT[:, k, :], wo[:, l, k, :], start=(k == 0), stop=(k == NJ - 1))
                m.then_inc(*done(("wo", a)))

            def feed_forward(l, half):
                f = l * 2 + half
                fill()
                pe.wait_ge(*hn_ready.at(it, 4 * f + 4))
                pe.wait_ge(*freed(it, ("hT", f)))
                for ft in range(FT):
                    for v in range(2):
                        m = pe.transpose(bank(("hT", f))[:, ft * 256 + v * P:ft * 256 + (v + 1) * P],
                                         hn[:, v, ft * P:(ft + 1) * P], ident[:, :])
                m.then_inc(*done(("hT", f)))
                pe.wait_ge(*hT_ready.at(it, FT * (f + 1)))
                for i in range(NH):
                    rows = P if i < NH - 1 else LAST
                    pe.wait_ge(*freed(it, ("h", f, i)))
                    for part in range(2):
                        for ft in range(FT):
                            col = part * HID + i * P
                            m = pe.matmul(bank(("h", f, i))[0:rows, part * 256:(part + 1) * 256],
                                          w1[:, l, ft, col:col + rows], hT[:, ft, :], start=(ft == 0), stop=(ft == FT - 1))
                    m.then_inc(*done(("h", f, i)))
                pe.wait_ge(*freed(it, ("w2", f)))
                for v in range(2):
                    for i in range(NH):
                        rows = P if i < NH - 1 else LAST + 1
                        pe.wait_ge(*hid_ready.at(it, f * NH + (i + 1 if v == 0 else NH)))
                        m = pe.matmul(bank(("w2", f))[:, v * D:(v + 1) * D], hid[0:rows, i, v * WIN:(v + 1) * WIN],
                                      w2[0:rows, l, i, :], start=(i == 0), stop=(i == NH - 1))
                m.then_inc(*done(("w2", f)))
                fill()
                if l == 0:
                    pe.wait_ge(*x2_ready.at(it, f + 1))
                    pe.wait_ge(*freed(it, ("x2T", half)))
                    for ft in range(FT):
                        for v in range(2):
                            m = pe.transpose(bank(("x2T", half))[:, ft * 256 + v * P:ft * 256 + (v + 1) * P],
                                             X[:, 2 * half + v, ft * P:(ft + 1) * P], ident[:, :])
                    m.then_inc(*done(("x2T", half)))

            for kind, l, w in ITEMS:
                (attention if kind == "W" else feed_forward)(l, w)
            fill(2)
            for j in range(NJ):
                in_proj("z", j, INNER + j * P)
            for h in range(2):
                pe.wait_ge(*freed(it, ("out", h)))
                for v in range(2):
                    for j in range(NJ):
                        pe.wait_ge(*gated.at(it, j + 1))
                        m = pe.matmul(bank(("out", h))[:, v * D:(v + 1) * D],
                                      xconv[:, j, (2 * h + v) * WIN:(2 * h + v + 1) * WIN], outw[:, j, :],
                                      start=(j == 0), stop=(j == NJ - 1))
                m.then_inc(*done(("out", h)))

    ctx.close()


W_FILLS, F_FILLS = 7, 2
N_CONST, N_SET = 12, 9


def constants():
    f = np.float32
    half = np.arange(0, DH, 2, dtype=f)
    freq = (f(1.0) / f(10000.0) ** (half / f(DH))).astype(f)
    t = np.arange(TOKENS, dtype=f)
    ang = t[:, None] * freq[None, :]
    ang = np.concatenate([ang, ang], axis=-1)
    base = (half + f(0.4 * DH)) / f(1.4 * DH)
    power = (t - TOKENS // 2) / f(WIN // 2)
    scale = base[None, :] ** power[:, None]
    scale = np.concatenate([scale, scale], axis=-1)
    cos, sin = np.cos(ang), np.sin(ang)
    sign = np.concatenate([-np.ones(DH // 2, f), np.ones(DH // 2, f)])
    tab = np.stack([8.0 * cos * scale, 8.0 * sin * scale * sign, cos / scale, sin / scale * sign], axis=1)
    q = np.arange(WIN)[:, None]
    k = np.arange(WIN)[None, :]
    own = np.where(k <= q, 0.0, NEG)
    prev = np.where(k >= q, 0.0, NEG)
    never = np.full((WIN, WIN), NEG)
    mask = np.stack([np.concatenate([own, prev], 1), np.concatenate([prev, own], 1)], axis=1).reshape(P, 4 * WIN).astype(f)
    mask0 = np.concatenate([own, never], 1).astype(f)
    eye = np.eye(P, dtype=f)
    return {"tab": np.ascontiguousarray(tab.astype(f)), "mask": mask, "mask0": mask0, "ident": eye}


def kernel(L0_attn_x, L0_attn_in_proj_w, L0_attn_conv_w, L0_attn_conv_b, L0_attn_x_proj_w, L0_attn_dt_proj_w,
           L0_attn_dt_proj_b, L0_attn_A_log, L0_attn_D_param, L0_attn_out_proj_w, L0_ffn_wqkv, L0_ffn_q_scale,
           L0_ffn_k_scale, L0_ffn_wo, L0_ffn_ln_g, L0_ffn_ln_b, L0_ffn_w1, L0_ffn_b1, L0_ffn_w2, L0_ffn_b2):
    import concourse.bacc as bacc
    from concourse.bass_utils import run_bass_kernel_spmd
    f = np.float32

    def tiles(a, n):
        a = np.asarray(a)
        return np.ascontiguousarray(np.moveaxis(a.reshape(n, P, *a.shape[1:]), 0, 1))

    xp = np.asarray(L0_attn_x_proj_w)
    ssm = xp[RANK:].reshape(2, STATES, INNER).transpose(1, 0, 2).reshape(2 * STATES, INNER)
    xp = np.concatenate([ssm, xp[:RANK]], axis=0)
    b1 = np.asarray(L0_ffn_b1).reshape(LAYERS, 2, HID)
    b1p = np.zeros((2, LAYERS, NH * P), f)
    b1p[:, :, :HID] = np.moveaxis(b1, 1, 0)
    w2p = np.zeros((LAYERS, NH * P, D), f)
    w2p[:, :HID] = np.asarray(L0_ffn_w2)
    w2p[:, HID] = np.asarray(L0_ffn_b2)

    def cols(a, n):
        return np.asarray(a).reshape(n, P).T

    par = np.concatenate([
        tiles(L0_attn_A_log, NJ).reshape(P, -1),
        tiles(np.asarray(L0_attn_conv_w).reshape(INNER, TAPS), NJ).reshape(P, -1),
        cols(L0_attn_conv_b, NJ), cols(L0_attn_dt_proj_b, NJ), cols(L0_attn_D_param, NJ),
        cols(L0_ffn_ln_g, LAYERS * FT), cols(L0_ffn_ln_b, LAYERS * FT),
        cols(b1p[0], LAYERS * NH), cols(b1p[1], LAYERS * NH)], axis=1)
    qs, ks = np.asarray(L0_ffn_q_scale), np.asarray(L0_ffn_k_scale)
    qks = np.stack([qs, np.roll(qs, DH // 2, axis=1), ks, np.roll(ks, DH // 2, axis=1)], axis=1)
    arrays = {
        "x": np.asarray(L0_attn_x).reshape(TOKENS, D),
        "inw": tiles(np.asarray(L0_attn_in_proj_w).T, FT),
        "xpw": tiles(xp.T, NJ),
        "dtw": np.asarray(L0_attn_dt_proj_w).T,
        "outw": tiles(np.asarray(L0_attn_out_proj_w).T, NJ),
        "wqkv": np.moveaxis(np.asarray(L0_ffn_wqkv).reshape(LAYERS, FT, P, QKV), 2, 0),
        "wo": np.moveaxis(np.asarray(L0_ffn_wo).reshape(LAYERS, NJ, P, D), 2, 0),
        "w1": np.moveaxis(np.asarray(L0_ffn_w1).reshape(LAYERS, FT, P, 2 * HID), 2, 0),
        "w2": np.moveaxis(w2p.reshape(LAYERS, NH, P, D), 2, 0),
        "qks": np.broadcast_to(qks[None], (P, LAYERS, 4, DH)),
        "par": par,
        **constants(),
    }
    arrays = {k: np.ascontiguousarray(v) for k, v in arrays.items()}
    nc = bacc.Bacc("TRN2", target_bir_lowering=False, num_devices=1)
    io = {k: nc.dram_tensor(f"in_{k}", v.shape, mybir.dt.from_np(v.dtype), kind="ExternalInput").ap()
          for k, v in arrays.items()}
    io["out"] = nc.dram_tensor("out_y", (TOKENS, D), mybir.dt.float32, kind="ExternalOutput").ap()
    build(nc, io)
    r = run_bass_kernel_spmd(nc, [{f"in_{k}": v for k, v in arrays.items()}], core_ids=[0])
    return r.results[0]["out_y"].reshape(1, TOKENS, D)
```

```python
import numpy as np
import concourse.bass as bass
from concourse import mybir
from contextlib import ExitStack

P = 128
TOKENS, D = 4096, 256
T = 512
CHUNKS = TOKENS // T
WIN = 128
NW = T // WIN
FT = D // P
INNER = 512
NJ = INNER // P
STATES = 16
TAPS = 4
RANK = 16
XROWS = 2 * STATES + RANK
HEADS, DH = 8, 64
PAIRS = HEADS // 2
QKV = 3 * HEADS * DH
HID = 682
NH = -(-HID // P)
LAST = HID - (NH - 1) * P
LAYERS = 2
EPS = 1e-5
UNITS = STATES * NJ
GROUP = 2
NGROUPS = STATES // GROUP
DA_RING, H_RING = 3, 4
BANKS = 4
NEG = -1e30
C_ALOG = 0
C_CW = C_ALOG + NJ * STATES
C_CB = C_CW + NJ * TAPS
C_DTB = C_CB + NJ
C_DP = C_DTB + NJ
C_LG = C_DP + NJ
C_LB = C_LG + LAYERS * FT
C_B1A = C_LB + LAYERS * FT
C_B1G = C_B1A + LAYERS * NH
NPAR = C_B1G + LAYERS * NH


def build(nc, io):
    f32, bf16 = mybir.dt.float32, mybir.dt.bfloat16
    ALU, ACT = mybir.AluOpType, mybir.ActivationFunctionType
    AX = mybir.AxisListType
    ctx = ExitStack()

    def sb(name, shape, dt=f32):
        return ctx.enter_context(nc.sbuf_tensor(name, shape, dt))

    inw = sb("inw", [P, FT, 2 * INNER])
    xpw = sb("xpw", [P, NJ, XROWS])
    dtw = sb("dtw", [XROWS, INNER])
    outw = sb("outw", [P, NJ, D])
    wo = sb("wo", [P, LAYERS, NJ, D])
    w1 = sb("w1", [P, LAYERS, FT, 2 * HID])
    w2 = sb("w2", [P, LAYERS, NH, D])
    par = sb("par", [P, NPAR])
    qks = sb("qks", [P, LAYERS, 4, DH])
    ident = sb("ident", [P, P])
    identb = sb("identb", [P, P], bf16)
    mask = sb("mask", [P, 2, 2 * WIN], bf16)
    mask0 = sb("mask0", [P, 2 * WIN], bf16)
    amat = sb("amat", [P, NJ * STATES])
    powers = sb("powers", [P, HEADS * 2])
    wqkv = sb("wqkv", [P, FT, QKV])
    xtok = sb("xtok", [P, NW, D])
    tab = sb("tab", [P, 2, 4, DH])
    bc = sb("bc", [P, 2, GROUP, 2, T])
    xnT = sb("xnT", [P, FT, 1 + T])
    xin = sb("xin", [P, NJ, TAPS - 1 + T])
    halo = sb("halo", [P, NJ, TAPS - 1])
    xconv = sb("xconv", [P, NJ, T])
    dt_sb = sb("dt_sb", [P, NJ, T])
    xdbl = sb("xdbl", [XROWS, T])
    dA = sb("dA", [P, DA_RING, T])
    hb = sb("hb", [P, H_RING, T])
    state = sb("state", [P, UNITS])
    X = sb("X", [P, NW, D])
    stats = sb("stats", [P, NW, 2, 6])
    mv = sb("mv", [P, NW, 2])
    rstd = sb("rstd", [P, NW])
    x2T = sb("x2T", [P, FT, 1 + T])
    sq = sb("sq", [P, 2, HEADS * DH])
    rot = sb("rot", [P, 2, HEADS * DH])
    ssum = sb("ssum", [P, 2 * HEADS])
    rnorm = sb("rnorm", [P, 2 * HEADS])
    tabs = sb("tabs", [P, 4, DH])
    qT = sb("qT", [P, PAIRS, WIN])
    kT = sb("kT", [P, LAYERS, PAIRS, 2, WIN])
    V = sb("V", [P, LAYERS, 2, HEADS * DH])
    nmax = sb("nmax", [P, HEADS])
    rowsum = sb("rowsum", [P, HEADS])
    rinv = sb("rinv", [P, HEADS])
    probs = sb("probs", [P, 2, 2, 2 * WIN])
    pT = sb("pT", [P, 2, 4, WIN])
    o_sb = sb("o_sb", [P, HEADS * DH])
    oT = sb("oT", [P, NJ, WIN])
    sh = sb("sh", [P, LAYERS, NW, P])
    stats2 = sb("stats2", [P, 2, 2, 6])
    mv2 = sb("mv2", [P, 2, 2])
    rstd2 = sb("rstd2", [P, 2])
    hn = sb("hn", [P, 2, D])
    hT = sb("hT", [P, FT, 2 * WIN])
    gel = sb("gel", [P, 2, 2 * WIN])
    hid = sb("hid", [P, NH, 2 * WIN])
    scratch = nc.dram_tensor("bc_rows", [2 * STATES, T], f32, kind="Internal").ap()

    ybank = [ctx.enter_context(nc.psum_tensor(f"ysum{j}", [P, T], f32)) for j in range(NJ)]
    ring = [ctx.enter_context(nc.psum_tensor(f"ring{b}", [P, T], f32)) for b in range(BANKS)]

    class Signal:
        def __init__(self, name, per_chunk):
            self.sem = ctx.enter_context(nc.semaphore(name))
            self.per_chunk = per_chunk

        def at(self, it, count):
            assert -self.per_chunk < count <= self.per_chunk, (self.sem, count)
            return self.sem, it * self.per_chunk + (self.per_chunk + count)

    passed = ctx.enter_context(nc.semaphore("passed"))
    D16 = 16
    x_loaded = Signal("x_loaded", D16)
    mask0_ready = Signal("mask0_ready", 1)
    tab_loaded = [Signal(f"tab_loaded{s}", D16 * LAYERS * NW // 2) for s in range(2)]
    wqkv_loaded = [Signal(f"w{c}_loaded", D16 * LAYERS) for c in "qkv"]
    bc_stored = Signal("bc_stored", D16)
    bc_loaded = [Signal(f"bc_loaded{s}", D16 * NGROUPS // 2) for s in range(2)]
    shifted = [Signal(f"shifted{w}", D16 * LAYERS) for w in range(NW)]
    carried = [Signal(f"carried{w}", D16 * LAYERS) for w in range(NW)]
    out_stored = Signal("out_stored", D16)
    stats_ready = Signal("stats_ready", NW)
    mv_ready = Signal("mv_ready", NW)
    eps_added = Signal("eps_added", 1)
    rstd_ready = Signal("rstd_ready", 1)
    xn_ready = Signal("xn_ready", NW)
    full = [Signal(f"bank_full{b}", 0) for b in range(BANKS)]
    xnT_ready = Signal("xnT_ready", 2)
    halo_ready = Signal("halo_ready", 1)
    halo_saved = Signal("halo_saved", 1)
    xin_ready = Signal("xin_ready", NJ)
    tap0_ready = Signal("tap0_ready", NJ)
    conv_step = Signal("conv_step", NJ * (TAPS - 1))
    xconv_ready = Signal("xconv_ready", NJ)
    xdbl_ready = Signal("xdbl_ready", 1)
    dtv_ready = Signal("dtv_ready", NJ)
    dtmin_ready = Signal("dtmin_ready", NJ)
    dtexp_ready = Signal("dtexp_ready", NJ)
    dtlog_ready = Signal("dtlog_ready", NJ)
    dt_ready = Signal("dt_ready", NJ)
    u_ready = Signal("u_ready", NJ)
    dA_ready = Signal("dA_ready", UNITS)
    dBx_ready = Signal("dBx_ready", UNITS)
    h_ready = Signal("h_ready", UNITS)
    state_saved = Signal("state_saved", UNITS)
    hC_ready = Signal("hC_ready", UNITS)
    summed = Signal("summed", UNITS)
    silu_ready = Signal("silu_ready", NJ)
    skip_added = Signal("skip_added", NJ)
    gated = Signal("gated", NJ)
    branch_added = Signal("branch_added", 2)
    out_ready = Signal("out_ready", 1)
    xnT_carried = Signal("xnT_carried", 1)
    x2T_carried = Signal("x2T_carried", 1)
    NA = LAYERS * NW
    sq_ready = Signal("sq_ready", 2 * NA)
    ssum_ready = Signal("ssum_ready", 2 * NA)
    ssum_clipped = Signal("ssum_clipped", 2 * NA)
    rnorm_ready = Signal("rnorm_ready", 2 * NA)
    tabs_ready = Signal("tabs_ready", NA)
    sine_ready = Signal("sine_ready", 2 * NA)
    rotary_ready = Signal("rotary_ready", 2 * NA)
    rot_ready = Signal("rot_ready", 2 * NA)
    normed = Signal("normed", 2 * NA)
    v_ready = Signal("v_ready", NA)
    qT_ready = Signal("qT_ready", NA)
    kT_ready = Signal("kT_ready", NA)
    nmax_ready = Signal("nmax_ready", PAIRS * NA)
    probs_ready = Signal("probs_ready", HEADS * NA)
    pT_ready = Signal("pT_ready", PAIRS * NA)
    rinv_ready = Signal("rinv_ready", PAIRS * NA)
    o_ready = Signal("o_ready", PAIRS * NA)
    oT_ready = Signal("oT_ready", NA)
    x1_ready = Signal("x1_ready", NA)
    NF = LAYERS * 2
    stats2_ready = Signal("stats2_ready", 4 * NF)
    mv2_ready = Signal("mv2_ready", 2 * NF)
    eps2_added = Signal("eps2_added", NF)
    rstd2_ready = Signal("rstd2_ready", NF)
    hn_ready = Signal("hn_ready", 4 * NF)
    hT_ready = Signal("hT_ready", FT * NF)
    gelu_ready = Signal("gelu_ready", NH * NF)
    hid_ready = Signal("hid_ready", NH * NF)
    x2_ready = Signal("x2_ready", NF)
    x2T_ready = Signal("x2T_ready", 2)
    consts_loaded = ctx.enter_context(nc.semaphore("consts_loaded"))
    memory_set = ctx.enter_context(nc.semaphore("memory_set"))
    casts_done = ctx.enter_context(nc.semaphore("casts_done"))
    a_exp = ctx.enter_context(nc.semaphore("a_exp"))
    a_ready = ctx.enter_context(nc.semaphore("a_ready"))

    TIMELINE = [("norm",), ("xnT", 0), ("xnT", 1), ("q", 0), ("k", 0), ("heads", 0), ("v", 0), ("s", 0, 0)]
    SCAN, LONG = [("scan",)], [("scan",)] * 2
    SIDE = {0: [[("in", 0), ("in", 1)], [("in", 2), ("in", 3)], [("conv", 0), ("conv", 1)],
                [("conv", 2), ("conv", 3), ("silu",)]],
            1: [[("xdbl",)], [("dt", 0), ("dt", 1), ("dt", 2), ("dt", 3)], [("softplus",)], [("u",)]],
            NA - 1: [LONG, LONG, LONG, LONG]}

    def window(a):
        for p in range(PAIRS):
            side = SIDE.get(a, [LONG, LONG, LONG, SCAN])[p]
            if p == 1 and a:
                yield "oT", a - 1
            if p == PAIRS - 1 and a + 1 < NA:
                yield "heads", a + 1
                yield "o", a, p - 1
                yield from side
                yield "s", a + 1, 0
            else:
                if p < PAIRS - 1:
                    yield "s", a, p + 1
                if p:
                    yield "o", a, p - 1
                elif a:
                    yield "o", a - 1, PAIRS - 1
                    yield "v", a
                yield from side
            yield "pT", a, p
            if p == 1 and a:
                yield "wo", a - 1
            if a + 1 < NA and p in (1, 2):
                yield "qk"[p - 1], a + 1

    def feed(f, side):
        yield "stats", f
        yield from side[0]
        yield "hn", f
        yield from side[1]
        yield "hT", f
        for i in range(NH):
            yield "h", f, i
            if i == NH // 2 - 1:
                yield from side[2]
        yield from side[3]
        yield "w2", f
        yield from side[4]
        if f < 2:
            yield "x2T", f

    for kind, n in (("W", 0), ("W", 1), ("W", 2), ("F", 0), ("W", 3), ("W", 4), ("F", 1),
                    ("W", 5), ("W", 6), ("F", 2), ("W", 7)):
        if kind == "W":
            TIMELINE += window(n)
        else:
            TIMELINE += feed(n, [SCAN, SCAN, SCAN * 3, SCAN, LONG])
    TIMELINE += [("o", NA - 1, PAIRS - 1), ("oT", NA - 1), ("skip",), ("wo", NA - 1)]
    TIMELINE += feed(NF - 1, [[]] * 5)
    TIMELINE += [("z", j) for j in range(NJ)] + [("gate",), ("out", 0), ("out", 1), ("last",)]
    assert TIMELINE.count(("scan",)) == UNITS + 3

    order, emptied = [], {}

    def group(name, read):
        order.append(name)
        emptied[name] = read

    for stage, *n in TIMELINE:
        if stage == "xnT":
            group(("xnT", n[0]), (xnT_ready, n[0] + 1))
        elif stage == "in":
            group(("xin", n[0]), (xin_ready, n[0] + 1))
        elif stage == "xdbl":
            group(("xdbl",), (xdbl_ready, 1))
        elif stage == "dt":
            group(("dt", n[0]), (dtv_ready, n[0] + 1))
        elif stage in ("q", "k"):
            group((stage, n[0]), (rotary_ready, 2 * n[0] + 1 + (stage == "k")))
        elif stage == "v":
            group(("v", n[0]), (v_ready, n[0] + 1))
        elif stage == "heads":
            group(("kT", n[0]), (kT_ready, n[0] + 1))
            group(("qT", n[0]), (qT_ready, n[0] + 1))
        elif stage == "s":
            group(("s", *n), (probs_ready, n[0] * HEADS + 2 * n[1] + 2))
        elif stage == "pT":
            group(("pT", *n), (pT_ready, n[0] * PAIRS + n[1] + 1))
        elif stage == "o":
            group(("o", *n), (o_ready, n[0] * PAIRS + n[1] + 1))
        elif stage == "oT":
            group(("oT", n[0]), (oT_ready, n[0] + 1))
        elif stage == "wo":
            group(("wo", n[0]), (x1_ready, n[0] + 1))
        elif stage == "hT":
            group(("hT", n[0]), (hT_ready, FT * (n[0] + 1)))
        elif stage == "h":
            group(("h", *n), (hid_ready, n[0] * NH + n[1] + 1))
        elif stage == "w2":
            group(("w2", n[0]), (x2_ready, n[0] + 1))
        elif stage == "x2T":
            group(("x2T", n[0]), (x2T_ready, n[0] + 1))
        elif stage == "z":
            group(("z", n[0]), (silu_ready, n[0] + 1))
        elif stage == "out":
            group(("out", n[0]), (branch_added, n[0] + 1))
    while len(order) % BANKS:
        order.append(None)
    at = {name: n for n, name in enumerate(order) if name}
    for s in full:
        s.per_chunk = len(order) // BANKS

    def bank(name):
        return ring[at[name] % BANKS]

    def freed(it, name):
        n = at[name] - BANKS
        while order[n] is None:
            n -= BANKS
        sig, count = emptied[order[n]]
        return sig.at(it, count if n >= 0 else count - sig.per_chunk)

    def done(name):
        n = at[name]
        spare = n + BANKS < len(order) and order[n + BANKS] is None
        return full[n % BANKS].sem, 2 if spare else 1

    def filled(it, name):
        n = at[name]
        return full[n % BANKS].at(it, n // BANKS + done(name)[1])

    def freed_by(it, part, l):
        n = at[(part, NW - 1 if l else NA - 1)]
        return full[n % BANKS].at(it, n // BANKS + 1 - (0 if l else full[n % BANKS].per_chunk))

    def heads_of(p):
        first = 4 * (p // 2) + p % 2
        return first, first + 2

    def go(stages):
        for name, *args in TIMELINE:
            if name in stages:
                stages[name](*args)

    block = ctx.enter_context(nc.Block())

    def prime(eng, signals):
        for s in signals:
            eng.sem_inc(s.sem, s.per_chunk)

    @block.sync
    def _(sp):
        prime(sp, [x_loaded, *tab_loaded, *wqkv_loaded, bc_stored, *bc_loaded, *shifted,
                   *carried, out_stored])
        consts = [(inw, io["inw"]), (par, io["par"]), (ident, io["ident"]),
                  (xpw, io["xpw"]), (outw, io["outw"]), (wo, io["wo"]), (w1, io["w1"]), (w2, io["w2"]),
                  (qks, io["qks"])]
        for dst, src in consts:
            full_dst = dst[tuple(slice(None) for _ in dst.shape)]
            sp.dma_start(full_dst, src).then_inc(consts_loaded, D16)
        sp.dma_start(hb[:, 0, :], io["mask"]).then_inc(consts_loaded, D16)
        sp.dma_start(hb[:, 1, 0:2 * WIN], io["mask0"]).then_inc(consts_loaded, D16)
        sp.dma_start(dtw[2 * STATES:XROWS, :], io["dtw"]).then_inc(consts_loaded, D16)
        sp.wait_ge(memory_set, N_SET)

        with sp.Fori(0, CHUNKS) as it:
            sp.wait_ge(*out_ready.at(it, 0))
            sp.sem_inc(passed, 1)
            sp.dma_start(xtok[:, :, :], io["x"][bass.ds(it * T, T), :].rearrange("(w p) d -> p w d", p=P))\
              .then_inc(x_loaded.sem, D16)
            def load_wqkv(l, i):
                sp.wait_ge(*(freed_by(it, "qkv"[i], l)))
                sp.sem_inc(passed, 1)
                sp.dma_start(wqkv[:, :, i * 512:(i + 1) * 512], io["wqkv"][:, l, :, i * 512:(i + 1) * 512])\
                  .then_inc(wqkv_loaded[i].sem, D16)

            def load_tab(a):
                sp.wait_ge(*tabs_ready.at(it, a - 1))
                sp.sem_inc(passed, 1)
                sp.dma_start(tab[:, a % 2, :, :],
                             io["tab"][bass.ds(it * T + (a % NW) * WIN, WIN), :, :]).then_inc(tab_loaded[a % 2].sem, D16)

            def load_bc(g):
                sp.wait_ge(*hC_ready.at(it, (g - 1) * GROUP * NJ))
                sp.sem_inc(passed, 1)
                rows = 2 * GROUP
                src = scratch[g * rows:(g + 1) * rows, :].rearrange("r t -> (r t)")
                sp.dma_start(bc[:, g % 2, :, :, :].rearrange("p n c t -> p (n c t)"), src.partition_broadcast(P)).then_inc(bc_loaded[g % 2].sem, D16)

            def shift(l, w):
                a = l * NW + w
                sp.wait_ge(*x1_ready.at(it, a + 1))
                sp.sem_inc(passed, 1)
                sp.wait_ge(*hn_ready.at(it, hn_reads(l, w)))
                sp.sem_inc(passed, 1)
                sp.dma_start(sh[1:P, l, w, :], X[0:P - 1, w, P:D]).then_inc(shifted[w].sem, D16)
                sp.wait_ge(*hn_ready.at(it, hn_carry(l, w)))
                sp.sem_inc(passed, 1)
                sp.dma_start(sh[0:1, l, (w + 1) % NW, :], X[P - 1:P, w, P:D]).then_inc(carried[w].sem, D16)

            def hn_reads(l, w):
                return 4 * (l * 2 + w // 2) + 4 - hn_ready.per_chunk

            def hn_carry(l, w):
                if w == NW - 1:
                    return 4 * (l * 2) + 4
                return hn_reads(l, w + 1)

            def store_bc():
                sp.wait_ge(*xdbl_ready.at(it, 1))
                sp.sem_inc(passed, 1)
                sp.wait_ge(*bc_loaded[0].at(it, 0))
                sp.sem_inc(passed, 1)
                sp.wait_ge(*bc_loaded[1].at(it, 0))
                sp.sem_inc(passed, 1)
                sp.dma_start(scratch, xdbl[0:2 * STATES, :]).then_inc(bc_stored.sem, D16)
                sp.wait_ge(*bc_stored.at(it, D16))
                sp.sem_inc(passed, 1)
                load_bc(0)
                load_bc(1)

            for i in range(3):
                load_wqkv(0, i)
            load_tab(0)
            load_tab(1)
            scans = [0]

            def scan_step():
                scans[0] += 1
                g, rest = divmod(scans[0] - 3, GROUP * NJ)
                if rest == 0 and 0 < g < NGROUPS - 1:
                    load_bc(g + 1)

            def after_q(a):
                if a == NW - 1:
                    load_wqkv(1, 0)

            def after_k(a):
                if 1 <= a < NA - 1:
                    load_tab(a + 1)
                if a == NW - 1:
                    load_wqkv(1, 1)

            def after_v(a):
                if a == NW - 1:
                    load_wqkv(1, 2)

            go({"xdbl": store_bc, "scan": scan_step, "q": after_q, "k": after_k, "v": after_v,
                "wo": lambda a: shift(a // NW, a % NW)})
            sp.wait_ge(*out_ready.at(it, 1))
            sp.sem_inc(passed, 1)
            sp.dma_start(io["out"][bass.ds(it * T, T), :].rearrange("(w p) d -> p w d", p=P), X[:, :, :])\
              .then_inc(out_stored.sem, D16)
        sp.wait_ge(out_stored.sem, D16 * (CHUNKS + 1))
        sp.wait_ge(bc_stored.sem, D16 * (CHUNKS + 1))

    @block.vector
    def _(dve):
        prime(dve, [stats_ready, mv_ready, xn_ready, conv_step, dt_ready, u_ready, sine_ready, hn_ready, dBx_ready, h_ready,
                    hC_ready, skip_added, gated, branch_added, ssum_ready, rotary_ready,
                    nmax_ready, rinv_ready, o_ready, x1_ready, stats2_ready, mv2_ready, hid_ready,
                    x2_ready])
        dve.wait_ge(consts_loaded, N_CONST * D16)
        dve.wait_ge(memory_set, N_SET)
        dve.tensor_copy(mask[:, :, :], hb[:, 0, :].rearrange("p (s k) -> p s k", s=2)).then_inc(casts_done, 1)
        dve.tensor_copy(mask0[:, :], hb[:, 1, 0:2 * WIN]).then_inc(casts_done, 1)
        dve.tensor_copy(identb[:, :], ident[:, :]).then_inc(casts_done, 1)
        dve.wait_ge(casts_done, 3)

        with dve.Fori(0, CHUNKS) as it:
            def u_of(j):
                return xin[:, j, TAPS - 1:]

            def dBx(k):
                n, j = divmod(k, NJ)
                g = n // GROUP
                if j == 0 and n % GROUP == 0:
                    dve.wait_ge(*bc_loaded[g % 2].at(it, D16 * (g // 2 + 1)))
                if n == 0:
                    dve.wait_ge(*u_ready.at(it, j + 1))
                if n == 0:
                    dve.wait_ge(*dt_ready.at(it, j + 1))
                dve.wait_ge(*summed.at(it, k + 1 - H_RING))
                dve.tensor_tensor(hb[:, k % H_RING, :], u_of(j), bc[:, g % 2, n % GROUP, 0, :], ALU.mult)\
                   .then_inc(dBx_ready.sem, 1)

            def scan(k):
                dve.wait_ge(*dA_ready.at(it, k + 1))
                dve.wait_ge(*dBx_ready.at(it, k + 1))
                dve.wait_ge(*state_saved.at(it, k + 1 - UNITS))
                dve.tensor_tensor_scan(hb[:, k % H_RING, :], dA[:, k % DA_RING, :], hb[:, k % H_RING, :],
                                       state[:, k:k + 1], ALU.mult, ALU.add).then_inc(h_ready.sem, 1)

            def hC(k):
                n, j = divmod(k, NJ)
                g = n // GROUP
                dve.wait_ge(*h_ready.at(it, k + 1))
                dve.wait_ge(*state_saved.at(it, k + 1))
                dve.tensor_tensor(hb[:, k % H_RING, :], hb[:, k % H_RING, :], bc[:, g % 2, n % GROUP, 1, :],
                                  ALU.mult).then_inc(hC_ready.sem, 1)

            at_unit = [0]

            def fill(count=1):
                for _ in range(count):
                    k = at_unit[0]
                    if k < UNITS:
                        dBx(k)
                    if 0 <= k - 1 < UNITS:
                        scan(k - 1)
                    if 0 <= k - 2 < UNITS:
                        hC(k - 2)
                    at_unit[0] += 1

            def norm():
                dve.wait_ge(*x_loaded.at(it, D16))
                for w in range(NW):
                    dve.bn_stats(stats[:, w, 0, :], xtok[:, w, :]).then_inc(stats_ready.sem, 1)
                for w in range(NW):
                    dve.wait_ge(*stats_ready.at(it, w + 1))
                    dve.sem_inc(passed, 1)
                    dve.bn_aggr(mv[:, w, :], stats[:, w, 0, :]).then_inc(mv_ready.sem, 1)
                dve.wait_ge(*rstd_ready.at(it, 1))
                dve.wait_ge(*out_stored.at(it, 0))
                for w in range(NW):
                    dve.tensor_scalar(X[:, w, :], xtok[:, w, :], mv[:, w, 0:1], rstd[:, w:w + 1],
                                      ALU.subtract, ALU.mult).then_inc(xn_ready.sem, 1)

            def conv(j):
                dve.wait_ge(*tap0_ready.at(it, j + 1))
                for k in range(1, TAPS):
                    if k > 1:
                        dve.wait_ge(*conv_step.at(it, j * (TAPS - 1) + k - 1))
                    dve.scalar_tensor_tensor(xconv[:, j, :], xin[:, j, k:k + T],
                                             par[:, C_CW + j * TAPS + k:C_CW + j * TAPS + k + 1],
                                             xconv[:, j, :], ALU.mult, ALU.add).then_inc(conv_step.sem, 1)

            def softplus():
                for j in range(NJ):
                    dve.wait_ge(*dtlog_ready.at(it, j + 1))
                    dve.tensor_tensor(dt_sb[:, j, :], dt_sb[:, j, :], hb[:, j, :], ALU.max)\
                       .then_inc(dt_ready.sem, 1)

            def u():
                dve.wait_ge(*halo_saved.at(it, 1))
                for j in range(NJ):
                    dve.wait_ge(*dt_ready.at(it, j + 1))
                    dve.wait_ge(*xconv_ready.at(it, j + 1))
                    dve.tensor_tensor(u_of(j), dt_sb[:, j, :], xconv[:, j, :], ALU.mult).then_inc(u_ready.sem, 1)

            def rotate(i, name, a):
                n = 2 * a + i
                dve.wait_ge(*sq_ready.at(it, n + 1))
                dve.wait_ge(*rnorm_ready.at(it, n - 1))
                dve.tensor_reduce(ssum[:, i * HEADS:(i + 1) * HEADS], sq[:, i, :].rearrange("p (h d) -> p h d", d=DH),
                                  AX.X, ALU.add).then_inc(ssum_ready.sem, 1)
                src = bank((name, a))[:, :].rearrange("p (h d) -> p h d", d=DH)
                cos = tabs[:, 2 * i:2 * i + 1, :].to_broadcast([P, HEADS, DH])
                lo = tabs[:, 2 * i + 1:2 * i + 2, 0:DH // 2].to_broadcast([P, HEADS, DH // 2])
                hi = tabs[:, 2 * i + 1:2 * i + 2, DH // 2:DH].to_broadcast([P, HEADS, DH // 2])
                out = rot[:, i, :].rearrange("p (h d) -> p h d", d=DH)
                dve.wait_ge(*tabs_ready.at(it, a + 1))
                dve.wait_ge(*filled(it, (name, a)))
                dve.wait_ge(*normed.at(it, n - 1))
                dve.tensor_tensor(out[:, :, 0:DH // 2], src[:, :, DH // 2:DH], lo, ALU.mult)
                dve.tensor_tensor(out[:, :, DH // 2:DH], src[:, :, 0:DH // 2], hi, ALU.mult)\
                   .then_inc(sine_ready.sem, 1)
                dve.wait_ge(*ssum_ready.at(it, n + 1))
                dve.tensor_tensor(sq[:, i, :].rearrange("p (h d) -> p h d", d=DH), src, cos, ALU.mult)\
                   .then_inc(rotary_ready.sem, 1)

            def row_max(a, p):
                dve.wait_ge(*filled(it, ("s", a, p)))
                dve.wait_ge(*probs_ready.at(it, a * HEADS + 2 * p + 2 - HEADS))
                dve.tensor_reduce(nmax[:, 2 * p:2 * p + 2],
                                  bank(("s", a, p))[:, :].rearrange("p (h k) -> p h k", h=2),
                                  AX.X, ALU.max, negate=True).then_inc(nmax_ready.sem, 1)

            def head_out(a, p):
                n = a * PAIRS + p
                dve.wait_ge(*probs_ready.at(it, 2 * n + 2))
                dve.wait_ge(*o_ready.at(it, n + 1 - PAIRS))
                dve.reciprocal(rinv[:, 2 * p:2 * p + 2], rowsum[:, 2 * p:2 * p + 2]).then_inc(rinv_ready.sem, 1)
                dve.wait_ge(*filled(it, ("o", a, p)))
                dve.wait_ge(*rinv_ready.at(it, n + 1))
                if p == 0:
                    dve.wait_ge(*oT_ready.at(it, a))
                o_view = o_sb[:, :].rearrange("p (c e a d) -> p c e a d", c=2, e=2, a=2)
                dve.tensor_tensor(o_view[:, p // 2, :, p % 2, :],
                                  bank(("o", a, p))[:, 0:2 * DH].rearrange("p (h d) -> p h d", h=2),
                                  rinv[:, 2 * p:2 * p + 2].unsqueeze(2).to_broadcast([P, 2, DH]), ALU.mult)\
                   .then_inc(o_ready.sem, 1)

            def add_attention(a):
                l, w = divmod(a, NW)
                dve.wait_ge(*filled(it, ("wo", a)))
                if l:
                    dve.wait_ge(*x2_ready.at(it, w // 2 + 1))
                dve.tensor_tensor(X[:, w, :], bank(("wo", a))[:, 0:D], X[:, w, :], ALU.add)\
                   .then_inc(x1_ready.sem, 1)

            def shifted_stats(f):
                l, half = divmod(f, 2)
                for v in range(2):
                    w = 2 * half + v
                    dve.wait_ge(*x1_ready.at(it, l * NW + w + 1))
                    dve.wait_ge(*mv2_ready.at(it, 2 * f + v - 1))
                    dve.bn_stats(stats2[:, v, 0, :], X[:, w, 0:P]).then_inc(stats2_ready.sem, 1)
                    dve.wait_ge(*shifted[w].at(it, D16 * (l + 1)))
                    dve.wait_ge(*carried[(w - 1) % NW].at(it, D16 * (l + 1) if w else D16 * (l + 1) - carried[0].per_chunk))
                    dve.bn_stats(stats2[:, v, 1, :], sh[:, l, w, :]).then_inc(stats2_ready.sem, 1)
                for v in range(2):
                    dve.wait_ge(*stats2_ready.at(it, 4 * f + 2 * v + 2))
                    dve.wait_ge(*hn_ready.at(it, 4 * f))
                    dve.sem_inc(passed, 1)
                    dve.bn_aggr(mv2[:, v, :], stats2[:, v, :, :].rearrange("p a b -> p (a b)"))\
                       .then_inc(mv2_ready.sem, 1)

            def normalize(f):
                l, half = divmod(f, 2)
                dve.wait_ge(*rstd2_ready.at(it, f + 1))
                for v in range(2):
                    w = 2 * half + v
                    for ft, src in ((0, X[:, w, 0:P]), (1, sh[:, l, w, :])):
                        dve.tensor_scalar(hn[:, v, ft * P:(ft + 1) * P], src, mv2[:, v, 0:1], rstd2[:, v:v + 1],
                                          ALU.subtract, ALU.mult).then_inc(hn_ready.sem, 1)

            def hidden(f, i):
                l = f // 2
                rows = P if i < NH - 1 else LAST
                dve.wait_ge(*filled(it, ("h", f, i)))
                dve.wait_ge(*gelu_ready.at(it, f * NH + i + 1))
                b1a = C_B1A + l * NH + i
                dve.scalar_tensor_tensor(hid[0:rows, i, :], bank(("h", f, i))[0:rows, 0:2 * WIN],
                                         par[0:rows, b1a:b1a + 1], gel[0:rows, i % 2, :], ALU.add, ALU.mult)\
                   .then_inc(hid_ready.sem, 1)

            def add_feed(f):
                l, half = divmod(f, 2)
                dve.wait_ge(*filled(it, ("w2", f)))
                for w in (2 * half, 2 * half + 1):
                    dve.wait_ge(*shifted[w].at(it, D16 * (l + 1)))
                    dve.wait_ge(*carried[w].at(it, D16 * (l + 1)))
                dve.wait_ge(*hn_ready.at(it, 4 * f + 4))
                dve.tensor_tensor(X[:, 2 * half:2 * half + 2, :],
                                  bank(("w2", f))[:, :].rearrange("p (w d) -> p w d", w=2),
                                  X[:, 2 * half:2 * half + 2, :], ALU.add).then_inc(x2_ready.sem, 1)

            def skip():
                for j in range(NJ):
                    dve.wait_ge(*summed.at(it, UNITS - NJ + j + 1))
                    dve.scalar_tensor_tensor(xconv[:, j, :], xconv[:, j, :], par[:, C_DP + j:C_DP + j + 1],
                                             ybank[j][:, :], ALU.mult, ALU.add).then_inc(skip_added.sem, 1)

            def gate():
                for j in range(NJ):
                    dve.wait_ge(*skip_added.at(it, j + 1))
                    dve.wait_ge(*silu_ready.at(it, j + 1))
                    dve.tensor_tensor(xconv[:, j, :], xconv[:, j, :], dt_sb[:, j, :], ALU.mult).then_inc(gated.sem, 1)

            def add_mamba(h):
                dve.wait_ge(*x2_ready.at(it, NF))
                dve.wait_ge(*filled(it, ("out", h)))
                dve.tensor_tensor(X[:, 2 * h:2 * h + 2, :], bank(("out", h))[:, :].rearrange("p (w d) -> p w d", w=2),
                                  X[:, 2 * h:2 * h + 2, :], ALU.add).then_inc(branch_added.sem, 1)

            go({"norm": norm, "conv": conv, "softplus": softplus, "u": u, "scan": fill,
                "q": lambda a: rotate(0, "q", a), "k": lambda a: rotate(1, "k", a), "s": row_max, "o": head_out,
                "wo": add_attention, "stats": shifted_stats, "hn": normalize, "h": hidden, "w2": add_feed,
                "skip": skip, "gate": gate, "out": add_mamba})

    @block.scalar
    def _(act):
        prime(act, [xnT_ready, xin_ready, tap0_ready, xconv_ready, xdbl_ready, dtv_ready, dtexp_ready,
                    dtlog_ready, dA_ready, silu_ready, sq_ready, v_ready, qT_ready, kT_ready, probs_ready,
                    pT_ready, oT_ready, hT_ready, gelu_ready, x2T_ready])
        act.wait_ge(consts_loaded, N_CONST * D16)
        act.wait_ge(memory_set, N_SET)
        act.activation(amat[:, :], par[:, C_ALOG:C_ALOG + NJ * STATES], ACT.Exp).then_inc(a_exp, 1)
        act.wait_ge(a_exp, 1)
        act.mul(amat[:, :], amat[:, :], -1.0).then_inc(a_ready, 1)
        act.wait_ge(a_ready, 1)

        with act.Fori(0, CHUNKS) as it:
            at_unit = [0]

            def fill(count=1):
                for _ in range(count):
                    k = at_unit[0]
                    n, j = divmod(k, NJ)
                    if k >= UNITS:
                        return
                    if n == 0:
                        act.wait_ge(*dt_ready.at(it, j + 1))
                    act.wait_ge(*h_ready.at(it, k + 1 - DA_RING))
                    act.activation(dA[:, k % DA_RING, :], dt_sb[:, j, :], ACT.Exp,
                                   scale=amat[:, j * STATES + n:j * STATES + n + 1]).then_inc(dA_ready.sem, 1)
                    at_unit[0] += 1

            def xnT_out(h):
                act.wait_ge(*xnT_carried.at(it, 0))
                act.wait_ge(*filled(it, ("xnT", h)))
                act.activation(xnT[:, :, 1 + h * 256:1 + (h + 1) * 256],
                               bank(("xnT", h))[:, :].rearrange("p (f t) -> p f t", f=FT), ACT.Copy)\
                   .then_inc(xnT_ready.sem, 1)

            def conv_input(j):
                if j == 0:
                    act.wait_ge(*halo_ready.at(it, 1))
                    act.wait_ge(*hC_ready.at(it, 0))
                    act.wait_ge(*gated.at(it, 0))
                act.wait_ge(*filled(it, ("xin", j)))
                act.activation(xin[:, j, TAPS - 1:], bank(("xin", j))[:, :], ACT.Copy).then_inc(xin_ready.sem, 1)
                act.wait_ge(*xin_ready.at(it, j + 1))
                act.activation(xconv[:, j, :], xin[:, j, 0:T], ACT.Identity,
                               bias=par[:, C_CB + j:C_CB + j + 1],
                               scale=par[:, C_CW + j * TAPS:C_CW + j * TAPS + 1]).then_inc(tap0_ready.sem, 1)

            def silu():
                for j in range(NJ):
                    act.wait_ge(*conv_step.at(it, (j + 1) * (TAPS - 1)))
                    act.activation(xconv[:, j, :], xconv[:, j, :], ACT.Silu).then_inc(xconv_ready.sem, 1)
                act.preload_act_table_set("natural_log_exp_and_others")

            def xdbl_out():
                act.wait_ge(*filled(it, ("xdbl",)))
                act.wait_ge(*bc_stored.at(it, 0))
                act.activation(xdbl[:, :], bank(("xdbl",))[0:XROWS, :], ACT.Copy).then_inc(xdbl_ready.sem, 1)

            def dt_out(j):
                act.wait_ge(*filled(it, ("dt", j)))
                act.activation(dt_sb[:, j, :], bank(("dt", j))[:, :], ACT.Identity,
                               bias=par[:, C_DTB + j:C_DTB + j + 1]).then_inc(dtv_ready.sem, 1)

            def softplus():
                for j in range(NJ):
                    act.wait_ge(*dtmin_ready.at(it, j + 1))
                    act.activation(hb[:, j, :], hb[:, j, :], ACT.Exp).then_inc(dtexp_ready.sem, 1)
                for j in range(NJ):
                    act.wait_ge(*dtexp_ready.at(it, j + 1))
                    act.activation(hb[:, j, :], hb[:, j, :], ACT.Ln, bias=1.0).then_inc(dtlog_ready.sem, 1)

            def square(i, name, a):
                n = 2 * a + i
                act.wait_ge(*normed.at(it, n - 1))
                act.wait_ge(*filled(it, (name, a)))
                act.activation(sq[:, i, :], bank((name, a))[:, :], ACT.Square).then_inc(sq_ready.sem, 1)

            def heads_out(a):
                l, w = divmod(a, NW)
                act.wait_ge(*filled(it, ("kT", a)))
                act.activation(kT[:, l, :, w % 2, :], bank(("kT", a))[:, :].rearrange("p (a t) -> p a t", a=PAIRS),
                               ACT.Copy).then_inc(kT_ready.sem, 1)
                act.wait_ge(*filled(it, ("qT", a)))
                act.activation(qT[:, :, :], bank(("qT", a))[:, :].rearrange("p (a t) -> p a t", a=PAIRS), ACT.Copy)\
                   .then_inc(qT_ready.sem, 1)

            def v_out(a):
                l, w = divmod(a, NW)
                act.wait_ge(*filled(it, ("v", a)))
                act.wait_ge(*o_ready.at(it, a * PAIRS))
                act.activation(V[:, l, w % 2, :], bank(("v", a))[:, :], ACT.Copy).then_inc(v_ready.sem, 1)

            def exps(a, p):
                n = a * PAIRS + p
                act.wait_ge(*nmax_ready.at(it, n + 1))
                act.wait_ge(*rinv_ready.at(it, n + 1 - PAIRS))
                for hh in range(2):
                    c = 2 * p + hh
                    act.activation(probs[:, p % 2, hh, :], bank(("s", a, p))[:, hh * 256:(hh + 1) * 256], ACT.Exp,
                                   bias=nmax[:, c:c + 1], accum_out=rowsum[:, c:c + 1])\
                       .then_inc(probs_ready.sem, 1)

            def pT_out(a, p):
                n = a * PAIRS + p
                act.wait_ge(*filled(it, ("pT", a, p)))
                act.wait_ge(*o_ready.at(it, n - 1))
                act.activation(pT[:, p % 2, :, :], bank(("pT", a, p))[:, :].rearrange("p (a t) -> p a t", a=4),
                               ACT.Copy).then_inc(pT_ready.sem, 1)

            def oT_out(a):
                act.wait_ge(*filled(it, ("oT", a)))
                act.activation(oT[:, :, :], bank(("oT", a))[:, :].rearrange("p (a t) -> p a t", a=NJ), ACT.Copy)\
                   .then_inc(oT_ready.sem, 1)

            def hT_out(f):
                l = f // 2
                act.wait_ge(*filled(it, ("hT", f)))
                for ft in range(FT):
                    act.activation(hT[:, ft, :], bank(("hT", f))[:, ft * 256:(ft + 1) * 256], ACT.Identity,
                                   bias=par[:, C_LB + l * FT + ft:C_LB + l * FT + ft + 1],
                                   scale=par[:, C_LG + l * FT + ft:C_LG + l * FT + ft + 1])\
                       .then_inc(hT_ready.sem, 1)

            def gelu(f, i):
                l = f // 2
                rows = P if i < NH - 1 else LAST
                act.wait_ge(*filled(it, ("h", f, i)))
                act.wait_ge(*hid_ready.at(it, f * NH + i - 1))
                b1g = C_B1G + l * NH + i
                act.activation(gel[0:rows, i % 2, :], bank(("h", f, i))[0:rows, 256:512], ACT.Gelu,
                               bias=par[0:rows, b1g:b1g + 1]).then_inc(gelu_ready.sem, 1)

            def x2T_out(half):
                act.wait_ge(*filled(it, ("x2T", half)))
                act.wait_ge(*x2T_carried.at(it, 0))
                act.activation(x2T[:, :, 1 + half * 256:1 + (half + 1) * 256],
                               bank(("x2T", half))[:, :].rearrange("p (f t) -> p f t", f=FT), ACT.Copy)\
                   .then_inc(x2T_ready.sem, 1)

            def z_gate(j):
                act.wait_ge(*dA_ready.at(it, UNITS))
                act.wait_ge(*filled(it, ("z", j)))
                act.activation(dt_sb[:, j, :], bank(("z", j))[:, :], ACT.Silu).then_inc(silu_ready.sem, 1)

            go({"xnT": xnT_out, "in": conv_input, "silu": silu, "xdbl": xdbl_out, "dt": dt_out,
                "softplus": softplus, "q": lambda a: square(0, "q", a), "k": lambda a: square(1, "k", a),
                "heads": heads_out, "v": v_out, "s": exps, "pT": pT_out, "oT": oT_out, "hT": hT_out,
                "h": gelu, "x2T": x2T_out, "z": z_gate, "scan": fill})

    @block.gpsimd
    def _(pool):
        for t in (xnT, x2T, state, halo, V, kT, sh):
            pool.memset(t[tuple(slice(None) for _ in t.shape)], 0.0).then_inc(memory_set, 1)
        pool.memset(powers[:, :], -0.5).then_inc(memory_set, 1)
        pool.memset(hid[:, :, :], 1.0).then_inc(memory_set, 1)
        prime(pool, [eps_added, rstd_ready, halo_ready, halo_saved, dtmin_ready, state_saved, out_ready,
                     xnT_carried, x2T_carried, mask0_ready, ssum_clipped, rnorm_ready, tabs_ready, rot_ready, normed,
                     eps2_added, rstd2_ready])
        pool.wait_ge(consts_loaded, N_CONST * D16)
        pool.wait_ge(memory_set, N_SET)

        with pool.Fori(0, CHUNKS) as it:
            at_unit = [0]

            def fill(count=1):
                for _ in range(count):
                    k = at_unit[0] - 1
                    if k >= 0:
                        pool.wait_ge(*h_ready.at(it, k + 1))
                        pool.sem_inc(passed, 1)
                        pool.tensor_copy(state[:, k:k + 1], hb[:, k % H_RING, T - 1:T]).then_inc(state_saved.sem, 1)
                    at_unit[0] += 1

            def norm():
                pool.wait_ge(*halo_saved.at(it, 0))
                pool.wait_ge(*hC_ready.at(it, 0))
                pool.sem_inc(passed, 1)
                pool.tensor_copy(xin[:, :, 0:TAPS - 1], halo[:, :, :]).then_inc(halo_ready.sem, 1)
                pool.wait_ge(*mv_ready.at(it, NW))
                pool.wait_ge(*xn_ready.at(it, 0))
                pool.sem_inc(passed, 1)
                pool.tensor_scalar(rstd[:, :], mv[:, :, 1], EPS, None, ALU.add).then_inc(eps_added.sem, 1)
                pool.wait_ge(*eps_added.at(it, 1))
                pool.sem_inc(passed, 1)
                pool.tensor_tensor(rstd[:, :], rstd[:, :], powers[:, 0:NW], ALU.pow).then_inc(rstd_ready.sem, 1)

            def save_halo():
                pool.wait_ge(*xin_ready.at(it, NJ))
                pool.wait_ge(*halo_ready.at(it, 1))
                pool.sem_inc(passed, 1)
                pool.tensor_copy(halo[:, :, :], xin[:, :, T:T + TAPS - 1]).then_inc(halo_saved.sem, 1)

            def clip_dt(j):
                pool.wait_ge(*dtv_ready.at(it, j + 1))
                pool.wait_ge(*summed.at(it, 0))
                pool.sem_inc(passed, 1)
                pool.tensor_scalar(hb[:, j, :], dt_sb[:, j, :], 40.0, None, ALU.min).then_inc(dtmin_ready.sem, 1)

            def scale_tables(a):
                pool.wait_ge(*tab_loaded[a % 2].at(it, D16 * (a // 2 + 1)))
                pool.wait_ge(*rotary_ready.at(it, 2 * a))
                pool.sem_inc(passed, 1)
                pool.tensor_tensor(tabs[:, :, :], tab[:, a % 2, :, :], qks[:, a // NW, :, :], ALU.mult)\
                    .then_inc(tabs_ready.sem, 1)

            def scale_heads(i, a):
                n = 2 * a + i
                part = slice(i * HEADS, (i + 1) * HEADS)
                pool.wait_ge(*ssum_ready.at(it, n + 1))
                pool.sem_inc(passed, 1)
                pool.tensor_scalar(rnorm[:, part], ssum[:, part], 1e-24, None, ALU.max).then_inc(ssum_clipped.sem, 1)
                pool.wait_ge(*ssum_clipped.at(it, n + 1))
                pool.sem_inc(passed, 1)
                pool.tensor_tensor(rnorm[:, part], rnorm[:, part], powers[:, part], ALU.pow).then_inc(rnorm_ready.sem, 1)
                pool.wait_ge(*sine_ready.at(it, n + 1))
                pool.wait_ge(*rotary_ready.at(it, n + 1))
                pool.sem_inc(passed, 1)
                pool.tensor_tensor(rot[:, i, :], rot[:, i, :], sq[:, i, :], ALU.add).then_inc(rot_ready.sem, 1)
                pool.wait_ge(*rot_ready.at(it, n + 1))
                pool.wait_ge(*rnorm_ready.at(it, n + 1))
                pool.sem_inc(passed, 1)
                r = rot[:, i, :].rearrange("p (h d) -> p h d", d=DH)
                pool.tensor_tensor(r, r, rnorm[:, part].unsqueeze(2).to_broadcast([P, HEADS, DH]), ALU.mult)\
                    .then_inc(normed.sem, 1)

            def rstd_of(f):
                pool.wait_ge(*mv2_ready.at(it, 2 * f + 2))
                pool.wait_ge(*hn_ready.at(it, 4 * f))
                pool.sem_inc(passed, 1)
                pool.tensor_scalar(rstd2[:, :], mv2[:, :, 1], EPS, None, ALU.add).then_inc(eps2_added.sem, 1)
                pool.wait_ge(*eps2_added.at(it, f + 1))
                pool.sem_inc(passed, 1)
                pool.tensor_tensor(rstd2[:, :], rstd2[:, :], powers[:, 0:2], ALU.pow).then_inc(rstd2_ready.sem, 1)

            def q_side(a):
                scale_tables(a)
                scale_heads(0, a)

            def carry():
                pool.wait_ge(*filled(it, ("z", NJ - 1)))
                pool.sem_inc(passed, 1)
                pool.tensor_copy(xnT[:, 1, 0:1], xnT[:, 1, T:T + 1]).then_inc(xnT_carried.sem, 1)
                pool.wait_ge(*filled(it, ("v", NA - 1)))
                pool.sem_inc(passed, 1)
                pool.tensor_copy(x2T[:, 1, 0:1], x2T[:, 1, T:T + 1]).then_inc(x2T_carried.sem, 1)
                pool.wait_ge(*probs_ready.at(it, HEADS * (NW + 1)))
                pool.sem_inc(passed, 1)
                pool.tensor_copy(mask0[:, :], mask[:, 0, :]).then_inc(mask0_ready.sem, 1)
                pool.wait_ge(*branch_added.at(it, 2))
                pool.sem_inc(passed, 1)
                pool.tensor_tensor(X[:, :, :], X[:, :, :], xtok[:, :, :], ALU.add).then_inc(out_ready.sem, 1)

            def keep_state():
                if at_unit[0] <= UNITS:
                    fill()

            go({"norm": norm, "silu": save_halo, "dt": clip_dt, "q": q_side, "k": lambda a: scale_heads(1, a),
                "stats": rstd_of, "scan": keep_state, "last": carry})

    @block.tensor
    def _(pe):
        prime(pe, [*full, summed])
        pe.wait_ge(consts_loaded, N_CONST * D16)
        pe.wait_ge(memory_set, N_SET)
        pe.wait_ge(casts_done, 3)

        with pe.Fori(0, CHUNKS) as it:
            at_unit = [0]

            def fill(count=1):
                for _ in range(count):
                    k = at_unit[0] - 3
                    if 0 <= k < UNITS:
                        n, j = divmod(k, NJ)
                        pe.wait_ge(*hC_ready.at(it, k + 1))
                        if n == 0:
                            pe.wait_ge(*skip_added.at(it, j + 1 - NJ))
                        pe.matmul(ybank[j][:, :], ident[:, :], hb[:, k % H_RING, :], start=(n == 0),
                                  stop=(n == STATES - 1)).then_inc(summed.sem, 1)
                    at_unit[0] += 1

            def flip(name, src):
                for b, block_ in enumerate(src):
                    m = pe.transpose(bank(name)[:, b * P:(b + 1) * P], block_, ident[:, :])
                m.then_inc(*done(name))

            def blocks_of(t, first):
                return [t[:, first + v, ft * P:(ft + 1) * P] for ft in range(FT) for v in range(2)]

            def flip_xn(h):
                pe.wait_ge(*xn_ready.at(it, 2 * h + 2))
                pe.wait_ge(*freed(it, ("xnT", h)))
                flip(("xnT", h), blocks_of(X, 2 * h))

            def in_proj(name, j, col):
                pe.wait_ge(*freed(it, (name, j)))
                pe.wait_ge(*xnT_ready.at(it, 2))
                for ft in range(FT):
                    m = pe.matmul(bank((name, j))[:, :], inw[:, ft, col:col + P], xnT[:, ft, 1:1 + T],
                                  start=(ft == 0), stop=(ft == FT - 1))
                m.then_inc(*done((name, j)))

            def x_dbl():
                pe.wait_ge(*freed(it, ("xdbl",)))
                for j in range(NJ):
                    pe.wait_ge(*xconv_ready.at(it, j + 1))
                    m = pe.matmul(bank(("xdbl",))[0:XROWS, :], xpw[:, j, :], xconv[:, j, :],
                                  start=(j == 0), stop=(j == NJ - 1))
                m.then_inc(*done(("xdbl",)))

            def dt_proj(j):
                pe.wait_ge(*xdbl_ready.at(it, 1))
                pe.wait_ge(*freed(it, ("dt", j)))
                pe.matmul(bank(("dt", j))[:, :], dtw[2 * STATES:XROWS, j * P:(j + 1) * P],
                          xdbl[2 * STATES:XROWS, :], start=True, stop=True).then_inc(*done(("dt", j)))

            def project(i, a):
                l, w = divmod(a, NW)
                name = ("qkv"[i], a)
                pe.wait_ge(*wqkv_loaded[i].at(it, D16 * (l + 1)))
                if l:
                    pe.wait_ge(*x2T_ready.at(it, w // 2 + 1))
                else:
                    pe.wait_ge(*xnT_ready.at(it, w // 2 + 1))
                pe.wait_ge(*freed(it, name))
                for ft in range(FT):
                    off = w * WIN + (1 - ft)
                    m = pe.matmul(bank(name)[:, :], (x2T if l else xnT)[:, ft, off:off + WIN],
                                  wqkv[:, ft, i * 512:(i + 1) * 512], start=(ft == 0), stop=(ft == FT - 1))
                m.then_inc(*done(name))

            def heads(a):
                for i, name in ((1, "kT"), (0, "qT")):
                    pe.wait_ge(*normed.at(it, 2 * a + i + 1))
                    pe.wait_ge(*freed(it, (name, a)))
                    flip((name, a), [rot[:, i, p * P:(p + 1) * P] for p in range(PAIRS)])

            def scores(a, p):
                l, w = divmod(a, NW)
                pe.wait_ge(*qT_ready.at(it, a + 1))
                pe.wait_ge(*kT_ready.at(it, a + 1))
                if a == 0:
                    pe.wait_ge(*mask0_ready.at(it, 0))
                pe.wait_ge(*freed(it, ("s", a, p)))
                s = bank(("s", a, p))
                msk = mask0[:, :] if w == 0 else mask[:, w % 2, :]
                for hh in range(2):
                    pe.matmul(s[:, hh * 256:(hh + 1) * 256], identb[:, :], msk, start=(hh == 0), stop=False,
                              skip_group_check=True)
                for hh, h in enumerate(heads_of(p)):
                    rows = slice((h % 2) * DH, (h % 2 + 1) * DH)
                    m = pe.matmul(s[:, hh * 256:(hh + 1) * 256], qT[rows, h // 2, :],
                                  kT[rows, l, h // 2, :, :].rearrange("p a b -> p (a b)"),
                                  start=False, stop=True, skip_group_check=True)
                m.then_inc(*done(("s", a, p)))

            def flip_probs(a, p):
                pe.wait_ge(*probs_ready.at(it, a * HEADS + 2 * p + 2))
                pe.wait_ge(*freed(it, ("pT", a, p)))
                flip(("pT", a, p), [probs[:, p % 2, hh, s * WIN:(s + 1) * WIN] for hh in range(2) for s in range(2)])

            def head_out(a, p):
                pe.wait_ge(*v_ready.at(it, a + 1))
                pe.wait_ge(*pT_ready.at(it, a * PAIRS + p + 1))
                pe.wait_ge(*freed(it, ("o", a, p)))
                for hh, h in enumerate(heads_of(p)):
                    for s in range(2):
                        m = pe.matmul(bank(("o", a, p))[:, hh * DH:(hh + 1) * DH], pT[:, p % 2, 2 * hh + s, :],
                                      V[:, a // NW, s, h * DH:(h + 1) * DH], start=(s == 0), stop=(s == 1))
                m.then_inc(*done(("o", a, p)))

            def flip_out(a):
                pe.wait_ge(*o_ready.at(it, (a + 1) * PAIRS))
                pe.wait_ge(*freed(it, ("oT", a)))
                flip(("oT", a), [o_sb[:, k * P:(k + 1) * P] for k in range(NJ)])

            def attention_out(a):
                pe.wait_ge(*oT_ready.at(it, a + 1))
                pe.wait_ge(*freed(it, ("wo", a)))
                for k in range(NJ):
                    m = pe.matmul(bank(("wo", a))[:, 0:D], oT[:, k, :], wo[:, a // NW, k, :],
                                  start=(k == 0), stop=(k == NJ - 1))
                m.then_inc(*done(("wo", a)))

            def flip_hn(f):
                pe.wait_ge(*hn_ready.at(it, 4 * f + 4))
                pe.wait_ge(*freed(it, ("hT", f)))
                flip(("hT", f), blocks_of(hn, 0))

            def hidden(f, i):
                rows = P if i < NH - 1 else LAST
                pe.wait_ge(*hT_ready.at(it, FT * (f + 1)))
                pe.wait_ge(*freed(it, ("h", f, i)))
                for part in range(2):
                    for ft in range(FT):
                        col = part * HID + i * P
                        m = pe.matmul(bank(("h", f, i))[0:rows, part * 256:(part + 1) * 256],
                                      w1[:, f // 2, ft, col:col + rows], hT[:, ft, :], start=(ft == 0), stop=(ft == FT - 1))
                m.then_inc(*done(("h", f, i)))

            def feed_out(f):
                pe.wait_ge(*freed(it, ("w2", f)))
                for v in range(2):
                    for i in range(NH):
                        rows = P if i < NH - 1 else LAST + 1
                        if v == 0:
                            pe.wait_ge(*hid_ready.at(it, f * NH + i + 1))
                        m = pe.matmul(bank(("w2", f))[:, v * D:(v + 1) * D], hid[0:rows, i, v * WIN:(v + 1) * WIN],
                                      w2[0:rows, f // 2, i, :], start=(i == 0), stop=(i == NH - 1))
                m.then_inc(*done(("w2", f)))

            def flip_x2(half):
                pe.wait_ge(*x2_ready.at(it, half + 1))
                pe.wait_ge(*freed(it, ("x2T", half)))
                flip(("x2T", half), blocks_of(X, 2 * half))

            def out_proj(h):
                pe.wait_ge(*freed(it, ("out", h)))
                for v in range(2):
                    for j in range(NJ):
                        pe.wait_ge(*gated.at(it, j + 1))
                        m = pe.matmul(bank(("out", h))[:, v * D:(v + 1) * D],
                                      xconv[:, j, (2 * h + v) * WIN:(2 * h + v + 1) * WIN], outw[:, j, :],
                                      start=(j == 0), stop=(j == NJ - 1))
                m.then_inc(*done(("out", h)))

            go({"xnT": flip_xn, "in": lambda j: in_proj("xin", j, j * P), "xdbl": x_dbl, "dt": dt_proj,
                "q": lambda a: project(0, a), "k": lambda a: project(1, a), "v": lambda a: project(2, a),
                "heads": heads, "s": scores, "pT": flip_probs, "o": head_out, "oT": flip_out,
                "wo": attention_out, "hT": flip_hn, "h": hidden, "w2": feed_out, "x2T": flip_x2,
                "z": lambda j: in_proj("z", j, INNER + j * P), "out": out_proj, "scan": fill})

    ctx.close()


N_CONST, N_SET = 12, 9


def constants():
    f = np.float32
    half = np.arange(0, DH, 2, dtype=f)
    freq = (f(1.0) / f(10000.0) ** (half / f(DH))).astype(f)
    t = np.arange(TOKENS, dtype=f)
    ang = t[:, None] * freq[None, :]
    ang = np.concatenate([ang, ang], axis=-1)
    base = (half + f(0.4 * DH)) / f(1.4 * DH)
    power = (t - TOKENS // 2) / f(WIN // 2)
    scale = base[None, :] ** power[:, None]
    scale = np.concatenate([scale, scale], axis=-1)
    cos, sin = np.cos(ang), np.sin(ang)
    sign = np.concatenate([-np.ones(DH // 2, f), np.ones(DH // 2, f)])
    tab = np.stack([8.0 * cos * scale, 8.0 * sin * scale * sign, cos / scale, sin / scale * sign], axis=1)
    q = np.arange(WIN)[:, None]
    k = np.arange(WIN)[None, :]
    own = np.where(k <= q, 0.0, NEG)
    prev = np.where(k >= q, 0.0, NEG)
    never = np.full((WIN, WIN), NEG)
    mask = np.stack([np.concatenate([own, prev], 1), np.concatenate([prev, own], 1)], axis=1).reshape(P, 4 * WIN).astype(f)
    mask0 = np.concatenate([own, never], 1).astype(f)
    eye = np.eye(P, dtype=f)
    return {"tab": np.ascontiguousarray(tab.astype(f)), "mask": mask, "mask0": mask0, "ident": eye}


def kernel(L0_attn_x, L0_attn_in_proj_w, L0_attn_conv_w, L0_attn_conv_b, L0_attn_x_proj_w, L0_attn_dt_proj_w,
           L0_attn_dt_proj_b, L0_attn_A_log, L0_attn_D_param, L0_attn_out_proj_w, L0_ffn_wqkv, L0_ffn_q_scale,
           L0_ffn_k_scale, L0_ffn_wo, L0_ffn_ln_g, L0_ffn_ln_b, L0_ffn_w1, L0_ffn_b1, L0_ffn_w2, L0_ffn_b2):
    import concourse.bacc as bacc
    from concourse.bass_utils import run_bass_kernel_spmd
    f = np.float32

    def tiles(a, n):
        a = np.asarray(a)
        return np.ascontiguousarray(np.moveaxis(a.reshape(n, P, *a.shape[1:]), 0, 1))

    xp = np.asarray(L0_attn_x_proj_w)
    ssm = xp[RANK:].reshape(2, STATES, INNER).transpose(1, 0, 2).reshape(2 * STATES, INNER)
    xp = np.concatenate([ssm, xp[:RANK]], axis=0)
    b1 = np.asarray(L0_ffn_b1).reshape(LAYERS, 2, HID)
    b1p = np.zeros((2, LAYERS, NH * P), f)
    b1p[:, :, :HID] = np.moveaxis(b1, 1, 0)
    w2p = np.zeros((LAYERS, NH * P, D), f)
    w2p[:, :HID] = np.asarray(L0_ffn_w2)
    w2p[:, HID] = np.asarray(L0_ffn_b2)

    def cols(a, n):
        return np.asarray(a).reshape(n, P).T

    par = np.concatenate([
        tiles(L0_attn_A_log, NJ).reshape(P, -1),
        tiles(np.asarray(L0_attn_conv_w).reshape(INNER, TAPS), NJ).reshape(P, -1),
        cols(L0_attn_conv_b, NJ), cols(L0_attn_dt_proj_b, NJ), cols(L0_attn_D_param, NJ),
        cols(L0_ffn_ln_g, LAYERS * FT), cols(L0_ffn_ln_b, LAYERS * FT),
        cols(b1p[0], LAYERS * NH), cols(b1p[1], LAYERS * NH)], axis=1)
    qs, ks = np.asarray(L0_ffn_q_scale), np.asarray(L0_ffn_k_scale)
    qks = np.stack([qs, np.roll(qs, DH // 2, axis=1), ks, np.roll(ks, DH // 2, axis=1)], axis=1)
    arrays = {
        "x": np.asarray(L0_attn_x).reshape(TOKENS, D),
        "inw": tiles(np.asarray(L0_attn_in_proj_w).T, FT),
        "xpw": tiles(xp.T, NJ),
        "dtw": np.asarray(L0_attn_dt_proj_w).T,
        "outw": tiles(np.asarray(L0_attn_out_proj_w).T, NJ),
        "wqkv": np.moveaxis(np.asarray(L0_ffn_wqkv).reshape(LAYERS, FT, P, QKV), 2, 0),
        "wo": np.moveaxis(np.asarray(L0_ffn_wo).reshape(LAYERS, NJ, P, D), 2, 0),
        "w1": np.moveaxis(np.asarray(L0_ffn_w1).reshape(LAYERS, FT, P, 2 * HID), 2, 0),
        "w2": np.moveaxis(w2p.reshape(LAYERS, NH, P, D), 2, 0),
        "qks": np.broadcast_to(qks[None], (P, LAYERS, 4, DH)),
        "par": par,
        **constants(),
    }
    arrays = {k: np.ascontiguousarray(v) for k, v in arrays.items()}
    nc = bacc.Bacc("TRN2", target_bir_lowering=False, num_devices=1)
    io = {k: nc.dram_tensor(f"in_{k}", v.shape, mybir.dt.from_np(v.dtype), kind="ExternalInput").ap()
          for k, v in arrays.items()}
    io["out"] = nc.dram_tensor("out_y", (TOKENS, D), mybir.dt.float32, kind="ExternalOutput").ap()
    build(nc, io)
    r = run_bass_kernel_spmd(nc, [{f"in_{k}": v for k, v in arrays.items()}], core_ids=[0])
    return r.results[0]["out_y"].reshape(1, TOKENS, D)
```

```python
import numpy as np
import concourse.bass as bass
from concourse import mybir
from contextlib import ExitStack

P = 128
TOKENS, D = 4096, 256
T = 512
CHUNKS = TOKENS // T
WIN = 128
NW = T // WIN
FT = D // P
INNER = 512
NJ = INNER // P
STATES = 16
TAPS = 4
RANK = 16
XROWS = 2 * STATES + RANK
HEADS, DH = 8, 64
PAIRS = HEADS // 2
QKV = 3 * HEADS * DH
HID = 682
NH = -(-HID // P)
LAST = HID - (NH - 1) * P
LAYERS = 2
EPS = 1e-5
UNITS = STATES * NJ
GROUP = 2
NGROUPS = STATES // GROUP
DA_RING, H_RING = 6, 4
SUMS = UNITS // GROUP
BANKS = 4
NEG = -1e30
C_ALOG = 0
C_CW = C_ALOG + NJ * STATES
C_CB = C_CW + NJ * TAPS
C_DTB = C_CB + NJ
C_DP = C_DTB + NJ
C_LG = C_DP + NJ
C_LB = C_LG + LAYERS * FT
C_B1A = C_LB + LAYERS * FT
C_B1G = C_B1A + LAYERS * NH
NPAR = C_B1G + LAYERS * NH


PE_ORDER = """
s(0,1) xnT(1) pT(0,0) q(1) s(0,2) in(0) in(1) pT(0,1) k(1) in(2) s(0,3) in(3) o(0,0) pT(0,2) heads(1)
s(1,0) pT(0,3) o(0,1) o(0,2) s(1,1) o(0,3) xdbl pT(1,0) q(2) dt(0) v(1) dt(1) s(1,2) pT(1,1) dt(2) dt(3)
k(2) oT(0) o(1,0) s(1,3) o(1,1) pT(1,2) wo(0) heads(2) s(2,0) pT(1,3) o(1,2) s(2,1) pT(2,0) q(3) v(2)
sum o(1,3) s(2,2) oT(1) pT(2,1) s(2,3) o(2,0) k(3) wo(1) o(2,1) sum pT(2,2) heads(3) s(3,0) pT(2,3) sum
hT(0) o(2,2) h(0,0) h(0,1) sum h(0,2) h(0,3) h(0,4) h(0,5) sum s(3,1) w2(0) sum x2T(0) pT(3,0) o(2,3)
v(3) q(4) sum s(3,2) k(4) sum pT(3,1) sum o(3,0) oT(2) s(3,3) o(3,1) wo(2) pT(3,2) heads(4) sum s(4,0)
pT(3,3) s(4,1) pT(4,0) o(3,2) v(4) q(5) sum sum s(4,2) o(3,3) pT(4,1) oT(3) o(4,0) s(4,3) k(5) sum
pT(4,2) wo(3) o(4,1) heads(5) s(5,0) hT(1) sum sum h(1,0) h(1,1) h(1,2) sum h(1,3) o(4,2) h(1,4) sum
pT(4,3) h(1,5) w2(1) s(5,1) pT(5,0) o(4,3) sum x2T(1) oT(4) v(5) q(6) s(5,2) sum k(6) sum sum pT(5,1)
o(5,0) s(5,3) pT(5,2) wo(4) o(5,1) heads(6) sum s(6,0) o(5,2) pT(5,3) s(6,1) o(5,3) v(6) pT(6,0) q(7)
sum sum s(6,2) oT(5) pT(6,1) k(7) o(6,0) s(6,3) wo(5) pT(6,2) o(6,1) heads(7) sum s(7,0) pT(6,3) hT(2)
sum h(2,0) h(2,1) h(2,2) o(6,2) h(2,3) h(2,4) h(2,5) w2(2) s(7,1) sum o(6,3) pT(7,0) sum s(7,2) v(7)
pT(7,1) sum o(7,0) s(7,3) oT(6) z(0) wo(6) z(1) o(7,1) pT(7,2) sum sum o(7,2) z(2) pT(7,3) z(3) +xnT(0)
sum o(7,3) +q(0) +k(0) oT(7) out(0) wo(7) +v(0) out(1) hT(3) +heads(0) h(3,0) h(3,1) h(3,2) +s(0,0)
h(3,3) h(3,4) h(3,5) w2(3)
"""
DVE_ORDER = """
s(0,1) pT(0,0) s(0,2) turn(q,1) conv(0) turn(k,1) pT(0,1) s(0,3) conv(1) o(0,0) conv(2) pT(0,2) s(1,0)
o(0,1) conv(3) start(0) start(1) pT(0,3) s(1,1) o(0,2) pT(1,0) o(0,3) turn(q,2) s(1,2) pT(1,1) dt(0)
dt(1) dt(2) dt(3) turn(k,2) o(1,0) s(1,3) pT(1,2) o(1,1) dtmax u scan wo(0) scan s(2,0) scan pT(1,3)
s(2,1) o(1,2) scan scan turn(q,3) pT(2,0) o(1,3) s(2,2) scan scan pT(2,1) o(2,0) s(2,3) pT(2,2)
turn(k,3) wo(1) scan o(2,1) stats(0) scan hn(0) s(3,0) scan scan scan pT(2,3) o(2,2) h(0,0) h(0,1) scan
scan h(0,2) h(0,3) scan h(0,4) h(0,5) s(3,1) scan scan pT(3,0) w2(0) scan scan o(2,3) scan turn(q,4)
s(3,2) pT(3,1) scan turn(k,4) o(3,0) scan s(3,3) pT(3,2) o(3,1) scan wo(2) scan s(4,0) pT(3,3) scan
s(4,1) o(3,2) scan scan turn(q,5) pT(4,0) s(4,2) o(3,3) pT(4,1) scan scan s(4,3) o(4,0) scan pT(4,2)
turn(k,5) wo(3) scan o(4,1) stats(1) scan hn(1) scan s(5,0) pT(4,3) scan scan h(1,0) scan h(1,1) scan
h(1,2) o(4,2) h(1,3) scan h(1,4) scan h(1,5) scan scan s(5,1) w2(1) pT(5,0) o(4,3) scan scan scan s(5,2)
turn(q,6) scan turn(k,6) scan pT(5,1) o(5,0) s(5,3) scan pT(5,2) o(5,1) wo(4) scan s(6,0) scan pT(5,3)
o(5,2) s(6,1) scan scan pT(6,0) o(5,3) turn(q,7) s(6,2) scan scan turn(k,7) pT(6,1) wo(5) o(6,0) s(6,3)
pT(6,2) o(6,1) stats(2) scan hn(2) scan s(7,0) pT(6,3) scan scan h(2,0) h(2,1) h(2,2) o(6,2) scan scan
h(2,3) h(2,4) h(2,5) scan s(7,1) pT(7,0) w2(2) scan s(7,2) o(6,3) scan pT(7,1) scan s(7,3) o(7,0)
pT(7,2) scan wo(6) scan scan scan o(7,1) pT(7,3) o(7,2) +norm(0) +xn(0) skip gate o(7,3) +turn(q,0)
+turn(k,0) branch(0) wo(7) stats(3) hn(3) branch(1) h(3,0) +s(0,0) h(3,1) h(3,2) h(3,3) +norm(1) h(3,4)
h(3,5) w2(3) +xn(1)
"""
ACT_ORDER = """
s(0,1) xnT(1) q(1) pT(0,0) s(0,2) in(0) k(1) in(1) pT(0,1) in(2) s(0,3) in(3) heads(1) pT(0,2) s(1,0)
pT(0,3) silu s(1,1) xdbl q(2) pT(1,0) v(1) dt(0) dt(1) s(1,2) pT(1,1) dt(2) dt(3) k(2) oT(0) softplus
s(1,3) pT(1,2) dA dA dA heads(2) dA dA s(2,0) pT(1,3) q(3) s(2,1) pT(2,0) v(2) dA dA s(2,2) oT(1)
pT(2,1) dA k(3) s(2,3) pT(2,2) dA dA heads(3) s(3,0) hT(0) dA pT(2,3) dA dA h(0,0) h(0,1) dA h(0,2)
h(0,3) dA h(0,4) h(0,5) dA s(3,1) dA dA dA x2T(0) pT(3,0) q(4) v(3) dA dA k(4) dA dA s(3,2) pT(3,1)
oT(2) dA s(3,3) pT(3,2) heads(4) dA s(4,0) pT(3,3) dA s(4,1) q(5) pT(4,0) dA dA dA dA v(4) s(4,2) oT(3)
pT(4,1) k(5) dA dA s(4,3) pT(4,2) heads(5) hT(1) dA dA dA dA s(5,0) h(1,0) h(1,1) h(1,2) dA dA h(1,3)
h(1,4) h(1,5) dA dA pT(4,3) dA s(5,1) pT(5,0) dA dA x2T(1) q(6) oT(4) v(5) dA s(5,2) k(6) dA dA dA dA
pT(5,1) s(5,3) pT(5,2) dA heads(6) dA s(6,0) pT(5,3) s(6,1) pT(6,0) q(7) v(6) dA dA oT(5) dA s(6,2) k(7)
pT(6,1) s(6,3) pT(6,2) heads(7) dA dA dA hT(2) s(7,0) pT(6,3) dA h(2,0) h(2,1) h(2,2) dA h(2,3) h(2,4)
h(2,5) dA dA s(7,1) dA dA dA pT(7,0) v(7) s(7,2) pT(7,1) dA oT(6) s(7,3) z(0) z(1) pT(7,2) z(2) pT(7,3)
+xnT(0) z(3) +q(0) +k(0) oT(7) +v(0) hT(3) +heads(0) h(3,0) h(3,1) h(3,2) +s(0,0) h(3,3) h(3,4) h(3,5)
"""
POOL_ORDER = """
halo q(1) turn(q,1) turn(k,1) q(2) silu scan turn(q,2) turn(k,2) scan scan q(3) turn(q,3) scan scan scan
scan turn(k,3) stats(0) scan q(4) scan scan scan scan scan scan scan scan scan scan scan scan turn(q,4)
turn(k,4) scan scan scan scan q(5) scan scan scan scan scan turn(q,5) turn(k,5) scan scan stats(1) scan
scan scan scan scan scan scan q(6) scan scan scan scan scan turn(q,6) scan turn(k,6) scan scan scan scan
scan scan scan q(7) turn(q,7) turn(k,7) stats(2) scan scan outer(0) scan scan scan scan scan scan scan
scan scan scan +norm(0) carry +q(0) scan scan +turn(q,0) +turn(k,0) stats(3) outer(1) +norm(1) scan scan
"""
SP_ORDER = """
k(1) xdbl k(2) wo(0) q(3) scan scan k(3) scan scan scan scan scan scan wo(1) scan scan scan v(3) scan
scan scan scan scan scan scan scan scan scan k(4) scan scan scan scan scan scan wo(2) scan k(5) wo(3)
scan scan scan k(6) scan scan scan scan scan scan scan scan scan scan scan scan scan scan scan wo(4)
q(7) scan scan scan scan scan scan scan scan scan scan k(7) wo(5) v(7) wo(6) scan scan +x(0) wo(7) scan
store(0) scan scan scan scan scan scan scan scan +x(1) store(1)
"""


def stages_of(order):
    out = []
    for word in order.split():
        name, _, args = word.lstrip("+").rstrip(")").partition("(")
        out.append((int(word[0] == "+"), name, *(int(a) if a.isdigit() else a for a in args.split(",") if a)))
    return out


def build(nc, io):
    f32, bf16 = mybir.dt.float32, mybir.dt.bfloat16
    ALU, ACT = mybir.AluOpType, mybir.ActivationFunctionType
    AX = mybir.AxisListType
    ctx = ExitStack()

    def sb(name, shape, dt=f32):
        return ctx.enter_context(nc.sbuf_tensor(name, shape, dt))

    inw = sb("inw", [P, FT, 2 * INNER])
    xpw = sb("xpw", [P, NJ, XROWS])
    dtw = sb("dtw", [XROWS, INNER])
    outw = sb("outw", [P, NJ, D])
    wo = sb("wo", [P, LAYERS, NJ, D])
    w1 = sb("w1", [P, LAYERS, FT, 2 * HID])
    w2 = sb("w2", [P, LAYERS, NH, D])
    par = sb("par", [P, NPAR])
    qks = sb("qks", [P, LAYERS, 4, DH])
    ident = sb("ident", [P, P])
    identb = sb("identb", [P, P], bf16)
    mask = sb("mask", [P, 2, 2 * WIN], bf16)
    mask0 = sb("mask0", [P, 2 * WIN], bf16)
    amat = sb("amat", [P, NJ * STATES])
    powers = sb("powers", [P, HEADS * 2])
    wqkv = sb("wqkv", [P, FT, QKV])
    xtok = sb("xtok", [P, NW, D])
    tab = sb("tab", [P, 2, 4, DH])
    bc = sb("bc", [P, 2, GROUP, 2, T])
    xnT = sb("xnT", [P, FT, 1 + T])
    xin = sb("xin", [P, NJ, TAPS - 1 + T])
    halo = sb("halo", [P, NJ, TAPS - 1])
    xconv = sb("xconv", [P, NJ, T])
    dt_sb = sb("dt_sb", [P, NJ, T])
    xdbl = sb("xdbl", [XROWS, T])
    dA = sb("dA", [P, DA_RING, T])
    hb = sb("hb", [P, H_RING, T])
    state = sb("state", [P, UNITS])
    X = sb("X", [P, NW, D])
    stats = sb("stats", [P, NW, 2, 6])
    mv = sb("mv", [P, NW, 2])
    rstd = sb("rstd", [P, NW])
    x2T = sb("x2T", [P, FT, 1 + T])
    sq = sb("sq", [P, 2, HEADS * DH])
    rot = sb("rot", [P, 2, HEADS * DH])
    ssum = sb("ssum", [P, 2 * HEADS])
    rnorm = sb("rnorm", [P, 2 * HEADS])
    tabs = sb("tabs", [P, 4, DH])
    qT = sb("qT", [P, PAIRS, WIN])
    kT = sb("kT", [P, LAYERS, PAIRS, 2, WIN])
    V = sb("V", [P, LAYERS, 2, HEADS * DH])
    nmax = sb("nmax", [P, HEADS])
    rowsum = sb("rowsum", [P, HEADS])
    rinv = sb("rinv", [P, HEADS])
    probs = sb("probs", [P, 2, 2, 2 * WIN])
    pT = sb("pT", [P, 2, 4, WIN])
    o_sb = sb("o_sb", [P, HEADS * DH])
    oT = sb("oT", [P, NJ, WIN])
    sh = sb("sh", [P, LAYERS, NW, P])
    stats2 = sb("stats2", [P, 2, 2, 6])
    mv2 = sb("mv2", [P, 2, 2])
    rstd2 = sb("rstd2", [P, 2])
    hn = sb("hn", [P, 2, D])
    hT = sb("hT", [P, FT, 2 * WIN])
    gel = hn
    hid = sb("hid", [P, NH, 2 * WIN])
    scratch = nc.dram_tensor("bc_rows", [2 * STATES, T], f32, kind="Internal").ap()

    ybank = [ctx.enter_context(nc.psum_tensor(f"ysum{j}", [P, T], f32)) for j in range(NJ)]
    ring = [ctx.enter_context(nc.psum_tensor(f"ring{b}", [P, T], f32)) for b in range(BANKS)]

    class Signal:
        def __init__(self, name, per_chunk):
            self.sem = ctx.enter_context(nc.semaphore(name))
            self.per_chunk = per_chunk

        def at(self, chunk, count):
            assert -self.per_chunk < count <= self.per_chunk, (self.sem, count)
            reg, ahead = chunk
            level = (ahead + 1) * self.per_chunk + count
            return self.sem, level if reg is None else reg * self.per_chunk + level

    def ahead_of(chunk, n):
        return chunk[0], chunk[1] + n

    def token(chunk, n=0):
        reg, ahead = chunk
        return ahead * T + n if reg is None else reg * T + (ahead * T + n)

    passed = ctx.enter_context(nc.semaphore("passed"))
    D16 = 16
    x_loaded = [Signal(f"x_loaded{h}", D16) for h in range(2)]
    mask0_ready = Signal("mask0_ready", 1)
    tab_loaded = [Signal(f"tab_loaded{s}", D16 * LAYERS * NW // 2) for s in range(2)]
    wqkv_loaded = [Signal(f"w{c}_loaded", D16 * LAYERS) for c in "qkv"]
    bc_stored = Signal("bc_stored", D16)
    bc_loaded = [Signal(f"bc_loaded{s}", D16 * NGROUPS // 2) for s in range(2)]
    shifted = [Signal(f"shifted{w}", D16 * LAYERS) for w in range(NW)]
    carried = [Signal(f"carried{w}", D16 * LAYERS) for w in range(NW)]
    out_stored = [Signal(f"out_stored{h}", D16) for h in range(2)]
    stats_ready = Signal("stats_ready", NW)
    mv_ready = Signal("mv_ready", NW)
    eps_added = Signal("eps_added", 2)
    rstd_ready = Signal("rstd_ready", 2)
    xn_ready = Signal("xn_ready", NW)
    x0_ready = Signal("x0_ready", NW)
    full = [Signal(f"bank_full{b}", 0) for b in range(BANKS)]
    xnT_ready = Signal("xnT_ready", 2)
    halo_ready = Signal("halo_ready", 1)
    halo_saved = Signal("halo_saved", 1)
    xin_ready = Signal("xin_ready", NJ)
    tap0_ready = Signal("tap0_ready", NJ)
    conv_step = Signal("conv_step", NJ * (TAPS - 1))
    xconv_ready = Signal("xconv_ready", NJ)
    xdbl_ready = Signal("xdbl_ready", 1)
    dtv_ready = Signal("dtv_ready", NJ)
    dtmin_ready = Signal("dtmin_ready", NJ)
    dtexp_ready = Signal("dtexp_ready", NJ)
    dtlog_ready = Signal("dtlog_ready", NJ)
    dt_ready = Signal("dt_ready", NJ)
    u_ready = Signal("u_ready", NJ)
    dA_ready = Signal("dA_ready", UNITS)
    dBx_ready = Signal("dBx_ready", SUMS)
    h_ready = Signal("h_ready", UNITS)
    state_saved = Signal("state_saved", UNITS)
    hC_ready = Signal("hC_ready", SUMS)
    pair_added = Signal("pair_added", SUMS)
    summed = Signal("summed", SUMS)
    silu_ready = Signal("silu_ready", NJ)
    skip_added = Signal("skip_added", NJ)
    gated = Signal("gated", NJ)
    branch_added = Signal("branch_added", 2)
    outer_added = Signal("outer_added", 2)
    xnT_carried = Signal("xnT_carried", 1)
    x2T_carried = Signal("x2T_carried", 1)
    NA = LAYERS * NW
    sq_ready = Signal("sq_ready", 2 * NA)
    ssum_ready = Signal("ssum_ready", 2 * NA)
    ssum_clipped = Signal("ssum_clipped", 2 * NA)
    rnorm_ready = Signal("rnorm_ready", 2 * NA)
    tabs_ready = Signal("tabs_ready", NA)
    sine_ready = Signal("sine_ready", 2 * NA)
    rotary_ready = Signal("rotary_ready", 2 * NA)
    rot_ready = Signal("rot_ready", 2 * NA)
    normed = Signal("normed", 2 * NA)
    v_ready = Signal("v_ready", NA)
    qT_ready = Signal("qT_ready", NA)
    kT_ready = Signal("kT_ready", NA)
    nmax_ready = Signal("nmax_ready", PAIRS * NA)
    probs_ready = Signal("probs_ready", HEADS * NA)
    pT_ready = Signal("pT_ready", PAIRS * NA)
    rinv_ready = Signal("rinv_ready", PAIRS * NA)
    o_ready = Signal("o_ready", PAIRS * NA)
    oT_ready = Signal("oT_ready", NA)
    x1_ready = Signal("x1_ready", NA)
    NF = LAYERS * 2
    stats2_ready = Signal("stats2_ready", 4 * NF)
    mv2_ready = Signal("mv2_ready", 2 * NF)
    eps2_added = Signal("eps2_added", NF)
    rstd2_ready = Signal("rstd2_ready", NF)
    hn_ready = Signal("hn_ready", 4 * NF)
    hT_ready = Signal("hT_ready", FT * NF)
    gelu_ready = Signal("gelu_ready", NH * NF)
    hid_ready = Signal("hid_ready", NH * NF)
    x2_ready = Signal("x2_ready", NF)
    x2T_ready = Signal("x2T_ready", 2)
    consts_loaded = ctx.enter_context(nc.semaphore("consts_loaded"))
    weights_loaded = ctx.enter_context(nc.semaphore("weights_loaded"))
    memory_set = ctx.enter_context(nc.semaphore("memory_set"))
    casts_done = ctx.enter_context(nc.semaphore("casts_done"))
    a_exp = ctx.enter_context(nc.semaphore("a_exp"))
    a_ready = ctx.enter_context(nc.semaphore("a_ready"))

    order, emptied, early = [], {}, {}

    def group(name, read):
        order.append(name)
        emptied[name] = read
        early[name] = later

    for later, stage, *n in stages_of(PE_ORDER):
        if stage == "xnT":
            group(("xnT", n[0]), (xnT_ready, n[0] + 1))
        elif stage == "in":
            group(("xin", n[0]), (xin_ready, n[0] + 1))
        elif stage == "xdbl":
            group(("xdbl",), (xdbl_ready, 1))
        elif stage == "dt":
            group(("dt", n[0]), (dtv_ready, n[0] + 1))
        elif stage in ("q", "k"):
            group((stage, n[0]), (rotary_ready, 2 * n[0] + 1 + (stage == "k")))
        elif stage == "v":
            group(("v", n[0]), (v_ready, n[0] + 1))
        elif stage == "heads":
            group(("kT", n[0]), (kT_ready, n[0] + 1))
            group(("qT", n[0]), (qT_ready, n[0] + 1))
        elif stage == "s":
            group(("s", *n), (probs_ready, n[0] * HEADS + 2 * n[1] + 2))
        elif stage == "pT":
            group(("pT", *n), (pT_ready, n[0] * PAIRS + n[1] + 1))
        elif stage == "o":
            group(("o", *n), (o_ready, n[0] * PAIRS + n[1] + 1))
        elif stage == "oT":
            group(("oT", n[0]), (oT_ready, n[0] + 1))
        elif stage == "wo":
            group(("wo", n[0]), (x1_ready, n[0] + 1))
        elif stage == "hT":
            group(("hT", n[0]), (hT_ready, FT * (n[0] + 1)))
        elif stage == "h":
            group(("h", *n), (hid_ready, n[0] * NH + n[1] + 1))
        elif stage == "w2":
            group(("w2", n[0]), (x2_ready, n[0] + 1))
        elif stage == "x2T":
            group(("x2T", n[0]), (x2T_ready, n[0] + 1))
        elif stage == "z":
            group(("z", n[0]), (silu_ready, n[0] + 1))
        elif stage == "out":
            group(("out", n[0]), (branch_added, n[0] + 1))
    while len(order) % BANKS:
        order.append(None)
    at = {name: n for n, name in enumerate(order) if name}
    for s in full:
        s.per_chunk = len(order) // BANKS

    def bank(name):
        return ring[at[name] % BANKS]

    def freed(it, name):
        turn = ahead_of(it, -early[name])
        n = at[name] - BANKS
        while order[n] is None or (turn[0] is None and n >= 0 and not early[order[n]]):
            n -= BANKS
        sig, count = emptied[order[n]]
        if turn[0] is None and n < 0:
            return sig.at((None, -1), count)
        return sig.at(ahead_of(turn, early[order[n]] - (n < 0)), count)

    def done(name):
        n = at[name]
        spare = n + BANKS < len(order) and order[n + BANKS] is None
        return full[n % BANKS].sem, 2 if spare else 1

    def primed(b):
        return full[b].per_chunk - sum(done(g)[1] for g in order[b::BANKS] if g and early[g])

    def filled(it, name):
        n = at[name]
        b = n % BANKS
        turn = ahead_of(it, -early[name])
        if turn[0] is None:
            return full[b].sem, primed(b) + sum(done(g)[1] for g in order[b:n + 1:BANKS] if g and early[g])
        return full[b].at(turn, n // BANKS + done(name)[1])

    def unit(k):
        g, rest = divmod(k, GROUP * NJ)
        return g, rest // GROUP, rest % GROUP

    def heads_of(p):
        first = 4 * (p // 2) + p % 2
        return first, first + 2

    def first_stages(order, stages):
        for later, name, *args in stages_of(order):
            if later:
                stages[name](*args)

    def all_stages(order, stages, stages_ahead):
        for later, name, *args in stages_of(order):
            (stages_ahead if later else stages)[name](*args)

    block = ctx.enter_context(nc.Block())

    def prime(eng, signals):
        for s in signals:
            eng.sem_inc(s.sem, s.per_chunk)

    @block.sync
    def _(sp):
        prime(sp, [*x_loaded, *tab_loaded, *wqkv_loaded, bc_stored, *bc_loaded, *shifted,
                   *carried, *out_stored])
        early_ones = [(ident, io["ident"]), (par, io["par"]), (qks, io["qks"])]
        for dst, src in early_ones:
            sp.dma_start(dst[tuple(slice(None) for _ in dst.shape)], src).then_inc(consts_loaded, D16)
        sp.dma_start(hb[:, 0, :], io["mask"]).then_inc(consts_loaded, D16)
        sp.dma_start(hb[:, 1, 0:2 * WIN], io["mask0"]).then_inc(consts_loaded, D16)

        def stages(it):
            def load_x(h):
                sp.wait_ge(*outer_added.at(it, h - 1))
                sp.sem_inc(passed, 1)
                rows = io["x"][bass.ds(token(it, h * 2 * WIN), 2 * WIN), :]
                sp.dma_start(xtok[:, 2 * h:2 * h + 2, :], rows.rearrange("(w p) d -> p w d", p=P))\
                  .then_inc(x_loaded[h].sem, D16)
                if h == 0:
                    load_tab(0)
                    load_tab(1)

            def load_wqkv(l, i):
                sp.wait_ge(*filled(it, ("qkv"[i], NW - 1 if l else NA - 1)))
                sp.sem_inc(passed, 1)
                sp.dma_start(wqkv[:, :, i * 512:(i + 1) * 512], io["wqkv"][:, l, :, i * 512:(i + 1) * 512])\
                  .then_inc(wqkv_loaded[i].sem, D16)

            def load_tab(a):
                sp.wait_ge(*tabs_ready.at(it, a - 1))
                sp.sem_inc(passed, 1)
                sp.dma_start(tab[:, a % 2, :, :],
                             io["tab"][bass.ds(token(it, (a % NW) * WIN), WIN), :, :])\
                  .then_inc(tab_loaded[a % 2].sem, D16)

            def load_bc(g):
                sp.wait_ge(*hC_ready.at(it, (g - 1) * NJ))
                sp.sem_inc(passed, 1)
                rows = 2 * GROUP
                src = scratch[g * rows:(g + 1) * rows, :].rearrange("r t -> (r t)")
                sp.dma_start(bc[:, g % 2, :, :, :].rearrange("p n c t -> p (n c t)"), src.partition_broadcast(P))\
                  .then_inc(bc_loaded[g % 2].sem, D16)

            def shift(l, w):
                a = l * NW + w
                sp.wait_ge(*x1_ready.at(it, a + 1))
                sp.sem_inc(passed, 1)
                sp.wait_ge(*hn_ready.at(it, hn_reads(l, w)))
                sp.sem_inc(passed, 1)
                sp.dma_start(sh[1:P, l, w, :], X[0:P - 1, w, P:D]).then_inc(shifted[w].sem, D16)
                sp.wait_ge(*hn_ready.at(it, hn_carry(l, w)))
                sp.sem_inc(passed, 1)
                sp.dma_start(sh[0:1, l, (w + 1) % NW, :], X[P - 1:P, w, P:D]).then_inc(carried[w].sem, D16)

            def hn_reads(l, w):
                return 4 * (l * 2 + w // 2) + 4 - hn_ready.per_chunk

            def hn_carry(l, w):
                if w == NW - 1:
                    return 4 * (l * 2) + 4
                return hn_reads(l, w + 1)

            def store_bc():
                sp.wait_ge(*xdbl_ready.at(it, 1))
                sp.sem_inc(passed, 1)
                sp.wait_ge(*bc_loaded[0].at(it, 0))
                sp.sem_inc(passed, 1)
                sp.wait_ge(*bc_loaded[1].at(it, 0))
                sp.sem_inc(passed, 1)
                sp.dma_start(scratch, xdbl[0:2 * STATES, :]).then_inc(bc_stored.sem, D16)
                sp.wait_ge(*bc_stored.at(it, D16))
                sp.sem_inc(passed, 1)
                load_bc(0)
                load_bc(1)

            scans = [0]

            def scan_step():
                scans[0] += 1
                g, rest = divmod(scans[0] - 2, GROUP * NJ)
                if rest == 0 and 0 < g < NGROUPS - 1:
                    load_bc(g + 1)

            def projected(i, a):
                if i == 1 and 1 <= a < NA - 1:
                    load_tab(a + 1)
                if a % NW == NW - 1:
                    load_wqkv(1 - a // NW, i)

            def store(h):
                if h == 0:
                    sp.wait_ge(*branch_added.at(it, 1))
                    sp.sem_inc(passed, 1)
                else:
                    sp.wait_ge(*x2_ready.at(it, NF))
                    sp.sem_inc(passed, 1)
                rows = io["out"][bass.ds(token(it, h * 2 * WIN), 2 * WIN), :]
                sp.dma_start(rows.rearrange("(w p) d -> p w d", p=P), X[:, 2 * h:2 * h + 2, :])\
                  .then_inc(out_stored[h].sem, D16)

            return {"x": load_x, "xdbl": store_bc, "scan": scan_step, "q": lambda a: projected(0, a),
                    "k": lambda a: projected(1, a), "v": lambda a: projected(2, a),
                    "wo": lambda a: shift(a // NW, a % NW), "store": store}

        first_stages(SP_ORDER, stages((None, 0)))
        for i in range(3):
            sp.dma_start(wqkv[:, :, i * 512:(i + 1) * 512], io["wqkv"][:, 0, :, i * 512:(i + 1) * 512])\
              .then_inc(wqkv_loaded[i].sem, D16)
        for dst, src in [(inw, io["inw"]), (xpw, io["xpw"]), (wo, io["wo"]), (w1, io["w1"]), (w2, io["w2"]),
                         (outw, io["outw"])]:
            sp.dma_start(dst[tuple(slice(None) for _ in dst.shape)], src).then_inc(weights_loaded, D16)
        sp.dma_start(dtw[2 * STATES:XROWS, :], io["dtw"]).then_inc(weights_loaded, D16)
        sp.wait_ge(memory_set, N_SET)
        with sp.Fori(0, CHUNKS) as chunk:
            all_stages(SP_ORDER, stages((chunk, 0)), stages((chunk, 1)))
        sp.wait_ge(out_stored[0].sem, D16 * (CHUNKS + 1))
        sp.wait_ge(out_stored[1].sem, D16 * (CHUNKS + 1))
        sp.wait_ge(bc_stored.sem, D16 * (CHUNKS + 1))

    @block.vector
    def _(dve):
        prime(dve, [pair_added, dtmin_ready, stats_ready, mv_ready, xn_ready, x0_ready, conv_step, dt_ready,
                    u_ready, sine_ready, hn_ready, dBx_ready, h_ready,
                    hC_ready, skip_added, gated, branch_added, ssum_ready, rotary_ready,
                    nmax_ready, rinv_ready, o_ready, x1_ready, stats2_ready, mv2_ready, hid_ready,
                    x2_ready])
        dve.wait_ge(consts_loaded, N_CONST * D16)
        dve.wait_ge(memory_set, N_SET)
        dve.tensor_copy(mask[:, :, :], hb[:, 0, :].rearrange("p (s k) -> p s k", s=2)).then_inc(casts_done, 1)
        dve.tensor_copy(mask0[:, :], hb[:, 1, 0:2 * WIN]).then_inc(casts_done, 1)
        dve.tensor_copy(identb[:, :], ident[:, :]).then_inc(casts_done, 1)
        dve.wait_ge(casts_done, 3)

        def stages(it):
            def u_of(j):
                return xin[:, j, TAPS - 1:]

            def dBx(m):
                g, j, _ = unit(2 * m)
                if m % NJ == 0:
                    dve.wait_ge(*bc_loaded[g % 2].at(it, D16 * (g // 2 + 1)))
                if g == 0:
                    dve.wait_ge(*u_ready.at(it, j + 1))
                dve.wait_ge(*hC_ready.at(it, m - 1))
                dve.wait_ge(*state_saved.at(it, 2 * m - 2))
                slot = 2 * m % H_RING
                u_pair = xin[:, j:j + 1, TAPS - 1:].to_broadcast([P, GROUP, T])
                dve.tensor_tensor(hb[:, slot:slot + 2, :], u_pair, bc[:, g % 2, :, 0, :], ALU.mult)\
                   .then_inc(dBx_ready.sem, 1)

            def scan(k):
                dve.wait_ge(*dA_ready.at(it, k + 1))
                dve.wait_ge(*dBx_ready.at(it, k // 2 + 1))
                dve.wait_ge(*state_saved.at(it, k + 1 - UNITS))
                dve.tensor_tensor_scan(hb[:, k % H_RING, :], dA[:, k % DA_RING, :], hb[:, k % H_RING, :],
                                       state[:, k:k + 1], ALU.mult, ALU.add).then_inc(h_ready.sem, 1)

            def hC(m):
                g, _, _ = unit(2 * m)
                dve.wait_ge(*h_ready.at(it, 2 * m + 2))
                slot, out = 2 * m % H_RING, 2 * m % DA_RING
                dve.tensor_tensor(dA[:, out:out + 2, :], hb[:, slot:slot + 2, :], bc[:, g % 2, :, 1, :],
                                  ALU.mult).then_inc(hC_ready.sem, 1)

            def add_pair(m):
                dve.wait_ge(*hC_ready.at(it, m + 1))
                slot = (2 * m + 1) % DA_RING
                dve.tensor_tensor(dA[:, slot, :], dA[:, 2 * m % DA_RING, :], dA[:, slot, :], ALU.add)\
                   .then_inc(pair_added.sem, 1)

            at_unit = [0]

            def fill(count=1):
                for _ in range(count):
                    k = at_unit[0]
                    if 0 <= k - 1 < UNITS:
                        scan(k - 1)
                    if k % 2 == 0 and k >= 4:
                        add_pair(k // 2 - 2)
                    if k % 2 == 0 and k < UNITS:
                        dBx(k // 2)
                    if k % 2 and 1 <= k // 2 <= SUMS:
                        hC(k // 2 - 1)
                    at_unit[0] += 1

            def norm(h):
                dve.wait_ge(*x_loaded[h].at(it, D16))
                for w in (2 * h, 2 * h + 1):
                    dve.wait_ge(*mv_ready.at(it, w + 1 - NW))
                    dve.bn_stats(stats[:, w, 0, :], xtok[:, w, :]).then_inc(stats_ready.sem, 1)
                for w in (2 * h, 2 * h + 1):
                    dve.wait_ge(*stats_ready.at(it, w + 1))
                    dve.wait_ge(*xn_ready.at(it, w + 1 - NW))
                    dve.wait_ge(*x0_ready.at(it, w + 1 - NW))
                    dve.sem_inc(passed, 1)
                    dve.bn_aggr(mv[:, w, :], stats[:, w, 0, :]).then_inc(mv_ready.sem, 1)

            def normalized(out, w):
                return dve.tensor_scalar(out, xtok[:, w, :], mv[:, w, 0:1], rstd[:, w:w + 1], ALU.subtract, ALU.mult)

            def xn(h):
                dve.wait_ge(*rstd_ready.at(it, h + 1))
                dve.wait_ge(*hid_ready.at(ahead_of(it, -1), NH * (NF - 1 + h)))
                for w in (2 * h, 2 * h + 1):
                    if h == 0:
                        dve.wait_ge(*filled(ahead_of(it, -1), ("hT", NF - 2)))
                    else:
                        dve.wait_ge(*filled(ahead_of(it, -1), ("hT", NF - 1)))
                    normalized(hn[:, w % 2, :], w).then_inc(xn_ready.sem, 1)

            def start(h):
                dve.wait_ge(*rstd_ready.at(it, h + 1))
                dve.wait_ge(*out_stored[h].at(it, 0))
                for w in (2 * h, 2 * h + 1):
                    normalized(X[:, w, :], w).then_inc(x0_ready.sem, 1)

            def conv(j):
                dve.wait_ge(*tap0_ready.at(it, j + 1))
                for k in range(1, TAPS):
                    if k > 1:
                        dve.wait_ge(*conv_step.at(it, j * (TAPS - 1) + k - 1))
                    dve.scalar_tensor_tensor(xconv[:, j, :], xin[:, j, k:k + T],
                                             par[:, C_CW + j * TAPS + k:C_CW + j * TAPS + k + 1],
                                             xconv[:, j, :], ALU.mult, ALU.add).then_inc(conv_step.sem, 1)

            def clip(j):
                dve.wait_ge(*dtv_ready.at(it, j + 1))
                dve.wait_ge(*summed.at(it, 0))
                dve.tensor_scalar(dA[:, j, :], dt_sb[:, j, :], 40.0, None, ALU.min).then_inc(dtmin_ready.sem, 1)

            def softplus():
                for j in range(NJ):
                    dve.wait_ge(*dtlog_ready.at(it, j + 1))
                    dve.tensor_tensor(dt_sb[:, j, :], dt_sb[:, j, :], dA[:, j, :], ALU.max)\
                       .then_inc(dt_ready.sem, 1)

            def u():
                dve.wait_ge(*halo_saved.at(it, 1))
                for j in range(NJ):
                    dve.wait_ge(*dt_ready.at(it, j + 1))
                    dve.wait_ge(*xconv_ready.at(it, j + 1))
                    dve.tensor_tensor(u_of(j), dt_sb[:, j, :], xconv[:, j, :], ALU.mult).then_inc(u_ready.sem, 1)

            def rotate(name, a):
                i = "qk".index(name)
                n = 2 * a + i
                dve.wait_ge(*sq_ready.at(it, n + 1))
                dve.wait_ge(*rnorm_ready.at(it, n - 1))
                dve.tensor_reduce(ssum[:, i * HEADS:(i + 1) * HEADS], sq[:, i, :].rearrange("p (h d) -> p h d", d=DH),
                                  AX.X, ALU.add).then_inc(ssum_ready.sem, 1)
                src = bank((name, a))[:, :].rearrange("p (h d) -> p h d", d=DH)
                cos = tabs[:, 2 * i:2 * i + 1, :].to_broadcast([P, HEADS, DH])
                lo = tabs[:, 2 * i + 1:2 * i + 2, 0:DH // 2].to_broadcast([P, HEADS, DH // 2])
                hi = tabs[:, 2 * i + 1:2 * i + 2, DH // 2:DH].to_broadcast([P, HEADS, DH // 2])
                out = rot[:, i, :].rearrange("p (h d) -> p h d", d=DH)
                dve.wait_ge(*tabs_ready.at(it, a + 1))
                dve.wait_ge(*filled(it, (name, a)))
                dve.wait_ge(*normed.at(it, n - 1))
                dve.tensor_tensor(out[:, :, 0:DH // 2], src[:, :, DH // 2:DH], lo, ALU.mult)
                dve.tensor_tensor(out[:, :, DH // 2:DH], src[:, :, 0:DH // 2], hi, ALU.mult)\
                   .then_inc(sine_ready.sem, 1)
                dve.wait_ge(*ssum_ready.at(it, n + 1))
                dve.tensor_tensor(sq[:, i, :].rearrange("p (h d) -> p h d", d=DH), src, cos, ALU.mult)\
                   .then_inc(rotary_ready.sem, 1)

            def row_max(a, p):
                dve.wait_ge(*filled(it, ("s", a, p)))
                dve.wait_ge(*probs_ready.at(it, a * HEADS + 2 * p + 2 - HEADS))
                dve.tensor_reduce(nmax[:, 2 * p:2 * p + 2],
                                  bank(("s", a, p))[:, :].rearrange("p (h k) -> p h k", h=2),
                                  AX.X, ALU.max, negate=True).then_inc(nmax_ready.sem, 1)

            def invert(a, p):
                n = a * PAIRS + p
                dve.wait_ge(*probs_ready.at(it, 2 * n + 2))
                dve.wait_ge(*o_ready.at(it, n + 1 - PAIRS))
                dve.reciprocal(rinv[:, 2 * p:2 * p + 2], rowsum[:, 2 * p:2 * p + 2]).then_inc(rinv_ready.sem, 1)

            def head_out(a, p):
                n = a * PAIRS + p
                dve.wait_ge(*filled(it, ("o", a, p)))
                dve.wait_ge(*rinv_ready.at(it, n + 1))
                if p == 0:
                    dve.wait_ge(*filled(it if a else ahead_of(it, -1), ("oT", (a - 1) % NA)))
                o_view = o_sb[:, :].rearrange("p (c e a d) -> p c e a d", c=2, e=2, a=2)
                dve.tensor_tensor(o_view[:, p // 2, :, p % 2, :],
                                  bank(("o", a, p))[:, 0:2 * DH].rearrange("p (h d) -> p h d", h=2),
                                  rinv[:, 2 * p:2 * p + 2].unsqueeze(2).to_broadcast([P, 2, DH]), ALU.mult)\
                   .then_inc(o_ready.sem, 1)

            def add_attention(a):
                l, w = divmod(a, NW)
                dve.wait_ge(*filled(it, ("wo", a)))
                if l:
                    dve.wait_ge(*x2_ready.at(it, w // 2 + 1))
                else:
                    dve.wait_ge(*x0_ready.at(it, w + 1))
                dve.tensor_tensor(X[:, w, :], bank(("wo", a))[:, 0:D], X[:, w, :], ALU.add)\
                   .then_inc(x1_ready.sem, 1)

            def shifted_stats(f):
                l, half = divmod(f, 2)
                for v in range(2):
                    w = 2 * half + v
                    dve.wait_ge(*x1_ready.at(it, l * NW + w + 1))
                    dve.wait_ge(*mv2_ready.at(it, 2 * f + v - 1))
                    dve.bn_stats(stats2[:, v, 0, :], X[:, w, 0:P]).then_inc(stats2_ready.sem, 1)
                    dve.wait_ge(*shifted[w].at(it, D16 * (l + 1)))
                    dve.wait_ge(*carried[(w - 1) % NW].at(it, D16 * (l + 1) - (0 if w else D16 * LAYERS)))
                    dve.bn_stats(stats2[:, v, 1, :], sh[:, l, w, :]).then_inc(stats2_ready.sem, 1)
                for v in range(2):
                    dve.wait_ge(*stats2_ready.at(it, 4 * f + 2 * v + 2))
                    dve.wait_ge(*hn_ready.at(it, 4 * f))
                    dve.sem_inc(passed, 1)
                    dve.bn_aggr(mv2[:, v, :], stats2[:, v, :, :].rearrange("p a b -> p (a b)"))\
                       .then_inc(mv2_ready.sem, 1)

            def normalize(f):
                l, half = divmod(f, 2)
                dve.wait_ge(*rstd2_ready.at(it, f + 1))
                dve.wait_ge(*hid_ready.at(it, NH * f))
                if f == NF - 1:
                    dve.wait_ge(*filled(ahead_of(it, 1), ("xnT", 0)))
                elif f == 0:
                    dve.wait_ge(*filled(it, ("xnT", 1)))
                for v in range(2):
                    w = 2 * half + v
                    for ft, src in ((0, X[:, w, 0:P]), (1, sh[:, l, w, :])):
                        dve.tensor_scalar(hn[:, v, ft * P:(ft + 1) * P], src, mv2[:, v, 0:1], rstd2[:, v:v + 1],
                                          ALU.subtract, ALU.mult).then_inc(hn_ready.sem, 1)

            def hidden(f, i):
                l = f // 2
                rows = P if i < NH - 1 else LAST
                dve.wait_ge(*filled(it, ("h", f, i)))
                dve.wait_ge(*gelu_ready.at(it, f * NH + i + 1))
                b1a = C_B1A + l * NH + i
                dve.scalar_tensor_tensor(hid[0:rows, i, :], bank(("h", f, i))[0:rows, 0:2 * WIN],
                                         par[0:rows, b1a:b1a + 1], gel[0:rows, i % 2, :], ALU.add, ALU.mult)\
                   .then_inc(hid_ready.sem, 1)

            def add_feed(f):
                l, half = divmod(f, 2)
                dve.wait_ge(*filled(it, ("w2", f)))
                for w in (2 * half, 2 * half + 1):
                    dve.wait_ge(*shifted[w].at(it, D16 * (l + 1)))
                    dve.wait_ge(*carried[w].at(it, D16 * (l + 1)))
                dve.wait_ge(*hn_ready.at(it, 4 * f + 4))
                if l == LAYERS - 1:
                    dve.wait_ge(*outer_added.at(it, half + 1))
                if f == NF - 1:
                    dve.wait_ge(*branch_added.at(it, 2))
                dve.tensor_tensor(X[:, 2 * half:2 * half + 2, :],
                                  bank(("w2", f))[:, :].rearrange("p (w d) -> p w d", w=2),
                                  X[:, 2 * half:2 * half + 2, :], ALU.add).then_inc(x2_ready.sem, 1)

            def skip():
                for j in range(NJ):
                    dve.wait_ge(*summed.at(it, SUMS - NJ + j + 1))
                    dve.scalar_tensor_tensor(xconv[:, j, :], xconv[:, j, :], par[:, C_DP + j:C_DP + j + 1],
                                             ybank[j][:, :], ALU.mult, ALU.add).then_inc(skip_added.sem, 1)

            def gate():
                for j in range(NJ):
                    dve.wait_ge(*skip_added.at(it, j + 1))
                    dve.wait_ge(*silu_ready.at(it, j + 1))
                    dve.tensor_tensor(xconv[:, j, :], xconv[:, j, :], dt_sb[:, j, :], ALU.mult).then_inc(gated.sem, 1)

            def add_mamba(h):
                if h == 0:
                    dve.wait_ge(*x2_ready.at(it, NF - 1))
                else:
                    dve.wait_ge(*outer_added.at(it, 2))
                dve.wait_ge(*filled(it, ("out", h)))
                dve.tensor_tensor(X[:, 2 * h:2 * h + 2, :], bank(("out", h))[:, :].rearrange("p (w d) -> p w d", w=2),
                                  X[:, 2 * h:2 * h + 2, :], ALU.add).then_inc(branch_added.sem, 1)

            return {"norm": norm, "xn": xn, "start": start, "conv": conv, "dt": clip, "dtmax": softplus,
                    "u": u, "scan": fill,
                    "turn": rotate, "s": row_max, "pT": invert, "o": head_out,
                    "wo": add_attention, "stats": shifted_stats, "hn": normalize, "h": hidden, "w2": add_feed,
                    "skip": skip, "gate": gate, "branch": add_mamba}

        first_stages(DVE_ORDER, stages((None, 0)))
        with dve.Fori(0, CHUNKS) as chunk:
            all_stages(DVE_ORDER, stages((chunk, 0)), stages((chunk, 1)))

    @block.scalar
    def _(act):
        prime(act, [xnT_ready, xin_ready, tap0_ready, xconv_ready, xdbl_ready, dtv_ready, dtexp_ready,
                    dtlog_ready, dA_ready, silu_ready, sq_ready, v_ready, qT_ready, kT_ready, probs_ready,
                    pT_ready, oT_ready, hT_ready, gelu_ready, x2T_ready])
        act.wait_ge(consts_loaded, N_CONST * D16)
        act.wait_ge(memory_set, N_SET)
        act.activation(amat[:, :], par[:, C_ALOG:C_ALOG + NJ * STATES], ACT.Exp).then_inc(a_exp, 1)
        act.wait_ge(a_exp, 1)
        act.mul(amat[:, :], amat[:, :], -1.0).then_inc(a_ready, 1)
        act.wait_ge(a_ready, 1)

        def stages(it):
            at_unit = [0]

            def fill(count=1):
                for _ in range(count):
                    k = at_unit[0]
                    g, j, i = unit(k)
                    n = g * GROUP + i
                    if g == 0:
                        act.wait_ge(*dt_ready.at(it, max(j, min(k, NJ - 1)) + 1))
                    if i:
                        act.wait_ge(*summed.at(it, (k - DA_RING) // 2 + 1))
                    else:
                        act.wait_ge(*pair_added.at(it, (k - DA_RING) // 2 + 1))
                    act.activation(dA[:, k % DA_RING, :], dt_sb[:, j, :], ACT.Exp,
                                   scale=amat[:, j * STATES + n:j * STATES + n + 1]).then_inc(dA_ready.sem, 1)
                    at_unit[0] += 1

            def xnT_out(h):
                act.wait_ge(*xnT_carried.at(it, 0))
                act.wait_ge(*filled(it, ("xnT", h)))
                act.activation(xnT[:, :, 1 + h * 256:1 + (h + 1) * 256],
                               bank(("xnT", h))[:, :].rearrange("p (f t) -> p f t", f=FT), ACT.Copy)\
                   .then_inc(xnT_ready.sem, 1)

            def conv_input(j):
                if j == 0:
                    act.wait_ge(*halo_ready.at(it, 1))
                    act.wait_ge(*hC_ready.at(it, 0))
                    act.wait_ge(*gated.at(it, 0))
                act.wait_ge(*filled(it, ("xin", j)))
                act.activation(xin[:, j, TAPS - 1:], bank(("xin", j))[:, :], ACT.Copy).then_inc(xin_ready.sem, 1)
                act.wait_ge(*xin_ready.at(it, j + 1))
                act.activation(xconv[:, j, :], xin[:, j, 0:T], ACT.Identity,
                               bias=par[:, C_CB + j:C_CB + j + 1],
                               scale=par[:, C_CW + j * TAPS:C_CW + j * TAPS + 1]).then_inc(tap0_ready.sem, 1)

            def silu():
                for j in range(NJ):
                    act.wait_ge(*conv_step.at(it, (j + 1) * (TAPS - 1)))
                    act.activation(xconv[:, j, :], xconv[:, j, :], ACT.Silu).then_inc(xconv_ready.sem, 1)
                act.preload_act_table_set("natural_log_exp_and_others")

            def xdbl_out():
                act.wait_ge(*filled(it, ("xdbl",)))
                act.wait_ge(*bc_stored.at(it, 0))
                act.activation(xdbl[:, :], bank(("xdbl",))[0:XROWS, :], ACT.Copy).then_inc(xdbl_ready.sem, 1)

            def dt_out(j):
                act.wait_ge(*filled(it, ("dt", j)))
                act.activation(dt_sb[:, j, :], bank(("dt", j))[:, :], ACT.Identity,
                               bias=par[:, C_DTB + j:C_DTB + j + 1]).then_inc(dtv_ready.sem, 1)

            def softplus():
                for j in range(NJ):
                    act.wait_ge(*dtmin_ready.at(it, j + 1))
                    act.activation(dA[:, j, :], dA[:, j, :], ACT.Exp).then_inc(dtexp_ready.sem, 1)
                for j in range(NJ):
                    act.wait_ge(*dtexp_ready.at(it, j + 1))
                    act.activation(dA[:, j, :], dA[:, j, :], ACT.Ln, bias=1.0).then_inc(dtlog_ready.sem, 1)

            def square(i, name, a):
                n = 2 * a + i
                act.wait_ge(*normed.at(it, n - 1))
                act.wait_ge(*filled(it, (name, a)))
                act.activation(sq[:, i, :], bank((name, a))[:, :], ACT.Square).then_inc(sq_ready.sem, 1)

            def heads_out(a):
                l, w = divmod(a, NW)
                act.wait_ge(*filled(it, ("kT", a)))
                act.activation(kT[:, l, :, w % 2, :], bank(("kT", a))[:, :].rearrange("p (a t) -> p a t", a=PAIRS),
                               ACT.Copy).then_inc(kT_ready.sem, 1)
                act.wait_ge(*filled(it, ("qT", a)))
                act.activation(qT[:, :, :], bank(("qT", a))[:, :].rearrange("p (a t) -> p a t", a=PAIRS), ACT.Copy)\
                   .then_inc(qT_ready.sem, 1)

            def v_out(a):
                l, w = divmod(a, NW)
                act.wait_ge(*filled(it, ("v", a)))
                act.wait_ge(*filled(it if a else ahead_of(it, -1), ("o", (a - 1) % NA, PAIRS - 1)))
                act.activation(V[:, l, w % 2, :], bank(("v", a))[:, :], ACT.Copy).then_inc(v_ready.sem, 1)

            def exps(a, p):
                n = a * PAIRS + p
                act.wait_ge(*nmax_ready.at(it, n + 1))
                act.wait_ge(*rinv_ready.at(it, n + 1 - PAIRS))
                for hh in range(2):
                    c = 2 * p + hh
                    act.activation(probs[:, p % 2, hh, :], bank(("s", a, p))[:, hh * 256:(hh + 1) * 256], ACT.Exp,
                                   bias=nmax[:, c:c + 1], accum_out=rowsum[:, c:c + 1])\
                       .then_inc(probs_ready.sem, 1)

            def pT_out(a, p):
                n = a * PAIRS + p
                act.wait_ge(*filled(it, ("pT", a, p)))
                act.wait_ge(*o_ready.at(it, n - 1))
                act.activation(pT[:, p % 2, :, :], bank(("pT", a, p))[:, :].rearrange("p (a t) -> p a t", a=4),
                               ACT.Copy).then_inc(pT_ready.sem, 1)

            def oT_out(a):
                act.wait_ge(*filled(it, ("oT", a)))
                act.activation(oT[:, :, :], bank(("oT", a))[:, :].rearrange("p (a t) -> p a t", a=NJ), ACT.Copy)\
                   .then_inc(oT_ready.sem, 1)

            def hT_out(f):
                l = f // 2
                act.wait_ge(*filled(it, ("hT", f)))
                for ft in range(FT):
                    act.activation(hT[:, ft, :], bank(("hT", f))[:, ft * 256:(ft + 1) * 256], ACT.Identity,
                                   bias=par[:, C_LB + l * FT + ft:C_LB + l * FT + ft + 1],
                                   scale=par[:, C_LG + l * FT + ft:C_LG + l * FT + ft + 1])\
                       .then_inc(hT_ready.sem, 1)

            def gelu(f, i):
                l = f // 2
                rows = P if i < NH - 1 else LAST
                act.wait_ge(*filled(it, ("h", f, i)))
                act.wait_ge(*hid_ready.at(it, f * NH + i - 1))
                b1g = C_B1G + l * NH + i
                act.activation(gel[0:rows, i % 2, :], bank(("h", f, i))[0:rows, 256:512], ACT.Gelu,
                               bias=par[0:rows, b1g:b1g + 1]).then_inc(gelu_ready.sem, 1)

            def x2T_out(half):
                act.wait_ge(*filled(it, ("x2T", half)))
                act.wait_ge(*x2T_carried.at(it, 0))
                act.activation(x2T[:, :, 1 + half * 256:1 + (half + 1) * 256],
                               bank(("x2T", half))[:, :].rearrange("p (f t) -> p f t", f=FT), ACT.Copy)\
                   .then_inc(x2T_ready.sem, 1)

            def z_gate(j):
                act.wait_ge(*dA_ready.at(it, UNITS))
                act.wait_ge(*filled(it, ("z", j)))
                act.activation(dt_sb[:, j, :], bank(("z", j))[:, :], ACT.Silu).then_inc(silu_ready.sem, 1)

            return {"xnT": xnT_out, "in": conv_input, "silu": silu, "xdbl": xdbl_out, "dt": dt_out,
                    "softplus": softplus, "q": lambda a: square(0, "q", a), "k": lambda a: square(1, "k", a),
                    "heads": heads_out, "v": v_out, "s": exps, "pT": pT_out, "oT": oT_out, "hT": hT_out,
                    "h": gelu, "x2T": x2T_out, "z": z_gate, "dA": fill}

        first_stages(ACT_ORDER, stages((None, 0)))
        with act.Fori(0, CHUNKS) as chunk:
            all_stages(ACT_ORDER, stages((chunk, 0)), stages((chunk, 1)))

    @block.gpsimd
    def _(pool):
        for t in (xnT, x2T, state, halo, V, kT, sh):
            pool.memset(t[tuple(slice(None) for _ in t.shape)], 0.0).then_inc(memory_set, 1)
        pool.memset(powers[:, :], -0.5).then_inc(memory_set, 1)
        pool.memset(hid[:, :, :], 1.0).then_inc(memory_set, 1)
        prime(pool, [eps_added, rstd_ready, halo_ready, halo_saved, state_saved, outer_added,
                     xnT_carried, x2T_carried, mask0_ready, ssum_clipped, rnorm_ready, tabs_ready, rot_ready, normed,
                     eps2_added, rstd2_ready])
        pool.wait_ge(consts_loaded, N_CONST * D16)
        pool.wait_ge(memory_set, N_SET)

        def stages(it):
            at_unit = [0]

            def fill(count=1):
                for _ in range(count):
                    k = at_unit[0] - 1
                    if k >= 0:
                        pool.wait_ge(*h_ready.at(it, k + 1))
                        pool.sem_inc(passed, 1)
                        pool.tensor_copy(state[:, k:k + 1], hb[:, k % H_RING, T - 1:T]).then_inc(state_saved.sem, 1)
                    at_unit[0] += 1

            def load_halo():
                pool.wait_ge(*halo_saved.at(it, 0))
                pool.wait_ge(*hC_ready.at(it, 0))
                pool.sem_inc(passed, 1)
                pool.tensor_copy(xin[:, :, 0:TAPS - 1], halo[:, :, :]).then_inc(halo_ready.sem, 1)

            def rstd_of_x(h):
                part = slice(2 * h, 2 * h + 2)
                pool.wait_ge(*mv_ready.at(it, 2 * h + 2))
                pool.wait_ge(*xn_ready.at(it, 2 * h + 2 - NW))
                pool.wait_ge(*x0_ready.at(it, 2 * h + 2 - NW))
                pool.sem_inc(passed, 1)
                pool.tensor_scalar(rstd[:, part], mv[:, part, 1], EPS, None, ALU.add).then_inc(eps_added.sem, 1)
                pool.wait_ge(*eps_added.at(it, h + 1))
                pool.sem_inc(passed, 1)
                pool.tensor_tensor(rstd[:, part], rstd[:, part], powers[:, 0:2], ALU.pow).then_inc(rstd_ready.sem, 1)

            def save_halo():
                pool.wait_ge(*xin_ready.at(it, NJ))
                pool.wait_ge(*halo_ready.at(it, 1))
                pool.sem_inc(passed, 1)
                pool.tensor_copy(halo[:, :, :], xin[:, :, T:T + TAPS - 1]).then_inc(halo_saved.sem, 1)

            def scale_tables(a):
                pool.wait_ge(*tab_loaded[a % 2].at(it, D16 * (a // 2 + 1)))
                pool.wait_ge(*rotary_ready.at(it, 2 * a))
                pool.sem_inc(passed, 1)
                pool.tensor_tensor(tabs[:, :, :], tab[:, a % 2, :, :], qks[:, a // NW, :, :], ALU.mult)\
                    .then_inc(tabs_ready.sem, 1)

            def scale_heads(name, a):
                i = "qk".index(name)
                n = 2 * a + i
                part = slice(i * HEADS, (i + 1) * HEADS)
                pool.wait_ge(*ssum_ready.at(it, n + 1))
                pool.sem_inc(passed, 1)
                pool.tensor_scalar(rnorm[:, part], ssum[:, part], 1e-24, None, ALU.max).then_inc(ssum_clipped.sem, 1)
                pool.wait_ge(*ssum_clipped.at(it, n + 1))
                pool.sem_inc(passed, 1)
                pool.tensor_tensor(rnorm[:, part], rnorm[:, part], powers[:, part], ALU.pow).then_inc(rnorm_ready.sem, 1)
                pool.wait_ge(*sine_ready.at(it, n + 1))
                pool.wait_ge(*rotary_ready.at(it, n + 1))
                pool.sem_inc(passed, 1)
                pool.tensor_tensor(rot[:, i, :], rot[:, i, :], sq[:, i, :], ALU.add).then_inc(rot_ready.sem, 1)
                pool.wait_ge(*rot_ready.at(it, n + 1))
                pool.wait_ge(*rnorm_ready.at(it, n + 1))
                pool.sem_inc(passed, 1)
                r = rot[:, i, :].rearrange("p (h d) -> p h d", d=DH)
                pool.tensor_tensor(r, r, rnorm[:, part].unsqueeze(2).to_broadcast([P, HEADS, DH]), ALU.mult)\
                    .then_inc(normed.sem, 1)

            def rstd_of(f):
                pool.wait_ge(*mv2_ready.at(it, 2 * f + 2))
                pool.wait_ge(*hn_ready.at(it, 4 * f))
                pool.sem_inc(passed, 1)
                pool.tensor_scalar(rstd2[:, :], mv2[:, :, 1], EPS, None, ALU.add).then_inc(eps2_added.sem, 1)
                pool.wait_ge(*eps2_added.at(it, f + 1))
                pool.sem_inc(passed, 1)
                pool.tensor_tensor(rstd2[:, :], rstd2[:, :], powers[:, 0:2], ALU.pow).then_inc(rstd2_ready.sem, 1)

            def add_outer(h):
                pool.wait_ge(*hn_ready.at(it, 4 * (NF - 2 + h) + 4))
                for w in (2 * h, 2 * h + 1):
                    pool.wait_ge(*shifted[w].at(it, D16 * LAYERS))
                    pool.wait_ge(*carried[w].at(it, D16 * LAYERS))
                pool.sem_inc(passed, 1)
                pool.tensor_tensor(X[:, 2 * h:2 * h + 2, :], X[:, 2 * h:2 * h + 2, :], xtok[:, 2 * h:2 * h + 2, :],
                                   ALU.add).then_inc(outer_added.sem, 1)

            def carry():
                pool.wait_ge(*filled(it, ("z", NJ - 1)))
                pool.sem_inc(passed, 1)
                pool.tensor_copy(xnT[:, 1, 0:1], xnT[:, 1, T:T + 1]).then_inc(xnT_carried.sem, 1)
                pool.wait_ge(*filled(it, ("v", NA - 1)))
                pool.sem_inc(passed, 1)
                pool.tensor_copy(x2T[:, 1, 0:1], x2T[:, 1, T:T + 1]).then_inc(x2T_carried.sem, 1)
                pool.wait_ge(*probs_ready.at(it, HEADS * (NW + 1)))
                pool.sem_inc(passed, 1)
                pool.tensor_copy(mask0[:, :], mask[:, 0, :]).then_inc(mask0_ready.sem, 1)

            def keep_state():
                if at_unit[0] <= UNITS:
                    fill()

            return {"halo": load_halo, "norm": rstd_of_x, "silu": save_halo, "q": scale_tables,
                    "turn": scale_heads, "stats": rstd_of, "scan": keep_state, "outer": add_outer,
                    "carry": carry}

        first_stages(POOL_ORDER, stages((None, 0)))
        with pool.Fori(0, CHUNKS) as chunk:
            all_stages(POOL_ORDER, stages((chunk, 0)), stages((chunk, 1)))

    @block.tensor
    def _(pe):
        prime(pe, [summed])
        for b, s in enumerate(full):
            pe.sem_inc(s.sem, primed(b))
        pe.wait_ge(consts_loaded, N_CONST * D16)
        pe.wait_ge(memory_set, N_SET)
        pe.wait_ge(casts_done, 3)

        def stages(it):
            at_unit = [0]

            def fill(count=1):
                for _ in range(count):
                    m = at_unit[0]
                    g, j, _ = unit(2 * m)
                    pe.wait_ge(*pair_added.at(it, m + 1))
                    if g == 0:
                        pe.wait_ge(*skip_added.at(it, j + 1 - NJ))
                    pe.matmul(ybank[j][:, :], ident[:, :], dA[:, (2 * m + 1) % DA_RING, :], start=(g == 0),
                              stop=(g == NGROUPS - 1)).then_inc(summed.sem, 1)
                    at_unit[0] += 1

            def flip(name, src):
                for b, block_ in enumerate(src):
                    m = pe.transpose(bank(name)[:, b * P:(b + 1) * P], block_, ident[:, :])
                m.then_inc(*done(name))

            def blocks_of(t, first):
                return [t[:, first + v, ft * P:(ft + 1) * P] for ft in range(FT) for v in range(2)]

            def flip_xn(h):
                pe.wait_ge(*xn_ready.at(it, 2 * h + 2))
                pe.wait_ge(*freed(it, ("xnT", h)))
                flip(("xnT", h), blocks_of(hn, 0))

            def in_proj(name, j, col):
                pe.wait_ge(*freed(it, (name, j)))
                pe.wait_ge(*xnT_ready.at(it, 2))
                for ft in range(FT):
                    m = pe.matmul(bank((name, j))[:, :], inw[:, ft, col:col + P], xnT[:, ft, 1:1 + T],
                                  start=(ft == 0), stop=(ft == FT - 1))
                m.then_inc(*done((name, j)))

            def x_dbl():
                pe.wait_ge(*freed(it, ("xdbl",)))
                for j in range(NJ):
                    pe.wait_ge(*xconv_ready.at(it, j + 1))
                    m = pe.matmul(bank(("xdbl",))[0:XROWS, :], xpw[:, j, :], xconv[:, j, :],
                                  start=(j == 0), stop=(j == NJ - 1))
                m.then_inc(*done(("xdbl",)))

            def dt_proj(j):
                pe.wait_ge(*xdbl_ready.at(it, 1))
                pe.wait_ge(*freed(it, ("dt", j)))
                pe.matmul(bank(("dt", j))[:, :], dtw[2 * STATES:XROWS, j * P:(j + 1) * P],
                          xdbl[2 * STATES:XROWS, :], start=True, stop=True).then_inc(*done(("dt", j)))

            def project(i, a):
                l, w = divmod(a, NW)
                name = ("qkv"[i], a)
                pe.wait_ge(*wqkv_loaded[i].at(it, D16 * (l + 1)))
                if l:
                    pe.wait_ge(*x2T_ready.at(it, w // 2 + 1))
                else:
                    pe.wait_ge(*xnT_ready.at(it, w // 2 + 1))
                pe.wait_ge(*freed(it, name))
                for ft in range(FT):
                    off = w * WIN + (1 - ft)
                    m = pe.matmul(bank(name)[:, :], (x2T if l else xnT)[:, ft, off:off + WIN],
                                  wqkv[:, ft, i * 512:(i + 1) * 512], start=(ft == 0), stop=(ft == FT - 1))
                m.then_inc(*done(name))

            def heads(a):
                for i, name in ((1, "kT"), (0, "qT")):
                    pe.wait_ge(*normed.at(it, 2 * a + i + 1))
                    pe.wait_ge(*freed(it, (name, a)))
                    flip((name, a), [rot[:, i, p * P:(p + 1) * P] for p in range(PAIRS)])

            def scores(a, p):
                l, w = divmod(a, NW)
                pe.wait_ge(*qT_ready.at(it, a + 1))
                pe.wait_ge(*kT_ready.at(it, a + 1))
                if a == 0:
                    pe.wait_ge(*mask0_ready.at(it, 0))
                pe.wait_ge(*freed(it, ("s", a, p)))
                s = bank(("s", a, p))
                msk = mask0[:, :] if w == 0 else mask[:, w % 2, :]
                for hh in range(2):
                    pe.matmul(s[:, hh * 256:(hh + 1) * 256], identb[:, :], msk, start=(hh == 0), stop=False,
                              skip_group_check=True)
                for hh, h in enumerate(heads_of(p)):
                    rows = slice((h % 2) * DH, (h % 2 + 1) * DH)
                    m = pe.matmul(s[:, hh * 256:(hh + 1) * 256], qT[rows, h // 2, :],
                                  kT[rows, l, h // 2, :, :].rearrange("p a b -> p (a b)"),
                                  start=False, stop=True, skip_group_check=True)
                m.then_inc(*done(("s", a, p)))

            def flip_probs(a, p):
                pe.wait_ge(*probs_ready.at(it, a * HEADS + 2 * p + 2))
                pe.wait_ge(*freed(it, ("pT", a, p)))
                flip(("pT", a, p), [probs[:, p % 2, hh, s * WIN:(s + 1) * WIN]
                                    for hh in range(2) for s in range(2)])

            def head_out(a, p):
                pe.wait_ge(*v_ready.at(it, a + 1))
                pe.wait_ge(*pT_ready.at(it, a * PAIRS + p + 1))
                pe.wait_ge(*freed(it, ("o", a, p)))
                for hh, h in enumerate(heads_of(p)):
                    for s in range(2):
                        m = pe.matmul(bank(("o", a, p))[:, hh * DH:(hh + 1) * DH], pT[:, p % 2, 2 * hh + s, :],
                                      V[:, a // NW, s, h * DH:(h + 1) * DH], start=(s == 0), stop=(s == 1))
                m.then_inc(*done(("o", a, p)))

            def flip_out(a):
                pe.wait_ge(*o_ready.at(it, (a + 1) * PAIRS))
                pe.wait_ge(*freed(it, ("oT", a)))
                flip(("oT", a), [o_sb[:, k * P:(k + 1) * P] for k in range(NJ)])

            def attention_out(a):
                pe.wait_ge(*oT_ready.at(it, a + 1))
                pe.wait_ge(*freed(it, ("wo", a)))
                for k in range(NJ):
                    m = pe.matmul(bank(("wo", a))[:, 0:D], oT[:, k, :], wo[:, a // NW, k, :],
                                  start=(k == 0), stop=(k == NJ - 1))
                m.then_inc(*done(("wo", a)))

            def flip_hn(f):
                pe.wait_ge(*hn_ready.at(it, 4 * f + 4))
                pe.wait_ge(*freed(it, ("hT", f)))
                flip(("hT", f), blocks_of(hn, 0))

            def hidden(f, i):
                rows = P if i < NH - 1 else LAST
                pe.wait_ge(*hT_ready.at(it, FT * (f + 1)))
                pe.wait_ge(*freed(it, ("h", f, i)))
                for part in range(2):
                    for ft in range(FT):
                        col = part * HID + i * P
                        m = pe.matmul(bank(("h", f, i))[0:rows, part * 256:(part + 1) * 256],
                                      w1[:, f // 2, ft, col:col + rows], hT[:, ft, :], start=(ft == 0), stop=(ft == FT - 1))
                m.then_inc(*done(("h", f, i)))

            def feed_out(f):
                pe.wait_ge(*freed(it, ("w2", f)))
                for v in range(2):
                    for i in range(NH):
                        rows = P if i < NH - 1 else LAST + 1
                        if v == 0:
                            pe.wait_ge(*hid_ready.at(it, f * NH + i + 1))
                        m = pe.matmul(bank(("w2", f))[:, v * D:(v + 1) * D], hid[0:rows, i, v * WIN:(v + 1) * WIN],
                                      w2[0:rows, f // 2, i, :], start=(i == 0), stop=(i == NH - 1))
                m.then_inc(*done(("w2", f)))

            def flip_x2(half):
                pe.wait_ge(*x2_ready.at(it, half + 1))
                pe.wait_ge(*freed(it, ("x2T", half)))
                flip(("x2T", half), blocks_of(X, 2 * half))

            def out_proj(h):
                pe.wait_ge(*freed(it, ("out", h)))
                for v in range(2):
                    for j in range(NJ):
                        pe.wait_ge(*gated.at(it, j + 1))
                        m = pe.matmul(bank(("out", h))[:, v * D:(v + 1) * D],
                                      xconv[:, j, (2 * h + v) * WIN:(2 * h + v + 1) * WIN], outw[:, j, :],
                                      start=(j == 0), stop=(j == NJ - 1))
                m.then_inc(*done(("out", h)))

            return {"xnT": flip_xn, "in": lambda j: in_proj("xin", j, j * P), "xdbl": x_dbl, "dt": dt_proj,
                    "q": lambda a: project(0, a), "k": lambda a: project(1, a), "v": lambda a: project(2, a),
                    "heads": heads, "s": scores, "pT": flip_probs, "o": head_out, "oT": flip_out,
                    "wo": attention_out, "hT": flip_hn, "h": hidden, "w2": feed_out, "x2T": flip_x2,
                    "z": lambda j: in_proj("z", j, INNER + j * P), "out": out_proj, "sum": fill}

        first_stages(PE_ORDER, stages((None, 0)))
        pe.wait_ge(weights_loaded, N_WEIGHTS * D16)
        with pe.Fori(0, CHUNKS) as chunk:
            all_stages(PE_ORDER, stages((chunk, 0)), stages((chunk, 1)))

    ctx.close()


N_CONST, N_WEIGHTS, N_SET = 5, 7, 9


def constants():
    f = np.float32
    half = np.arange(0, DH, 2, dtype=f)
    freq = (f(1.0) / f(10000.0) ** (half / f(DH))).astype(f)
    t = np.arange(TOKENS + T, dtype=f)
    ang = t[:, None] * freq[None, :]
    ang = np.concatenate([ang, ang], axis=-1)
    base = (half + f(0.4 * DH)) / f(1.4 * DH)
    power = (t - TOKENS // 2) / f(WIN // 2)
    scale = base[None, :] ** power[:, None]
    scale = np.concatenate([scale, scale], axis=-1)
    cos, sin = np.cos(ang), np.sin(ang)
    sign = np.concatenate([-np.ones(DH // 2, f), np.ones(DH // 2, f)])
    tab = np.stack([8.0 * cos * scale, 8.0 * sin * scale * sign, cos / scale, sin / scale * sign], axis=1)
    q = np.arange(WIN)[:, None]
    k = np.arange(WIN)[None, :]
    own = np.where(k <= q, 0.0, NEG)
    prev = np.where(k >= q, 0.0, NEG)
    never = np.full((WIN, WIN), NEG)
    mask = np.stack([np.concatenate([own, prev], 1), np.concatenate([prev, own], 1)], axis=1).reshape(P, 4 * WIN).astype(f)
    mask0 = np.concatenate([own, never], 1).astype(f)
    eye = np.eye(P, dtype=f)
    return {"tab": np.ascontiguousarray(tab.astype(f)), "mask": mask, "mask0": mask0, "ident": eye}


def kernel(L0_attn_x, L0_attn_in_proj_w, L0_attn_conv_w, L0_attn_conv_b, L0_attn_x_proj_w, L0_attn_dt_proj_w,
           L0_attn_dt_proj_b, L0_attn_A_log, L0_attn_D_param, L0_attn_out_proj_w, L0_ffn_wqkv, L0_ffn_q_scale,
           L0_ffn_k_scale, L0_ffn_wo, L0_ffn_ln_g, L0_ffn_ln_b, L0_ffn_w1, L0_ffn_b1, L0_ffn_w2, L0_ffn_b2):
    import concourse.bacc as bacc
    from concourse.bass_utils import run_bass_kernel_spmd
    f = np.float32

    def tiles(a, n):
        a = np.asarray(a)
        return np.ascontiguousarray(np.moveaxis(a.reshape(n, P, *a.shape[1:]), 0, 1))

    xp = np.asarray(L0_attn_x_proj_w)
    ssm = xp[RANK:].reshape(2, STATES, INNER).transpose(1, 0, 2).reshape(2 * STATES, INNER)
    xp = np.concatenate([ssm, xp[:RANK]], axis=0)
    b1 = np.asarray(L0_ffn_b1).reshape(LAYERS, 2, HID)
    b1p = np.zeros((2, LAYERS, NH * P), f)
    b1p[:, :, :HID] = np.moveaxis(b1, 1, 0)
    w2p = np.zeros((LAYERS, NH * P, D), f)
    w2p[:, :HID] = np.asarray(L0_ffn_w2)
    w2p[:, HID] = np.asarray(L0_ffn_b2)

    def cols(a, n):
        return np.asarray(a).reshape(n, P).T

    par = np.concatenate([
        tiles(L0_attn_A_log, NJ).reshape(P, -1),
        tiles(np.asarray(L0_attn_conv_w).reshape(INNER, TAPS), NJ).reshape(P, -1),
        cols(L0_attn_conv_b, NJ), cols(L0_attn_dt_proj_b, NJ), cols(L0_attn_D_param, NJ),
        cols(L0_ffn_ln_g, LAYERS * FT), cols(L0_ffn_ln_b, LAYERS * FT),
        cols(b1p[0], LAYERS * NH), cols(b1p[1], LAYERS * NH)], axis=1)
    qs, ks = np.asarray(L0_ffn_q_scale), np.asarray(L0_ffn_k_scale)
    qks = np.stack([qs, np.roll(qs, DH // 2, axis=1), ks, np.roll(ks, DH // 2, axis=1)], axis=1)
    arrays = {
        "x": np.concatenate([np.asarray(L0_attn_x).reshape(TOKENS, D), np.zeros((T, D), f)]),
        "inw": tiles(np.asarray(L0_attn_in_proj_w).T, FT),
        "xpw": tiles(xp.T, NJ),
        "dtw": np.asarray(L0_attn_dt_proj_w).T,
        "outw": tiles(np.asarray(L0_attn_out_proj_w).T, NJ),
        "wqkv": np.moveaxis(np.asarray(L0_ffn_wqkv).reshape(LAYERS, FT, P, QKV), 2, 0),
        "wo": np.moveaxis(np.asarray(L0_ffn_wo).reshape(LAYERS, NJ, P, D), 2, 0),
        "w1": np.moveaxis(np.asarray(L0_ffn_w1).reshape(LAYERS, FT, P, 2 * HID), 2, 0),
        "w2": np.moveaxis(w2p.reshape(LAYERS, NH, P, D), 2, 0),
        "qks": np.broadcast_to(qks[None], (P, LAYERS, 4, DH)),
        "par": par,
        **constants(),
    }
    arrays = {k: np.ascontiguousarray(v) for k, v in arrays.items()}
    nc = bacc.Bacc("TRN2", target_bir_lowering=False, num_devices=1)
    io = {k: nc.dram_tensor(f"in_{k}", v.shape, mybir.dt.from_np(v.dtype), kind="ExternalInput").ap()
          for k, v in arrays.items()}
    io["out"] = nc.dram_tensor("out_y", (TOKENS, D), mybir.dt.float32, kind="ExternalOutput").ap()
    build(nc, io)
    r = run_bass_kernel_spmd(nc, [{f"in_{k}": v for k, v in arrays.items()}], core_ids=[0])
    return r.results[0]["out_y"].reshape(1, TOKENS, D)
```
